# Optimizing a Trainium2 kernel written in Bass

```python
import numpy as np
import jax
import jax.numpy as jnp

def _softmax(x, axis=-1):
    return jax.nn.softmax(x, axis=axis)

def _gelu(x):
    return jax.nn.gelu(x, approximate=True)

def _silu(x):
    return jax.nn.silu(x)

def _sigmoid(x):
    return jax.nn.sigmoid(x)

def _layernorm(x, axis=-1, eps=1e-05):
    m = jnp.mean(x, axis=axis, keepdims=True)
    v = jnp.var(x, axis=axis, keepdims=True)
    return (x - m) / jnp.sqrt(v + eps)

def _scatter_add(tgt, idx, src, axis=0):
    return tgt.at[idx].add(src)

def _segment_sum(src, seg, n):
    return jax.ops.segment_sum(src, seg, n)
kernel_name = 'mk_hybrid_d1_jaxref_r8_cca585'

def setup_inputs(seed: int=0):
    np.random.seed(seed)
    _w = jnp.asarray

    def _L0_attn_a_setup():
        import jax, jax.numpy as jnp
        import numpy as np
        import math
        B, T, E, H, DQ, NB, MAXLEN = (4, 128, 128, 16, 64, 10, 128)
        NEG = -1000000000.0

        def _attn_forward(X, Wq, bq, Wk, Wv, Wproj, bproj, Wr, br, b_nd):
            b, t, e = X.shape
            maxlen = b_nd.shape[1]
            nb = b_nd.shape[0]
            h = H
            dq = Wq.shape[1] // h
            Q = (X @ Wq + bq).reshape(b, t, h, dq).transpose(0, 2, 1, 3)
            K = (X @ Wk).reshape(b, t, h, dq).transpose(0, 2, 1, 3)
            V = (X @ Wv).reshape(b, t, h, dq).transpose(0, 2, 1, 3)
            R = (X @ Wr + br).reshape(b, t, h, nb).transpose(0, 2, 1, 3)
            d = jnp.arange(t)[:, None] - jnp.arange(t)[None, :]
            valid = (d >= 0) & (d < maxlen)
            bias = jnp.where(valid, 0.0, NEG).astype(jnp.float32)
            D_ntT = jnp.where(valid[None, :, :], b_nd[:, jnp.clip(d, 0, maxlen - 1)], 0.0)
            extra = jnp.einsum('bhtn,ntp->bhtp', R, D_ntT)
            logits = jnp.einsum('bhtd,bhpd->bhtp', Q, K) / math.sqrt(dq) + bias + extra
            W = jax.nn.softmax(logits, axis=-1)
            A = jnp.einsum('bhtp,bhpd->bhtd', W, V)
            A = A.transpose(0, 2, 1, 3).reshape(b, t, h * dq)
            return A @ Wproj + bproj
        key = jax.random.key(seed)
        k = jax.random.split(key, 10)
        X = jax.random.normal(k[0], (B, T, E), jnp.float32)
        Wq = jax.random.normal(k[1], (E, H * DQ), jnp.float32) * (0.1 / math.sqrt(E))
        bq = jnp.zeros((H * DQ,), jnp.float32)
        Wk = jax.random.normal(k[2], (E, H * DQ), jnp.float32) * (0.2 / math.sqrt(E))
        Wv = jax.random.normal(k[3], (E, H * DQ), jnp.float32) * (1.0 / math.sqrt(E))
        Wproj = jax.random.normal(k[4], (H * DQ, E), jnp.float32) * (1.0 / math.sqrt(H * DQ))
        bproj = jnp.zeros((E,), jnp.float32)
        Wr = jax.random.normal(k[5], (E, H * NB), jnp.float32) * (0.1 / math.sqrt(E))
        br = jnp.zeros((H * NB,), jnp.float32)
        b_nd = jax.random.normal(k[6], (NB, MAXLEN), jnp.float32) * 0.2
        return dict(X=X, Wq=Wq, bq=bq, Wk=Wk, Wv=Wv, Wproj=Wproj, bproj=bproj, Wr=Wr, br=br, b_nd=b_nd)
    _L0_attn_a_in = _L0_attn_a_setup()

    def _L0_attn_b_setup():
        import jax, jax.numpy as jnp
        import numpy as np
        D_MODEL = 128
        N_HEADS = 16
        D_LATENT = 32
        HEAD_DIM = D_MODEL // N_HEADS

        def apply_rope(x):
            B, T, H, D = x.shape
            inv_freq = 1.0 / 10000.0 ** (jnp.arange(0, D, 2, dtype=jnp.float32) / D)
            t = jnp.arange(T, dtype=jnp.float32)
            freqs = t[:, None] * inv_freq[None, :]
            sin_f = jnp.sin(freqs)[None, :, None, :]
            cos_f = jnp.cos(freqs)[None, :, None, :]
            x1, x2 = jnp.split(x, 2, axis=-1)
            return jnp.concatenate([x1 * cos_f - x2 * sin_f, x1 * sin_f + x2 * cos_f], axis=-1)
        key = jax.random.key(seed)
        ks = jax.random.split(key, 10)
        B, T = (4, 512)
        s = lambda fan_in: 1.0 / np.sqrt(fan_in)
        return {'x': jax.random.normal(ks[0], (B, T, D_MODEL), dtype=jnp.float32), 'Wq': jax.random.normal(ks[1], (D_MODEL, D_MODEL), dtype=jnp.float32) * s(D_MODEL), 'bq': jnp.zeros((D_MODEL,), jnp.float32), 'Wdown': jax.random.normal(ks[2], (D_MODEL, D_LATENT), dtype=jnp.float32) * s(D_MODEL), 'bdown': jnp.zeros((D_LATENT,), jnp.float32), 'Wup': jax.random.normal(ks[3], (D_LATENT, 2 * D_MODEL), dtype=jnp.float32) * s(D_LATENT), 'bup': jnp.zeros((2 * D_MODEL,), jnp.float32), 'Wout': jax.random.normal(ks[4], (D_MODEL, D_MODEL), dtype=jnp.float32) * s(D_MODEL), 'bout': jnp.zeros((D_MODEL,), jnp.float32)}
    _L0_attn_b_in = _L0_attn_b_setup()

    def _L0_ffn_setup():
        import jax, jax.numpy as jnp
        import numpy as np
        import math
        HID, HD, E, MIN_E = (128, 128, 16, 2)
        B, T = (4, 256)
        IS_CAUSAL = True

        def _l2norm(x, axis):
            return x / jnp.sqrt(jnp.sum(x * x, axis=axis, keepdims=True) + 1e-12)

        def _gating(hidden_states, sim_matrix, gates):
            b, t, c = hidden_states.shape
            flat = hidden_states.reshape(b * t, c)
            logits = _l2norm(flat, -1) @ _l2norm(sim_matrix, 0) - jax.nn.sigmoid(gates)
            gated = jax.nn.relu(logits)
            mask = (gated > 0).astype(gated.dtype)
            inactive = jnp.sum(mask, axis=1) == 0
            _, top_idx = jax.lax.top_k(logits, MIN_E)
            fb = jnp.sum(jax.nn.one_hot(top_idx, E, dtype=mask.dtype), axis=1)
            mask = mask + inactive[:, None].astype(mask.dtype) * fb
            masked = jnp.where(mask > 0, gated, -jnp.inf)
            probs = jax.nn.softmax(masked, axis=-1)
            return probs
        key = jax.random.key(seed)
        ks = jax.random.split(key, 6)
        a_qkv = math.sqrt(6.0 / (HID + HD))
        a_o = math.sqrt(6.0 / (HD + HID))
        return {'hidden_states': jax.random.normal(ks[0], (B, T, HID), jnp.float32), 'sim_matrix': jax.random.normal(ks[1], (HID, E), jnp.float32), 'gates': jnp.zeros((E,), jnp.float32), 'q_proj': jax.random.uniform(ks[2], (E, HID, HD), jnp.float32, -a_qkv, a_qkv), 'k_proj': jax.random.uniform(ks[3], (E, HID, HD), jnp.float32, -a_qkv, a_qkv), 'v_proj': jax.random.uniform(ks[4], (E, HID, HD), jnp.float32, -a_qkv, a_qkv), 'o_proj': jax.random.uniform(ks[5], (E, HD, HID), jnp.float32, -a_o, a_o)}
    _L0_ffn_in = _L0_ffn_setup()
    _d = {'L0_attn_a_X': _L0_attn_a_in['X'], 'L0_attn_a_Wq': _L0_attn_a_in['Wq'], 'L0_attn_a_bq': _L0_attn_a_in['bq'], 'L0_attn_a_Wk': _L0_attn_a_in['Wk'], 'L0_attn_a_Wv': _L0_attn_a_in['Wv'], 'L0_attn_a_Wproj': _L0_attn_a_in['Wproj'], 'L0_attn_a_bproj': _L0_attn_a_in['bproj'], 'L0_attn_a_Wr': _L0_attn_a_in['Wr'], 'L0_attn_a_br': _L0_attn_a_in['br'], 'L0_attn_a_b_nd': _L0_attn_a_in['b_nd'], 'L0_attn_b_Wq': _L0_attn_b_in['Wq'], 'L0_attn_b_bq': _L0_attn_b_in['bq'], 'L0_attn_b_Wdown': _L0_attn_b_in['Wdown'], 'L0_attn_b_bdown': _L0_attn_b_in['bdown'], 'L0_attn_b_Wup': _L0_attn_b_in['Wup'], 'L0_attn_b_bup': _L0_attn_b_in['bup'], 'L0_attn_b_Wout': _L0_attn_b_in['Wout'], 'L0_attn_b_bout': _L0_attn_b_in['bout'], 'L0_ffn_sim_matrix': _L0_ffn_in['sim_matrix'], 'L0_ffn_gates': _L0_ffn_in['gates'], 'L0_ffn_q_proj': _L0_ffn_in['q_proj'], 'L0_ffn_k_proj': _L0_ffn_in['k_proj'], 'L0_ffn_v_proj': _L0_ffn_in['v_proj'], 'L0_ffn_o_proj': _L0_ffn_in['o_proj']}
    _x0 = _d['L0_attn_a_X']
    _d['L0_attn_a_X'] = jax.random.normal(jax.random.fold_in(jax.random.key(seed), 1), (16, 512, 128), dtype=_x0.dtype)
    del _x0
    return _d

def reference(L0_attn_a_X, L0_attn_a_Wq, L0_attn_a_bq, L0_attn_a_Wk, L0_attn_a_Wv, L0_attn_a_Wproj, L0_attn_a_bproj, L0_attn_a_Wr, L0_attn_a_br, L0_attn_a_b_nd, L0_attn_b_Wq, L0_attn_b_bq, L0_attn_b_Wdown, L0_attn_b_bdown, L0_attn_b_Wup, L0_attn_b_bup, L0_attn_b_Wout, L0_attn_b_bout, L0_ffn_sim_matrix, L0_ffn_gates, L0_ffn_q_proj, L0_ffn_k_proj, L0_ffn_v_proj, L0_ffn_o_proj):

    def _L0_attn_a_ref(X, Wq, bq, Wk, Wv, Wproj, bproj, Wr, br, b_nd):
        import jax, jax.numpy as jnp
        import numpy as np
        import math
        B, T, E, H, DQ, NB, MAXLEN = (4, 128, 128, 16, 64, 10, 128)
        NEG = -1000000000.0

        def _attn_forward(X, Wq, bq, Wk, Wv, Wproj, bproj, Wr, br, b_nd):
            b, t, e = X.shape
            maxlen = b_nd.shape[1]
            nb = b_nd.shape[0]
            h = H
            dq = Wq.shape[1] // h
            Q = (X @ Wq + bq).reshape(b, t, h, dq).transpose(0, 2, 1, 3)
            K = (X @ Wk).reshape(b, t, h, dq).transpose(0, 2, 1, 3)
            V = (X @ Wv).reshape(b, t, h, dq).transpose(0, 2, 1, 3)
            R = (X @ Wr + br).reshape(b, t, h, nb).transpose(0, 2, 1, 3)
            d = jnp.arange(t)[:, None] - jnp.arange(t)[None, :]
            valid = (d >= 0) & (d < maxlen)
            bias = jnp.where(valid, 0.0, NEG).astype(jnp.float32)
            D_ntT = jnp.where(valid[None, :, :], b_nd[:, jnp.clip(d, 0, maxlen - 1)], 0.0)
            extra = jnp.einsum('bhtn,ntp->bhtp', R, D_ntT)
            logits = jnp.einsum('bhtd,bhpd->bhtp', Q, K) / math.sqrt(dq) + bias + extra
            W = jax.nn.softmax(logits, axis=-1)
            A = jnp.einsum('bhtp,bhpd->bhtd', W, V)
            A = A.transpose(0, 2, 1, 3).reshape(b, t, h * dq)
            return A @ Wproj + bproj
        return _attn_forward(X, Wq, bq, Wk, Wv, Wproj, bproj, Wr, br, b_nd)

    def _L0_attn_b_ref(x, Wq, bq, Wdown, bdown, Wup, bup, Wout, bout):
        import jax, jax.numpy as jnp
        import numpy as np
        D_MODEL = 128
        N_HEADS = 16
        D_LATENT = 32
        HEAD_DIM = D_MODEL // N_HEADS

        def apply_rope(x):
            B, T, H, D = x.shape
            inv_freq = 1.0 / 10000.0 ** (jnp.arange(0, D, 2, dtype=jnp.float32) / D)
            t = jnp.arange(T, dtype=jnp.float32)
            freqs = t[:, None] * inv_freq[None, :]
            sin_f = jnp.sin(freqs)[None, :, None, :]
            cos_f = jnp.cos(freqs)[None, :, None, :]
            x1, x2 = jnp.split(x, 2, axis=-1)
            return jnp.concatenate([x1 * cos_f - x2 * sin_f, x1 * sin_f + x2 * cos_f], axis=-1)
        B, T, D = x.shape
        H, Dh = (N_HEADS, HEAD_DIM)
        q = x @ Wq + bq
        kv_latent = x @ Wdown + bdown
        kv = kv_latent @ Wup + bup
        q = q.reshape(B, T, H, Dh)
        kv = kv.reshape(B, T, H, 2 * Dh)
        k, v = jnp.split(kv, 2, axis=-1)
        q = apply_rope(q)
        k = apply_rope(k)
        att = jnp.einsum('bthd,btgd->bthg', q, k) / jnp.sqrt(jnp.float32(Dh))
        att = jax.nn.softmax(att, axis=-1)
        out = jnp.einsum('bthg,btgd->bthd', att, v)
        out = out.reshape(B, T, D)
        return out @ Wout + bout

    def _L0_ffn_ref(hidden_states, sim_matrix, gates, q_proj, k_proj, v_proj, o_proj):
        import jax, jax.numpy as jnp
        import numpy as np
        import math
        HID, HD, E, MIN_E = (128, 128, 16, 2)
        B, T = (4, 256)
        IS_CAUSAL = True

        def _l2norm(x, axis):
            return x / jnp.sqrt(jnp.sum(x * x, axis=axis, keepdims=True) + 1e-12)

        def _gating(hidden_states, sim_matrix, gates):
            b, t, c = hidden_states.shape
            flat = hidden_states.reshape(b * t, c)
            logits = _l2norm(flat, -1) @ _l2norm(sim_matrix, 0) - jax.nn.sigmoid(gates)
            gated = jax.nn.relu(logits)
            mask = (gated > 0).astype(gated.dtype)
            inactive = jnp.sum(mask, axis=1) == 0
            _, top_idx = jax.lax.top_k(logits, MIN_E)
            fb = jnp.sum(jax.nn.one_hot(top_idx, E, dtype=mask.dtype), axis=1)
            mask = mask + inactive[:, None].astype(mask.dtype) * fb
            masked = jnp.where(mask > 0, gated, -jnp.inf)
            probs = jax.nn.softmax(masked, axis=-1)
            return probs
        b, t, c = hidden_states.shape
        rw = _gating(hidden_states, sim_matrix, gates).reshape(b, t, E)
        q = jnp.einsum('btc,ech,bte->bth', hidden_states, q_proj, rw)
        k = jnp.einsum('btc,ech,bte->bth', hidden_states, k_proj, rw)
        v = jnp.einsum('btc,ech,bte->bth', hidden_states, v_proj, rw)
        scale = 1.0 / math.sqrt(HD)
        scores = jnp.einsum('bqh,bkh->bqk', q, k) * scale
        if IS_CAUSAL:
            causal = jnp.tril(jnp.ones((t, t), dtype=bool))
            scores = jnp.where(causal[None], scores, -jnp.inf)
        attn = jax.nn.softmax(scores, axis=-1)
        ao = jnp.einsum('bqk,bkh->bqh', attn, v)
        out = jnp.einsum('bth,ehc,bte->btc', ao, o_proj, rw)
        return out
    x = L0_attn_a_X
    x = x + _L0_attn_a_ref(_layernorm(x, axis=-1), L0_attn_a_Wq, L0_attn_a_bq, L0_attn_a_Wk, L0_attn_a_Wv, L0_attn_a_Wproj, L0_attn_a_bproj, L0_attn_a_Wr, L0_attn_a_br, L0_attn_a_b_nd)
    x = x + _L0_ffn_ref(_layernorm(x, axis=-1), L0_ffn_sim_matrix, L0_ffn_gates, L0_ffn_q_proj, L0_ffn_k_proj, L0_ffn_v_proj, L0_ffn_o_proj)
    x = x + _L0_attn_b_ref(_layernorm(x, axis=-1), L0_attn_b_Wq, L0_attn_b_bq, L0_attn_b_Wdown, L0_attn_b_bdown, L0_attn_b_Wup, L0_attn_b_bup, L0_attn_b_Wout, L0_attn_b_bout)
    x = x + _L0_ffn_ref(_layernorm(x, axis=-1), L0_ffn_sim_matrix, L0_ffn_gates, L0_ffn_q_proj, L0_ffn_k_proj, L0_ffn_v_proj, L0_ffn_o_proj)
    return x

_drawn_inputs = setup_inputs


def setup_inputs(seed=0):
    import zlib

    import numpy as np

    out = dict(_drawn_inputs(seed))
    spreads = {'L0_attn_a_bq': (0.0, 0.549),
     'L0_attn_a_bproj': (0.0, 0.1),
     'L0_attn_a_br': (0.0, 0.318),
     'L0_attn_b_bq': (0.0, 0.1),
     'L0_attn_b_bdown': (0.0, 0.1),
     'L0_attn_b_bup': (0.0, 0.1),
     'L0_attn_b_bout': (0.0, 0.1),
     'L0_ffn_gates': (0.0, 0.1)}
    factors = {'L0_attn_a_Wq': 4.337, 'L0_attn_a_Wk': 3.539, 'L0_attn_a_Wr': 3.056}
    for name, (base, spread) in spreads.items():
        noise = np.random.default_rng([zlib.crc32(name.encode()), seed]).standard_normal(out[name].shape)
        drawn = base * np.exp(spread * noise) if base else spread * noise
        out[name] = jnp.asarray(drawn.astype(out[name].dtype))
    for name, factor in factors.items():
        out[name] = (out[name] * factor).astype(out[name].dtype)
    return out
```

```python
from contextlib import ExitStack

import numpy as np
import concourse.bass as bass
from concourse import mybir

NBATCH, TOK, C = 16, 512, 128
P = 128
NT = TOK // P
H, DQ, NB, WIN = 16, 64, 10, 128
HP = H // 2
NE = 16
HB, DB, LAT = 16, 8, 32
NEG = -1.0e9
FMASK = -1.0e30
BIG = 1.0e30
LN_EPS = 1e-5
U = NT * HP



def heads(u):
    p = u % HP
    return [p // 2 * 4 + p % 2 + 2 * h for h in range(2)]




PROLOGUE = [("tr",)] + [("r", g) for g in range(4)] + [("g", 0, 0), ("g", 0, 1)]
PROLOGUE += [("qk", j) for j in range(HP)] + [("g", 0, 2), ("g", 0, 3)] + [("qk", j) for j in range(HP, 2 * HP)]
PROLOGUE += [("v", t, h) for t in range(NT) for h in range(2)]


def a_steps():
    s = [("ln",), ("tr",)]
    s += PROLOGUE[1:]
    for u in range(U):
        t, p = divmod(u, HP)
        s.append(("s", u))
        if u:
            s += [("t", u - 1), ("o", u - 1)]
        if p == 5:
            s.append(("pt", t, 0))
        if t and p == 1:
            s.append(("pt", t - 1, 1))
        if t and p == 2:
            s.append(("pp", t - 1))
        if t + 1 < NT and p % 2 == 1:
            s.append(("g", t + 1, p // 2))
    return s + [("t", U - 1), ("o", U - 1), ("pt", NT - 1, 1), ("pp", NT - 1)]


def experts(layer, phase):
    s = [("bc", layer, phase, 0)]
    for e in range(NE):
        if e + 1 < NE:
            s.append(("bc", layer, phase, e + 1))
        s.append(("mm", layer, phase, e))
    return s


def f_steps(f):
    s = [("xln", f), ("xtr", f), ("gl", f), ("ge", f), ("gt", f)] + experts(f, "qkv")
    s += [("qkve", f), ("vt", f)]
    for t in range(NT):
        s.append(("sc", f, t))
        if t:
            s.append(("tp", f, t - 1))
    return s + [("tp", f, NT - 1), ("av", f)] + experts(f, "o") + [("oe", f), ("ot", f)]


def b_steps():
    s = [("xln", "B"), ("xtr", "B"), ("lat",), ("bp", 0)]
    for t in range(NT):
        if t + 1 < NT:
            s.append(("bp", t + 1))
        s.append(("bq", t))
        if t:
            s.append(("bv", t - 1))
    return s + [("bv", NT - 1), ("bo",), ("br",)]


A_STEPS = a_steps()
X_STEPS = f_steps("F1") + b_steps() + f_steps("F2")

LENGTH = {"ln": 3, "tr": 1, "r": .85, "g": .87, "qk": .85, "v": .85, "s": 1.4, "t": .6, "o": .6, "pt": .3, "pp": 2,
          "xln": 3, "xtr": 1, "gl": 7, "ge": 4, "gt": 1, "bc": .2, "qkve": 1, "vt": 1, "sc": 1.5, "tp": .6, "av": 1.2,
          "oe": .5, "ot": .7, "lat": 1.5, "bp": 1.5, "bq": 5.5, "bv": 5, "bo": 1, "br": 1.5}


def length(s):
    if s[0] == "mm":
        return 2.6 if s[2] == "qkv" else .9
    return LENGTH[s[0]]


def merged():
    whole = [sum(map(length, x)) for x in (A_STEPS, X_STEPS)]
    done, at, out = [0.0, 0.0], [0, 0], []
    while at[0] < len(A_STEPS) or at[1] < len(X_STEPS):
        k = 0 if at[1] == len(X_STEPS) or (at[0] < len(A_STEPS) and done[0] / whole[0] <= done[1] / whole[1]) else 1
        step = (A_STEPS, X_STEPS)[k][at[k]]
        out.append((k, step))
        done[k] += length(step)
        at[k] += 1
    return out + [(0, ("handoff",))]


ORDER = merged()


def order(a, x):
    return [s for k, s in ORDER if (a, x)[k]]


ROTATION = ["S0", "S1", "TP", "OV"]


def a_bank(s):
    if s in PROLOGUE:
        return ROTATION[PROLOGUE.index(s) % 4]
    if s[0] == "s":
        return ROTATION[s[1] % 2]
    if s[0] in ("t", "g", "pt", "pp"):
        return "TP"
    if s[0] == "o" and s[1] % 4 == 3:
        return "OV"
    return None


def x_banks(s):
    kind = s[0]
    if kind in ("xtr", "gt", "ot", "bo"):
        return ["X2"]
    if kind in ("gl",):
        return ["X1"]
    if kind in ("bc", "vt"):
        return ["X3"]
    if kind == "qkve":
        return ["X0", "X1", "X2"]
    if kind == "sc":
        return [f"X{s[2] % 2}"]
    if kind == "tp":
        return [f"X{2 + s[2] % 2}"]
    if kind in ("av", "lat", "br"):
        return ["X0"]
    if kind == "oe":
        return ["X1"]
    if kind == "bp":
        return ["X1" if s[1] % 2 == 0 else "X3"]
    return []


BANK_USES = {b: [s for s in A_STEPS if a_bank(s) == b] for b in ROTATION}
BANK_USES |= {b: [s for s in X_STEPS if b in x_banks(s)] for b in ("X0", "X1", "X2", "X3")}


class Signal:

    def __init__(self, ctx, nc, name, keys, unit=1):
        self.sem = ctx.enter_context(nc.semaphore(name))
        self.turn = {k: n for n, k in enumerate(keys)}
        self.per, self.unit = len(keys), unit
        assert len(self.turn) == self.per

    def start(self):
        return self.per * self.unit

    def at(self, b, key=None, back=0):
        n = self.turn[key] + 1 if key is not None else self.per
        return (b + 1 - back) * self.start() + n * self.unit

    def before(self, b, key):
        return (b + 1) * self.start() + self.turn[key] * self.unit


def stack_kernel(nc, x, a_wq, a_bq, a_wk, a_wv, a_wproj, a_bproj, a_wr, a_br, a_bfun, b_wq, b_bq, b_wdown, b_bdown,
                 b_wup, b_bup, b_wout, b_bout, f_sim, f_gates, f_q, f_k, f_v, f_o, rope, out):
    f32, bf16 = mybir.dt.float32, mybir.dt.bfloat16
    ALU, ACT, AX = mybir.AluOpType, mybir.ActivationFunctionType, mybir.AxisListType
    ctx = ExitStack()
    with ctx:
        def sb(name, shape, dt=f32):
            return ctx.enter_context(nc.sbuf_tensor(name, shape, dt))

        def signal(name, keys, unit=1):
            s = Signal(ctx, nc, name, keys, unit)
            signals.append(s)
            return s

        signals = []
        wq, wk, wv = (sb(n, [P, H * DQ]) for n in ("wq", "wk", "wv"))
        wproj = sb("wproj", [P, HP, C])
        wr = sb("wr", [P, 4, P])
        bq = sb("bq", [P, HP])
        br = sb("br", [P, 4])
        bfun = sb("bfun", [P, 4, WIN])
        rows = sb("rows", [1, 2, C])
        ones = sb("ones", [P, P])
        ident = sb("ident", [P, P])
        wf = sb("wf", [P, 4, NE, P])
        sim = sb("sim", [P, NE])
        simn = sb("simn", [P, NE])
        sig = sb("sig", [P, NE])
        rank = sb("rank", [P, NE])
        select = sb("select", [P, NE, P], bf16)
        fmask = sb("fmask", [P, 3 * P + P])
        wqb = sb("wqb", [P, C])
        wdown = sb("wdown", [P, LAT])
        bdown = sb("bdown", [LAT, 1])
        wup = sb("wup", [LAT, 2 * C])
        biasb = sb("biasb", [P, 3 * C])
        wout = sb("wout", [P, C])
        ropet = sb("ropet", [P, NT, 2, DB])
        mhalf = sb("mhalf", [P, NE])
        xin = sb("xin", [P, NT, C])
        x1 = sb("x1", [P, NT, C])
        a_st = sb("a_st", [P, NT, 6])
        a_mv = sb("a_mv", [P, NT, 2])
        a_rs = sb("a_rs", [P, 2, NT])
        a_xn = sb("a_xn", [P, NT, C])
        a_xT = sb("a_xT", [P, TOK])
        QT = sb("QT", [P, HP, TOK])
        KT = sb("KT", [P, HP, TOK])
        V = sb("V", [P, NT, H * DQ])
        RT = sb("RT", [P, 4, TOK])
        G = sb("G", [P, HP, WIN])
        E = sb("E", [P, 2, HP, 2 * P])
        L = sb("L", [P, 2, 2, 2 * P])
        mx = sb("mx", [P, 2, 2])
        nmx = sb("nmx", [P, 2, 2])
        sums = sb("sums", [P, 2, H])
        rsums = sb("rsums", [P, 2, HP])
        PT = sb("PT", [P, 2, 4, P])
        AO = sb("AO", [P, TOK])
        AT = sb("AT", [P, HP, P])
        xres = sb("xres", [P, NT, C])
        x_st = sb("x_st", [P, NT, 6])
        x_mv = sb("x_mv", [P, NT, 2])
        x_rs = sb("x_rs", [P, 2, NT])
        x_xn = sb("x_xn", [P, NT, C])
        x_xT = sb("x_xT", [P, TOK])
        ss = sb("ss", [P, 3, NT])
        lg = sb("lg", [P, NT, NE])
        gt = sb("gt", [P, 12, NT, NE])
        g1 = sb("g1", [P, 10, NT])
        gb = sb("gb", [P, 2, NT, NE], bf16)
        rwsp = sb("rwsp", [P, NT, P])
        rwT = sb("rwT", [P, TOK], bf16)
        xs = sb("xs", [P, 2, TOK])
        x_sq = xs[:, 0].rearrange("p (t c) -> p t c", t=NT)
        qkvT = sb("qkvT", [P, 3, TOK])
        vr = sb("vr", [P, NT, P])
        FP = sb("FP", [P, 2, TOK])
        fm = sb("fm", [P, 4, NT])
        FPT = sb("FPT", [P, NT, TOK])
        aoT = sb("aoT", [P, TOK])
        oT = sb("oT", [P, TOK])
        yout = sb("yout", [P, NT, C])
        latT = aoT[0:LAT, :]
        qkvb = qkvT[:, :, :].rearrange("p a t -> p (a t)").rearrange("p (t n) -> p t n", t=NT)
        rp = xs[:, :, :].rearrange("p a (b n) -> p a b n", b=2)
        qkr = FP[:, :, 0:2 * C]
        att = FP[:, :, 2 * C:]
        W = FPT[:, :, :].rearrange("p a t -> p (a t)")
        ato = vr
        pb = oT[:, :].rearrange("p (t n) -> p t n", t=2)
        bm = sb("bm", [P, 2, 3, HB])

        names = ROTATION + ["X0", "X1", "X2", "X3"]
        bank = {n: ctx.enter_context(nc.psum_tensor(f"bank_{n}", [P, TOK], f32)) for n in names}
        scratch = nc.dram_tensor("bias_scratch", (2 * NT, P, HP, 2 * P), f32, kind="Internal")
        row = HP * 2 * P

        full = {n: signal(f"full_{n}", BANK_USES[n]) for n in names if n != "OV"}
        full["OV"] = signal("full_OV", [s for s in A_STEPS if a_bank(s) == "OV" and s[0] != "o"])
        free = {n: signal(f"free_{n}", BANK_USES[n]) for n in names}
        loaded = ctx.enter_context(nc.semaphore("loaded"))
        made = ctx.enter_context(nc.semaphore("made"))
        filled = ctx.enter_context(nc.semaphore("filled"))
        set_up = ctx.enter_context(nc.semaphore("set_up"))
        setup_mm = ctx.enter_context(nc.semaphore("setup_mm"))
        setup_act = ctx.enter_context(nc.semaphore("setup_act"))
        halves = [(t, g) for t in range(NT) for g in range(2)]
        x_in = signal("x_in", ["x"], 16)
        a_stats = signal("a_stats", ["x"])
        a_normed = signal("a_normed", ["x"])
        bias_out = signal("bias_out", halves, 16)
        bias_in = signal("bias_in", halves, 16)
        maxed = signal("maxed", list(range(U)))
        probs = signal("probs", list(range(U)))
        attended = signal("attended", list(range(U)))
        handed = signal("handed", ["x"])
        layers = ["F1", "B", "F2"]
        fl = ["F1", "F2"]
        x_stats = signal("x_stats", layers)
        x_normed = signal("x_normed", layers)
        squared = signal("squared", fl)
        scaled = signal("scaled", fl)
        gated = signal("gated", fl)
        gate_exp = signal("gate_exp", fl)
        routed = signal("routed", fl)
        tiles2 = [(f, t) for f in fl for t in range(NT)]
        f_maxed = signal("f_maxed", tiles2)
        f_probs = signal("f_probs", tiles2)
        f_inv = signal("f_inv", tiles2)
        f_norm = signal("f_norm", tiles2)
        roped = signal("roped", list(range(NT)))
        b_shift = signal("b_shift", list(range(NT)))
        b_exp = signal("b_exp", list(range(NT)))
        b_att = signal("b_att", list(range(NT)))
        y_out = signal("y_out", ["y"], 16)
        a_dve = signal("a_dve", list(range(1 + 2 * NT)))
        a_pool = signal("a_pool", list(range(2)))
        x_dve = signal("x_dve", list(range(3 + 6 * NT + 2 * 27)))
        x_pool = signal("x_pool", list(range(3 * 2 + 2 * 1 + 3 * NT)))

        up = b_wup.rearrange("l (h s d) -> l s h d", s=2, d=DB)
        bup = b_bup.rearrange("(a h s d) -> a s h d", a=1, s=2, d=DB)
        brv = a_br.rearrange("(g q n) -> q n g", g=4, n=NB)
        loads = [(wq[:, :], a_wq), (wk[:, :], a_wk), (wv[:, :], a_wv)]
        loads += [(bq[:, :], a_bq.rearrange("(j p) -> p j", p=P)),
                  (wproj[:, :, :], a_wproj.rearrange("(j p) c -> p j c", p=P)),
                  (rows[:, 0, :], a_bproj.rearrange("(a c) -> a c", a=1)),
                  (rows[:, 1, :], b_bout.rearrange("(a c) -> a c", a=1)),
                  (sim[:, :], f_sim), (sig[:, :], f_gates.rearrange("(a c) -> a c", a=1).to_broadcast([P, NE]))]
        for j, w in enumerate((f_q, f_k, f_v, f_o)):
            loads += [(wf[:, j, h:h + 8, :], w.rearrange("e c h -> c e h")[:, h:h + 8, :]) for h in (0, 8)]
        loads += [(wqb[:, :], b_wq), (wdown[:, :], b_wdown), (bdown[:, :], b_bdown.rearrange("(p a) -> p a", a=1)),
                  (biasb[:, 0:C], b_bq.rearrange("(a c) -> a c", a=1).to_broadcast([P, C])),
                  (wout[:, :], b_wout), (ropet[:, :, :, :], rope)]
        for j in range(2):
            loads += [(wup[:, j * C:(j + 1) * C].rearrange("l (h d) -> l h d", d=DB), up[:, j]),
                      (biasb[:, (j + 1) * C:(j + 2) * C].rearrange("p (h d) -> p h d", d=DB),
                       bup[:, j].to_broadcast([P, HB, DB]))]
        LOADED = 16 * (len(loads) + 9)
        CLEARED, MADE, SET_UP = 4, 10 + NE + 5, 5

        passed = ctx.enter_context(nc.semaphore("passed"))

        def wait_apart(eng, sem, value):
            eng.wait_ge(sem, value)
            eng.sem_inc(passed, 1)

        def chained(eng, sig, b, apart=False):
            n = [0]

            def then(ins):
                n[0] += 1
                ins.then_inc(sig.sem, 1)
                eng.wait_ge(sig.sem, (b + 1) * sig.per + n[0])
                if apart:
                    eng.sem_inc(passed, 1)
            then.count = n
            return then

        block = ctx.enter_context(nc.Block())

        def batches(eng, body):
            body(0, None)
            with eng.Fori(1, NBATCH) as i:
                body(i, i - 1)
            body(None, NBATCH - 1)

        def starts(eng, mine):
            for s in mine:
                eng.sem_inc(s.sem, s.start())

        xv = x.rearrange("b (t p) c -> b p t c", p=P)
        outv = out.rearrange("b (t p) c -> b p t c", p=P)

        @block.sync
        def _(sp):
            starts(sp, [x_in, bias_out, bias_in])
            for dst, src in loads:
                sp.dma_start(dst, src, allow_slow_non_contiguous=True).then_inc(loaded, 16)
            wait_apart(sp, made, CLEARED)
            for q in range(4):
                sp.dma_start(bfun[32 * q:32 * q + NB, q, :], a_bfun).then_inc(loaded, 16)
                sp.dma_start(br[32 * q:32 * q + NB, :], brv[q],
                             allow_slow_non_contiguous=True).then_inc(loaded, 16)
            sp.dma_start(wr[:, :, :].rearrange("c g (q r) -> c (g q) r", r=32)[:, :, 0:NB],
                         a_wr.rearrange("c (h n) -> c h n", n=NB)).then_inc(loaded, 16)
            for t in range(2 * NT):
                sp.dma_start(scratch.ap()[t].rearrange("p h k -> p (h k)"),
                             E[:, 0].rearrange("p h k -> p (h k)")).then_inc(filled, 16)
            wait_apart(sp, filled, 16 * 2 * NT)

            def body(a, x):
                if a is None:
                    return
                wait_apart(sp, a_normed.sem, a_normed.before(a, "x"))
                sp.dma_start(xin[:, :, :], xv[a]).then_inc(x_in.sem, 16)
                for n, (t, g) in enumerate(halves):
                    made_by = ("g", t, 2 * g + 1)
                    wait_apart(sp, free[a_bank(made_by)].sem, free[a_bank(made_by)].at(a, made_by))
                    skew = bass.AP(tensor=scratch, offset=n * P * row + 1, ap=[[row + 1, P], [2 * P, HP], [1, WIN]])
                    sp.dma_start(skew, G[:, :, :]).then_inc(bias_out.sem, 16)
                    wait_apart(sp, bias_out.sem, bias_out.at(a, (t, g)))
                    last = ("s", (t - 1) % NT * HP + 4 * g + 3)
                    wait_apart(sp, free["S1"].sem, free["S1"].at(a, last, back=0 if t else 1))
                    sp.dma_start(E[:, g], scratch.ap()[n]).then_inc(bias_in.sem, 16)

            batches(sp, body)

        @block.gpsimd
        def _(pool):
            v = nc.gpsimd
            starts(pool, [a_normed, a_pool, x_normed, x_pool, scaled, roped])
            v.memset(E[:, 0].rearrange("p h k -> p (h k)"), NEG).then_inc(made, 1)
            v.memset(wr[:, :, :], 0.0).then_inc(made, 1)
            v.memset(br[:, :], 0.0).then_inc(made, 1)
            v.memset(bfun[:, :, :], 0.0).then_inc(made, 1)
            v.memset(ident[:, :], 0.0).then_inc(made, 1)
            v.memset(select[:, :, :], 0.0).then_inc(made, 1)
            v.memset(fmask[:, :], 0.0).then_inc(made, 1)
            v.memset(ones[:, :], 1.0).then_inc(made, 1)
            v.memset(mhalf[:, :], -0.5).then_inc(made, 1)
            v.memset(rwsp[:, :, :], 0.0).then_inc(made, 1)
            for e in range(NE):
                v.memset(rank[:, e:e + 1], float(NE - e)).then_inc(made, 1)
            n = 10 + NE
            wait_apart(pool, made, n)
            v.affine_select(out=ident[:, :], in_=ident[:, :], compare_op=ALU.not_equal, fill=1.0, base=0,
                            pattern=[[-1, P]], channel_multiplier=1).then_inc(made, 1)
            v.affine_select(out=fmask[:, 3 * P:], in_=fmask[:, 3 * P:], compare_op=ALU.is_ge, fill=FMASK, base=0,
                            pattern=[[-1, P]], channel_multiplier=1).then_inc(made, 1)
            for s in range(3):
                v.affine_select(out=select[:, :, :], in_=select[:, :, :], compare_op=ALU.not_equal, fill=1.0,
                                base=-NE * s, pattern=[[-1, NE], [0, P]], channel_multiplier=1).then_inc(made, 1)
                wait_apart(pool, made, n + 3 + s)
            assert n + 5 == MADE

            def layernorm(b, then, src, stats_sig, key, st_mv, rs, xn, done):
                wait_apart(pool, stats_sig.sem, stats_sig.at(b, key))
                then(v.tensor_scalar(rs[:, 0], st_mv[:, :, 1], LN_EPS, None, ALU.add))
                then(v.tensor_tensor(out=rs[:, 1], in0=rs[:, 0], in1=mhalf[:, 0:NT], op=ALU.pow))
                for t in range(NT):
                    last = v.tensor_scalar(xn[:, t], src[:, t], st_mv[:, t, 0:1], rs[:, 1, t:t + 1],
                                           ALU.subtract, ALU.mult)
                last.then_inc(done.sem, 1)

            def rotate(b, then, t):
                src = qkvb[:, t, 0:2 * C].rearrange("p (h s d) -> p h s d", s=2, d=DB // 2)
                both = qkvb[:, t, 0:2 * C].rearrange("p (h d) -> p h d", d=DB)
                cos = ropet[:, t, 0, :].unsqueeze(1).to_broadcast([P, 2 * HB, DB])
                r = rp[:, t % 2]
                swapped = r[:, 1].rearrange("p (h s d) -> p h s d", s=2, d=DB // 2)
                b_bank = x_banks(("bp", t))[0]
                wait_apart(pool, free[b_bank].sem, free[b_bank].at(b, ("bp", t)))
                then(v.tensor_tensor(out=r[:, 0].rearrange("p (h d) -> p h d", d=DB), in0=both, in1=cos, op=ALU.mult))
                for s in range(2):
                    sin = ropet[:, t, 1, s * 4:s * 4 + 4].unsqueeze(1).to_broadcast([P, 2 * HB, DB // 2])
                    then(v.tensor_tensor(out=swapped[:, :, s], in0=src[:, :, 1 - s], in1=sin, op=ALU.mult))
                v.tensor_tensor(out=qkr[:, t % 2], in0=r[:, 0], in1=r[:, 1], op=ALU.add).then_inc(roped.sem, 1)

            def body(a, x):
                a_then = chained(pool, a_pool, a, apart=True) if a is not None else None
                x_then = chained(pool, x_pool, x, apart=True) if x is not None else None
                for s in order(a is not None, x is not None):
                    if s[0] == "ln":
                        wait_apart(pool, a_stats.sem, a_stats.at(a, "x"))
                        v.tensor_copy(x1[:, :, :], xin[:, :, :])
                        layernorm(a, a_then, xin, a_stats, "x", a_mv, a_rs, a_xn, a_normed)
                    elif s[0] == "xln":
                        layernorm(x, x_then, xres, x_stats, s[1], x_mv, x_rs, x_xn, x_normed)
                    elif s[0] == "gl":
                        wait_apart(pool, squared.sem, squared.at(x, s[1]))
                        x_then(v.tensor_scalar(ss[:, 1], ss[:, 0], 1e-12, None, ALU.add))
                        v.tensor_tensor(out=ss[:, 2], in0=ss[:, 1], in1=mhalf[:, 0:NT], op=ALU.pow).then_inc(scaled.sem, 1)
                    elif s[0] == "bp":
                        rotate(x, x_then, s[1])
                assert a is None or a_then.count[0] == a_pool.per
                assert x is None or x_then.count[0] == x_pool.per, x_then.count

            wait_apart(pool, loaded, LOADED)
            wait_apart(pool, set_up, SET_UP - 1)
            v.tensor_tensor(out=lg[:, 1, :], in0=lg[:, 0, :], in1=mhalf[:, :], op=ALU.pow).then_inc(made, 1)
            wait_apart(pool, set_up, SET_UP)
            batches(pool, body)

        @block.scalar
        def _(act):
            v = nc.scalar
            starts(act, [free[b] for b in ("S0", "S1", "TP")] + [free["X2"], probs, gate_exp, f_probs, b_exp, y_out])

            def copy(dst, src):
                return v.activation(dst, src, ACT.Copy)

            act.wait_ge(loaded, LOADED)
            v.activation(sig[:, :], sig[:, :], ACT.Exp, scale=-1.0).then_inc(setup_act, 1)
            v.activation(bq[:, :], bq[:, :], ACT.Copy, scale=DQ ** -0.5).then_inc(setup_act, 1)
            act.wait_ge(setup_act, 2)

            def body(a, x):
                for s in order(a is not None, x is not None):
                    k = s[0]
                    if k in ("tr", "r", "g", "qk", "v", "t", "pt"):
                        bk = a_bank(s)
                        act.wait_ge(full[bk].sem, full[bk].at(a, s))
                        src = bank[bk]
                        if k == "tr":
                            i = copy(a_xT[:, :], src[:, :])
                        elif k == "r":
                            i = v.activation(RT[:, s[1], :], src[:, :], ACT.Identity, bias=br[:, s[1]:s[1] + 1])
                        elif k == "g":
                            if s[2] % 2 == 0:
                                act.wait_ge(bias_out.sem, bias_out.before(a, (s[1], s[2] // 2)))
                            i = copy(G[:, 4 * (s[2] % 2):4 * (s[2] % 2) + 4, :], src[:, :].rearrange("p (h d) -> p h d", h=4))
                        elif k == "qk" and s[1] < HP:
                            i = v.activation(QT[:, s[1], :], src[:, :], ACT.Identity, bias=bq[:, s[1]:s[1] + 1],
                                             scale=DQ ** -0.5)
                        elif k == "qk":
                            i = copy(KT[:, s[1] - HP, :], src[:, :])
                        elif k == "v":
                            i = copy(V[:, s[1], s[2] * TOK:(s[2] + 1) * TOK], src[:, :])
                        elif k == "t":
                            blocks = slice(0, 4) if s[1] >= HP else slice(0, 2)
                            i = copy(PT[:, s[1] % 2, blocks, :],
                                     src[:, 0:blocks.stop * P].rearrange("p (k t) -> p k t", t=P))
                        else:
                            i = copy(AT[:, 4 * s[2]:4 * s[2] + 4, :], src[:, :].rearrange("p (k t) -> p k t", t=P))
                        i.then_inc(free[bk].sem, 1)
                    elif k == "s":
                        u = s[1]
                        t, p = divmod(u, HP)
                        lo = 0 if t else P
                        act.wait_ge(maxed.sem, maxed.at(a, u))
                        for h, head in enumerate(heads(u)):
                            i = v.activation(L[:, u % 2, h, lo:], L[:, u % 2, h, lo:], ACT.Exp,
                                             bias=nmx[:, u % 2, h:h + 1],
                                             accum_out=sums[:, t % 2, head:head + 1])
                        i.then_inc(probs.sem, 1)
                    elif k in ("xtr", "gt"):
                        act.wait_ge(full["X2"].sem, full["X2"].at(x, s))
                        copy((x_xT if k == "xtr" else rwT)[:, :], bank["X2"][:, :]).then_inc(free["X2"].sem, 1)
                    elif k == "ge":
                        act.wait_ge(gated.sem, gated.at(x, s[1]))
                        v.activation(gt[:, 11], gt[:, 10], ACT.Exp).then_inc(gate_exp.sem, 1)
                    elif k == "qkve":
                        for j in range(3):
                            act.wait_ge(full[f"X{j}"].sem, full[f"X{j}"].at(x, s))
                            copy(qkvT[:, j, :], bank[f"X{j}"][:, :]).then_inc(free[f"X{j}"].sem, 1)
                    elif k == "vt":
                        act.wait_ge(full["X3"].sem, full["X3"].at(x, s))
                        copy(vr[:, :, :], bank["X3"][:, :].rearrange("p (t h) -> p t h", h=P)).then_inc(free["X3"].sem, 1)
                    elif k == "sc":
                        f, t = s[1:]
                        n = (t + 1) * P
                        act.wait_ge(f_maxed.sem, f_maxed.at(x, (f, t)))
                        v.activation(FP[:, t % 2, 0:n], FP[:, t % 2, 0:n], ACT.Exp, bias=fm[:, 1, t:t + 1],
                                     scale=P ** -0.5, accum_out=fm[:, 2, t:t + 1]).then_inc(f_probs.sem, 1)
                    elif k == "tp":
                        f, t = s[1:]
                        bk = x_banks(s)[0]
                        act.wait_ge(full[bk].sem, full[bk].at(x, s))
                        copy(FPT[:, 0:t + 1, t * P:(t + 1) * P],
                             bank[bk][:, 0:(t + 1) * P].rearrange("p (k t) -> p k t", t=P)).then_inc(free[bk].sem, 1)
                    elif k in ("av", "oe"):
                        bk = x_banks(s)[0]
                        act.wait_ge(full[bk].sem, full[bk].at(x, s))
                        copy((aoT if k == "av" else oT)[:, :], bank[bk][:, :]).then_inc(free[bk].sem, 1)
                    elif k == "ot" and s[1] == "F2":
                        act.wait_ge(free["X2"].sem, free["X2"].at(x, s))
                        act.dma_start(outv[x], yout[:, :, :]).then_inc(y_out.sem, 16)
                    elif k == "lat":
                        act.wait_ge(full["X0"].sem, full["X0"].at(x, s))
                        v.activation(latT[:, :], bank["X0"][0:LAT, :], ACT.Identity,
                                     bias=bdown[:, :]).then_inc(free["X0"].sem, 1)
                    elif k == "bq":
                        t = s[1]
                        act.wait_ge(b_shift.sem, b_shift.at(x, t))
                        v.activation(pb[:, t % 2], att[:, t % 2], ACT.Exp, scale=DB ** -0.5).then_inc(b_exp.sem, 1)
                    elif k == "bo":
                        act.wait_ge(full["X2"].sem, full["X2"].at(x, s))
                        copy(oT[:, :], bank["X2"][:, :]).then_inc(free["X2"].sem, 1)

            batches(act, body)
            act.wait_ge(y_out.sem, y_out.at(NBATCH - 1))

        @block.vector
        def _(dve):
            v = nc.vector
            starts(dve, [free[b] for b in ("OV", "X0", "X1", "X3")]
                   + [a_stats, a_dve, maxed, handed, gated, routed, x_stats, squared, x_dve, f_maxed, f_inv, f_norm, b_shift, b_att])
            n = 0

            def then(ins):
                nonlocal n
                n += 1
                ins.then_inc(set_up, 1)
                dve.wait_ge(set_up, n)

            dve.wait_ge(setup_act, 2)
            dve.wait_ge(made, MADE)
            then(v.tensor_scalar(sig[:, :], sig[:, :], 1.0, None, ALU.add))
            then(v.reciprocal(sig[:, :], sig[:, :]))
            then(v.tensor_tensor(out=simn[:, :], in0=sim[:, :], in1=sim[:, :], op=ALU.mult))
            dve.wait_ge(setup_mm, 1)
            then(v.tensor_scalar(lg[:, 0, :], bank["X3"][:, 0:NE], 1e-12, None, ALU.add))
            dve.wait_ge(made, MADE + 1)
            then(v.tensor_tensor(out=simn[:, :], in0=sim[:, :], in1=lg[:, 1, :], op=ALU.mult))
            assert n == SET_UP

            def stats(b, then, src, st, mv, done):
                for t in range(NT):
                    i = v.bn_stats(out=st[:, t], in_=src[:, t])
                    if t == NT - 1:
                        then(i)
                        dve.sem_inc(passed, 1)
                for t in range(NT):
                    i = v.bn_aggr(out=mv[:, t], in_=st[:, t])
                i.then_inc(done.sem, 1)

            A = lambda n: gt[:, n]
            S = lambda n: g1[:, n]
            wide = lambda a: a.unsqueeze(2).to_broadcast([P, NT, NE])
            all_t = lambda a: a.unsqueeze(1).to_broadcast([P, NT, NE])
            tt = lambda o, a, c, op: v.tensor_tensor(out=o, in0=a, in1=c, op=op)

            red = lambda o, a, op: v.tensor_reduce(out=o, in_=a, axis=AX.X, op=op)

            def gate(b, then, f):
                dve.wait_ge(free["X1"].sem, free["X1"].at(b, ("gl", f)))
                then(tt(A(0), lg[:, :, :], all_t(sig[:, :]), ALU.subtract))
                then(v.tensor_scalar(A(1), A(0), 0.0, None, ALU.max))
                then(v.tensor_scalar(A(2), A(0), 0.0, None, ALU.is_gt))
                then(red(S(0), A(0), ALU.max))
                then(tt(A(3), A(0), wide(S(0)), ALU.is_equal))
                then(tt(A(4), A(3), all_t(rank[:, :]), ALU.mult))
                then(red(S(1), A(4), ALU.max))
                then(tt(A(5), A(4), wide(S(1)), ALU.is_equal))
                then(v.scalar_tensor_tensor(A(7), A(5), -BIG, A(0), ALU.mult, ALU.add))
                then(red(S(2), A(7), ALU.max))
                then(tt(A(3), A(7), wide(S(2)), ALU.is_equal))
                then(tt(A(4), A(3), all_t(rank[:, :]), ALU.mult))
                then(red(S(3), A(4), ALU.max))
                then(tt(A(6), A(4), wide(S(3)), ALU.is_equal))
                then(tt(A(7), A(5), A(6), ALU.add))
                then(red(S(4), A(2), ALU.max))
                then(v.tensor_scalar(S(5), S(4), -1.0, 1.0, ALU.mult, ALU.add))
                then(tt(A(8), A(7), wide(S(5)), ALU.mult))
                then(tt(A(9), A(8), A(2), ALU.add))
                then(red(S(6), A(1), ALU.max))
                tt(A(10), A(1), wide(S(6)), ALU.subtract).then_inc(gated.sem, 1)

            def weigh(b, then, f):
                dve.wait_ge(gate_exp.sem, gate_exp.at(b, f))
                then(tt(A(3), A(11), A(9), ALU.mult))
                then(red(S(7), A(3), ALU.add))
                then(v.reciprocal(S(8), S(7)))
                then(tt(A(4), A(3), wide(S(8)), ALU.mult))
                then(v.tensor_copy(gb[:, 0], A(4)))
                then(tt(A(5), A(4), gb[:, 0], ALU.subtract))
                then(v.tensor_copy(gb[:, 1], A(5)))
                v.tensor_copy(rwsp[:, :, 0:NE], gb[:, 0])
                v.tensor_copy(rwsp[:, :, NE:2 * NE], gb[:, 1])
                tt(rwsp[:, :, 2 * NE:3 * NE], A(5), gb[:, 1], ALU.subtract).then_inc(routed.sem, 1)

            def body(a, x):
                a_then = chained(dve, a_dve, a) if a is not None else None
                x_then = chained(dve, x_dve, x) if x is not None else None
                for s in order(a is not None, x is not None):
                    k = s[0]
                    if k == "ln":
                        dve.wait_ge(x_in.sem, x_in.at(a, "x"))
                        stats(a, a_then, xin, a_st, a_mv, a_stats)
                    elif k == "s":
                        u = s[1]
                        t, p = divmod(u, HP)
                        lo = 0 if t else P
                        bk = a_bank(s)
                        dve.wait_ge(bias_in.sem, bias_in.at(a, (t, p // 4)))
                        wait_apart(dve, full[bk].sem, full[bk].at(a, s))
                        for h, head in enumerate(heads(u)):
                            i = v.tensor_tensor_reduce(
                                out=L[:, u % 2, h, lo:], in0=bank[bk][:, h * 2 * P + lo:(h + 1) * 2 * P],
                                in1=E[:, p // 4, head % 8, lo:], scale=1.0, scalar=-3.0e38, op0=ALU.add, op1=ALU.max,
                                accum_out=mx[:, u % 2, h:h + 1])
                        i.then_inc(free[bk].sem, 1)
                        dve.wait_ge(free[bk].sem, free[bk].at(a, s))
                        v.tensor_scalar(nmx[:, u % 2], mx[:, u % 2], -1.0, None, ALU.mult).then_inc(maxed.sem, 1)
                    elif k == "o" and s[1] % 4 == 3:
                        u = s[1]
                        t, g = u // HP, u % HP // 4
                        dve.wait_ge(attended.sem, attended.at(a, u))
                        a_then(v.reciprocal(rsums[:, g], sums[:, t % 2, 8 * g:8 * g + 8]))
                        v.tensor_tensor(
                            out=AO[:, :].rearrange("p (h d) -> p h d", d=DQ),
                            in0=bank["OV"][:, :].rearrange("p (h d) -> p h d", d=DQ),
                            in1=rsums[:, g].unsqueeze(2).to_broadcast([P, 8, DQ]), op=ALU.mult).then_inc(free["OV"].sem, 1)
                    elif k == "pp":
                        dve.wait_ge(full["TP"].sem, full["TP"].at(a, s))
                        v.tensor_tensor(out=x1[:, s[1]], in0=bank["TP"][:, 0:C], in1=x1[:, s[1]],
                                        op=ALU.add).then_inc(free["TP"].sem, 1)
                    elif k == "handoff":
                        dve.wait_ge(free["TP"].sem, free["TP"].at(a, ("pp", NT - 1)))
                        if x is not None:
                            dve.wait_ge(free["X2"].sem, free["X2"].at(x, ("ot", "F2")))
                        v.tensor_copy(xres[:, :, :], x1[:, :, :]).then_inc(handed.sem, 1)
                    elif k == "xln":
                        if s[1] == "F1":
                            dve.wait_ge(handed.sem, handed.at(x, "x"))
                        elif s[1] == "B":
                            dve.wait_ge(free["X2"].sem, free["X2"].at(x, ("ot", "F1")))
                        else:
                            dve.wait_ge(free["X0"].sem, free["X0"].at(x, ("br",)))
                        stats(x, x_then, xres, x_st, x_mv, x_stats)
                    elif k == "xtr" and s[1] != "B":
                        dve.wait_ge(x_normed.sem, x_normed.at(x, s[1]))
                        for t in range(NT):
                            i = v.tensor_tensor_reduce(out=x_sq[:, t], in0=x_xn[:, t], in1=x_xn[:, t], scale=1.0,
                                                       scalar=0.0, op0=ALU.mult, op1=ALU.add,
                                                       accum_out=ss[:, 0, t:t + 1])
                        i.then_inc(squared.sem, 1)
                    elif k == "gl":
                        f = s[1]
                        dve.wait_ge(scaled.sem, scaled.at(x, f))
                        dve.wait_ge(full["X1"].sem, full["X1"].at(x, s))
                        v.tensor_tensor(out=lg[:, :, :], in0=bank["X1"][:, 0:NT * NE].rearrange("p (t e) -> p t e", e=NE),
                                        in1=ss[:, 2].unsqueeze(2).to_broadcast([P, NT, NE]),
                                        op=ALU.mult).then_inc(free["X1"].sem, 1)
                        gate(x, x_then, f)
                    elif k == "ge":
                        weigh(x, x_then, s[1])
                    elif k == "bc":
                        dve.wait_ge(full["X3"].sem, full["X3"].at(x, s))
                        src = x_xT if s[2] == "qkv" else aoT
                        if s[2] == "o" and s[3] == 0:
                            dve.wait_ge(free["X0"].sem, free["X0"].at(x, ("av", s[1])))
                        v.tensor_tensor(out=xs[:, s[3] % 2], in0=bank["X3"][:, :], in1=src[:, :],
                                        op=ALU.mult).then_inc(free["X3"].sem, 1)
                    elif k == "sc":
                        f, t = s[1:]
                        n = (t + 1) * P
                        bk = x_banks(s)[0]
                        wait_apart(dve, full[bk].sem, full[bk].at(x, s))
                        v.tensor_tensor_reduce(out=FP[:, t % 2, 0:n], in0=bank[bk][:, 0:n],
                                               in1=fmask[:, 4 * P - n:4 * P], scale=1.0, scalar=-3.0e38, op0=ALU.add,
                                               op1=ALU.max, accum_out=fm[:, 0, t:t + 1]).then_inc(free[bk].sem, 1)
                        dve.wait_ge(free[bk].sem, free[bk].at(x, s))
                        v.tensor_scalar(fm[:, 1, t:t + 1], fm[:, 0, t:t + 1], -(P ** -0.5), None,
                                        ALU.mult).then_inc(f_maxed.sem, 1)
                    elif k == "tp":
                        f, t = s[1:]
                        n = (t + 1) * P
                        dve.wait_ge(f_probs.sem, f_probs.at(x, (f, t)))
                        v.reciprocal(fm[:, 3, t:t + 1], fm[:, 2, t:t + 1]).then_inc(f_inv.sem, 1)
                        dve.wait_ge(f_inv.sem, f_inv.at(x, (f, t)))
                        v.tensor_scalar(FP[:, t % 2, 0:n], FP[:, t % 2, 0:n], fm[:, 3, t:t + 1], None,
                                        ALU.mult).then_inc(f_norm.sem, 1)
                    elif k == "ot" or k == "br":
                        f = s[1] if k == "ot" else "B"
                        bk = x_banks(s)[0]
                        dve.wait_ge(full[bk].sem, full[bk].at(x, s))
                        src = bank[bk][:, :].rearrange("p (t c) -> p t c", c=C)
                        if f == "F2":
                            dve.wait_ge(y_out.sem, y_out.before(x, "y"))
                        res = yout if f == "F2" else xres
                        v.tensor_tensor(out=res[:, :, :], in0=src, in1=xres[:, :, :], op=ALU.add).then_inc(free[bk].sem, 1)
                    elif k == "bp":
                        bk = x_banks(s)[0]
                        dve.wait_ge(full[bk].sem, full[bk].at(x, s))
                        v.tensor_tensor(out=qkvb[:, s[1]], in0=bank[bk][:, 0:3 * C], in1=biasb[:, :],
                                        op=ALU.add).then_inc(free[bk].sem, 1)
                    elif k == "bq":
                        t = s[1]
                        q = qkr[:, t % 2, 0:C].rearrange("p (h d) -> p h d", d=DB)
                        kk = qkr[:, t % 2, C:].rearrange("p (h d) -> p h d", d=DB)
                        full_shape = [P, HB, HB, DB]
                        at = att[:, t % 2]
                        by_head = at.rearrange("p (h g) -> p h g", g=HB)
                        dve.wait_ge(roped.sem, roped.at(x, t))
                        x_then(v.tensor_tensor(out=W[:, :].rearrange("p (h g d) -> p h g d", g=HB, d=DB),
                                               in0=q.unsqueeze(2).to_broadcast(full_shape),
                                               in1=kk.unsqueeze(1).to_broadcast(full_shape), op=ALU.mult))
                        x_then(v.tensor_reduce(out=at, in_=W[:, :].rearrange("p (n d) -> p n d", d=DB), axis=AX.X,
                                               op=ALU.add))
                        x_then(v.tensor_reduce(out=bm[:, t % 2, 0], in_=by_head, axis=AX.X, op=ALU.max))
                        v.tensor_tensor(out=by_head, in0=by_head,
                                        in1=bm[:, t % 2, 0].unsqueeze(2).to_broadcast([P, HB, HB]),
                                        op=ALU.subtract).then_inc(b_shift.sem, 1)
                    elif k == "bv":
                        t = s[1]
                        pr = pb[:, t % 2].rearrange("p (h g) -> p h g", g=HB)
                        vv = qkvb[:, t, 2 * C:].rearrange("p (g d) -> p d g", d=DB)
                        full_shape = [P, HB, DB, HB]
                        dve.wait_ge(b_exp.sem, b_exp.at(x, t))
                        v.tensor_reduce(out=bm[:, t % 2, 1], in_=pr, axis=AX.X, op=ALU.add)
                        x_then(v.tensor_tensor(out=W[:, :].rearrange("p (h d g) -> p h d g", d=DB, g=HB),
                                               in0=pr.unsqueeze(2).to_broadcast(full_shape),
                                               in1=vv.unsqueeze(1).to_broadcast(full_shape), op=ALU.mult))
                        x_then(v.reciprocal(bm[:, t % 2, 2], bm[:, t % 2, 1]))
                        o = ato[:, t].rearrange("p (h d) -> p h d", d=DB)
                        x_then(v.tensor_reduce(out=ato[:, t], in_=W[:, :].rearrange("p (n g) -> p n g", g=HB), axis=AX.X,
                                               op=ALU.add))
                        v.tensor_tensor(out=o, in0=o, in1=bm[:, t % 2, 2].unsqueeze(2).to_broadcast([P, HB, DB]),
                                        op=ALU.mult).then_inc(b_att.sem, 1)
                assert a is None or a_then.count[0] == a_dve.per, a_then.count
                assert x is None or x_then.count[0] == x_dve.per, x_then.count

            batches(dve, body)

        @block.tensor
        def _(pe):
            mm, trp = nc.tensor.matmul, nc.tensor.transpose
            starts(pe, list(full.values()) + [attended])
            pe.wait_ge(loaded, LOADED)
            pe.wait_ge(made, MADE)
            pe.wait_ge(set_up, 3)
            mm(bank["X3"][:, 0:NE], ones[:, :], simn[:, :], start=True, stop=True).then_inc(setup_mm, 1)
            pe.wait_ge(set_up, SET_UP)

            def body(a, x):
                def ready(b, bk, s):
                    pe.wait_ge(free[bk].sem, free[bk].at(b, s))

                def clear(b, bk, s):
                    pe.wait_ge(free[bk].sem, free[bk].before(b, s))

                for s in order(a is not None, x is not None):
                    k = s[0]
                    cols = lambda t: slice(t * P, (t + 1) * P)
                    if k == "tr":
                        bk = a_bank(s)
                        pe.wait_ge(a_normed.sem, a_normed.at(a, "x"))
                        clear(a, bk, s)
                        for t in range(NT):
                            i = trp(bank[bk][:, cols(t)], a_xn[:, t], ident[:, :])
                        i.then_inc(full[bk].sem, 1)
                    elif k == "r":
                        bk = a_bank(s)
                        if s[1] == 0:
                            ready(a, a_bank(("tr",)), ("tr",))
                        clear(a, bk, s)
                        mm(bank[bk][:, :], wr[:, s[1], :], a_xT[:, :], start=True, stop=True).then_inc(full[bk].sem, 1)
                    elif k == "g":
                        t, g = s[1:]
                        bk = a_bank(s)
                        if t == 0:
                            ready(a, a_bank(("r", g)), ("r", g))
                        clear(a, bk, s)
                        mm(bank[bk][:, :], RT[:, g, cols(t)], bfun[:, :, :].rearrange("p q d -> p (q d)"),
                           start=True, stop=True).then_inc(full[bk].sem, 1)
                    elif k == "qk":
                        bk = a_bank(s)
                        w, j = (wq, s[1]) if s[1] < HP else (wk, s[1] - HP)
                        clear(a, bk, s)
                        mm(bank[bk][:, :], w[:, cols(j)], a_xT[:, :], start=True, stop=True).then_inc(full[bk].sem, 1)
                    elif k == "v":
                        bk = a_bank(s)
                        clear(a, bk, s)
                        mm(bank[bk][:, :], a_xT[:, cols(s[1])], wv[:, s[2] * TOK:(s[2] + 1) * TOK],
                           start=True, stop=True).then_inc(full[bk].sem, 1)
                    elif k == "s":
                        u = s[1]
                        t, p = divmod(u, HP)
                        bk = a_bank(s)
                        if u == 0:
                            ready(a, a_bank(("v", NT - 1, 1)), ("v", NT - 1, 1))
                        clear(a, bk, s)
                        lo = 0 if t else P
                        for h, head in enumerate(heads(u)):
                            part = slice(head % 2 * DQ, head % 2 * DQ + DQ)
                            i = mm(bank[bk][:, h * 2 * P + lo:(h + 1) * 2 * P], QT[part, head // 2, cols(t)],
                                   KT[part, head // 2, max(t - 1, 0) * P:(t + 1) * P], start=True, stop=True)
                        i.then_inc(full[bk].sem, 1)
                    elif k == "t":
                        u = s[1]
                        pe.wait_ge(probs.sem, probs.at(a, u))
                        clear(a, "TP", s)
                        blocks = [(h, c) for h in range(2) for c in ((0, 1) if u >= HP else (1,))]
                        for n, (h, c) in enumerate(blocks):
                            i = trp(bank["TP"][:, cols(n)], L[:, u % 2, h, cols(c)], ident[:, :])
                        i.then_inc(full["TP"].sem, 1)
                    elif k == "o":
                        u = s[1]
                        t, p = divmod(u, HP)
                        ready(a, "TP", ("t", u))
                        if u % 4 == 0:
                            clear(a, "OV", ("o", u + 3))
                        keys = [t - 1, t] if t else [0]
                        for h, head in enumerate(heads(u)):
                            to = bank["OV"][:, head % 8 * DQ:(head % 8 + 1) * DQ]
                            for n, kt in enumerate(keys):
                                i = mm(to, PT[:, u % 2, h * len(keys) + n, :],
                                       V[:, kt, head * DQ:(head + 1) * DQ],
                                       start=(n == 0), stop=(n == len(keys) - 1))
                        i.then_inc(attended.sem, 1)
                    elif k == "pt":
                        t, g = s[1:]
                        ready(a, "OV", ("o", t * HP + 4 * g + 3))
                        clear(a, "TP", s)
                        for j in range(4):
                            i = trp(bank["TP"][:, cols(j)], AO[:, cols(j)], ident[:, :])
                        i.then_inc(full["TP"].sem, 1)
                    elif k == "pp":
                        ready(a, "TP", ("pt", s[1], 1))
                        clear(a, "TP", s)
                        mm(bank["TP"][:, 0:C], ones[0:1, :], rows[0:1, 0, :], start=True, stop=False)
                        for j in range(HP):
                            i = mm(bank["TP"][:, 0:C], AT[:, j, :], wproj[:, j, :], start=False, stop=(j == HP - 1))
                        i.then_inc(full["TP"].sem, 1)
                    elif k == "xtr":
                        pe.wait_ge(x_normed.sem, x_normed.at(x, s[1]))
                        clear(x, "X2", s)
                        for t in range(NT):
                            i = trp(bank["X2"][:, cols(t)], x_xn[:, t], ident[:, :])
                        i.then_inc(full["X2"].sem, 1)
                    elif k == "gl":
                        ready(x, "X2", ("xtr", s[1]))
                        clear(x, "X1", s)
                        for t in range(NT):
                            i = mm(bank["X1"][:, t * NE:(t + 1) * NE], x_xT[:, cols(t)], simn[:, :], start=True, stop=True)
                        i.then_inc(full["X1"].sem, 1)
                    elif k == "gt":
                        pe.wait_ge(routed.sem, routed.at(x, s[1]))
                        clear(x, "X2", s)
                        for t in range(NT):
                            i = trp(bank["X2"][:, cols(t)], rwsp[:, t], ident[:, :])
                        i.then_inc(full["X2"].sem, 1)
                    elif k == "bc":
                        if s[2:] == ("qkv", 0):
                            ready(x, "X2", ("gt", s[1]))
                        clear(x, "X3", s)
                        mm(bank["X3"][:, :], select[:, s[3], :], rwT[:, :], start=True, stop=True).then_inc(full["X3"].sem, 1)
                    elif k == "mm":
                        f, phase, e = s[1:]
                        ready(x, "X3", ("bc", f, phase, e))
                        to = (("X0", 0), ("X1", 1), ("X2", 2)) if phase == "qkv" else (("X1", 3),)
                        for bk, j in to:
                            if e == 0:
                                clear(x, bk, ("qkve" if phase == "qkv" else "oe", f))
                            i = mm(bank[bk][:, :], wf[:, j, e, :], xs[:, e % 2], start=(e == 0), stop=(e == NE - 1))
                            if e == NE - 1:
                                i.then_inc(full[bk].sem, 1)
                    elif k == "vt":
                        ready(x, "X2", ("qkve", s[1]))
                        clear(x, "X3", s)
                        for t in range(NT):
                            i = trp(bank["X3"][:, cols(t)], qkvT[:, 2, cols(t)], ident[:, :])
                        i.then_inc(full["X3"].sem, 1)
                    elif k == "sc":
                        f, t = s[1:]
                        bk = x_banks(s)[0]
                        if t == 0:
                            ready(x, "X0", ("qkve", f))
                            ready(x, "X1", ("qkve", f))
                        clear(x, bk, s)
                        mm(bank[bk][:, 0:(t + 1) * P], qkvT[:, 0, cols(t)], qkvT[:, 1, 0:(t + 1) * P],
                           start=True, stop=True).then_inc(full[bk].sem, 1)
                    elif k == "tp":
                        f, t = s[1:]
                        bk = x_banks(s)[0]
                        pe.wait_ge(f_norm.sem, f_norm.at(x, (f, t)))
                        clear(x, bk, s)
                        for j in range(t + 1):
                            i = trp(bank[bk][:, cols(j)], FP[:, t % 2, cols(j)], ident[:, :])
                        i.then_inc(full[bk].sem, 1)
                    elif k == "av":
                        ready(x, "X3", ("tp", s[1], NT - 1))
                        clear(x, "X0", s)
                        for j in range(NT):
                            i = mm(bank["X0"][:, j * P:], vr[:, j, :], FPT[:, j, j * P:], start=(j == 0), stop=(j == NT - 1))
                        i.then_inc(full["X0"].sem, 1)
                    elif k == "ot":
                        ready(x, "X1", ("oe", s[1]))
                        clear(x, "X2", s)
                        for t in range(NT):
                            i = trp(bank["X2"][:, cols(t)], oT[:, cols(t)], ident[:, :])
                        i.then_inc(full["X2"].sem, 1)
                    elif k == "lat":
                        ready(x, "X2", ("xtr", "B"))
                        clear(x, "X0", s)
                        mm(bank["X0"][0:LAT, :], wdown[:, :], x_xT[:, :], start=True, stop=True).then_inc(full["X0"].sem, 1)
                    elif k == "bp":
                        bk = x_banks(s)[0]
                        if s[1] == 0:
                            ready(x, "X0", ("lat",))
                        clear(x, bk, s)
                        mm(bank[bk][:, 0:C], x_xT[:, cols(s[1])], wqb[:, :], start=True, stop=True)
                        mm(bank[bk][:, C:3 * C], latT[:, cols(s[1])], wup[:, :], start=True, stop=True).then_inc(full[bk].sem, 1)
                    elif k == "bo":
                        clear(x, "X2", s)
                        pe.wait_ge(b_att.sem, b_att.at(x, NT - 1))
                        for t in range(NT):
                            i = trp(bank["X2"][:, cols(t)], ato[:, t], ident[:, :])
                        i.then_inc(full["X2"].sem, 1)
                    elif k == "br":
                        ready(x, "X2", ("bo",))
                        clear(x, "X0", s)
                        for t in range(NT):
                            mm(bank["X0"][:, cols(t)], ones[0:1, :], rows[0:1, 1, :], start=True, stop=False)
                            i = mm(bank["X0"][:, cols(t)], oT[:, cols(t)], wout[:, :], start=False, stop=True)
                        i.then_inc(full["X0"].sem, 1)

            batches(pe, body)


_ARGS = ["L0_attn_a_X", "L0_attn_a_Wq", "L0_attn_a_bq", "L0_attn_a_Wk", "L0_attn_a_Wv", "L0_attn_a_Wproj",
         "L0_attn_a_bproj", "L0_attn_a_Wr", "L0_attn_a_br", "L0_attn_a_b_nd", "L0_attn_b_Wq", "L0_attn_b_bq",
         "L0_attn_b_Wdown", "L0_attn_b_bdown", "L0_attn_b_Wup", "L0_attn_b_bup", "L0_attn_b_Wout", "L0_attn_b_bout",
         "L0_ffn_sim_matrix", "L0_ffn_gates", "L0_ffn_q_proj", "L0_ffn_k_proj", "L0_ffn_v_proj", "L0_ffn_o_proj"]


def rope_table():
    inv = 1.0 / 10000.0 ** (np.arange(0, DB, 2, dtype=np.float32) / np.float32(DB))
    angle = np.arange(TOK, dtype=np.float32)[:, None] * inv[None, :].astype(np.float32)
    cos, sin = np.cos(angle).astype(np.float32), np.sin(angle).astype(np.float32)
    table = np.stack([np.concatenate([cos, cos], 1), np.concatenate([-sin, sin], 1)], 1)
    return np.ascontiguousarray(table.reshape(NT, P, 2, DB).transpose(1, 0, 2, 3))


def kernel(**inputs):
    import concourse.bacc as _bacc
    from concourse import mybir as _mybir
    from concourse.bass_utils import run_bass_kernel_spmd as _run

    nc = _bacc.Bacc("TRN2", target_bir_lowering=False, num_devices=1)
    arrays, args = {}, []
    for name in _ARGS + ["rope"]:
        a = rope_table() if name == "rope" else np.asarray(inputs[name])
        if name == "L0_attn_a_b_nd":
            a = a[:, ::-1]
        a = np.ascontiguousarray(a)
        arrays[f"in_{name}"] = a
        args.append(nc.dram_tensor(f"in_{name}", a.shape, _mybir.dt.from_np(a.dtype), kind="ExternalInput").ap())
    args.append(nc.dram_tensor("out_0", (NBATCH, TOK, C), _mybir.dt.float32, kind="ExternalOutput").ap())
    stack_kernel(nc, *args)
    r = _run(nc, [arrays], core_ids=[0])
    return r.results[0]["out_0"]
```

```python
from contextlib import ExitStack

import numpy as np
import concourse.bass as bass
from concourse import mybir

NBATCH, TOK, C = 16, 512, 128
P = 128
NT = TOK // P
H, DQ, NB, WIN = 16, 64, 10, 128
HP = H // 2
NE = 16
HB, DB, LAT = 16, 8, 32
NEG = -1.0e9
FMASK = -1.0e30
BIG = 1.0e30
LN_EPS = 1e-5
U = NT * HP
SPLIT = 16.0
UNSPLIT = 1.0 / SPLIT ** 2


def heads(u):
    p = u % HP
    return [p // 2 * 4 + p % 2 + 2 * h for h in range(2)]


PROLOGUE = [("A", "tr")] + [("A", "r", g) for g in range(4)] + [("A", "g", 0, 0), ("A", "g", 0, 1)]
PROLOGUE += [("A", "qk", j) for j in range(HP)] + [("A", "g", 0, 2), ("A", "g", 0, 3)]
PROLOGUE += [("A", "qk", j) for j in range(HP, 2 * HP)] + [("A", "v", t, h) for t in range(NT) for h in range(2)]


def a_steps():
    s = [("A", "ln")] + PROLOGUE
    for u in range(U + 2):
        t, p = divmod(u, HP)
        if u < U:
            s.append(("A", "s", u))
        if 1 <= u <= U:
            s.append(("A", "t", u - 1))
        if u >= 2:
            s.append(("A", "o", u - 2))
        if p == 6:
            s.append(("A", "pt", t, 0))
        if t and p == 2:
            s.append(("A", "pt", t - 1, 1))
        if t and p == 3 and u < U:
            s.append(("A", "pp", t - 1))
        if t + 1 < NT and p % 2 == 1:
            s.append(("A", "g", t + 1, p // 2))
    return s + [("A", "pt", NT - 1, 1), ("A", "pp", NT - 1)]


def experts(f, phase):
    s = [(f, "bc", phase, e) for e in range(AHEAD)]
    for e in range(NE):
        s.append((f, "mm", phase, e))
        if e + AHEAD < NE:
            s.append((f, "bc", phase, e + AHEAD))
    return s


AHEAD = 4


def routing_steps(f):
    return [(f, "ln"), (f, "sq"), (f, "tr"), (f, "gl"), (f, "ge"), (f, "gt")]


def f_steps(f):
    s = experts(f, "qkv") + [(f, "qkve"), (f, "vt")]
    for t in range(NT):
        s.append((f, "sc", t))
        if t:
            s.append((f, "tp", t - 1))
    return s + [(f, "tp", NT - 1), (f, "av")] + experts(f, "o") + [(f, "oe"), (f, "ot")]


def b_steps():
    s = [("B", "ln"), ("B", "tr"), ("B", "lat"), ("B", "bp", 0)]
    for t in range(NT):
        if t + 1 < NT:
            s.append(("B", "bp", t + 1))
        s.append(("B", "bq", t))
        if t:
            s.append(("B", "bv", t - 1))
    return s + [("B", "bv", NT - 1), ("B", "bo"), ("B", "br")]


STEPS = {"A": a_steps(), "B": b_steps(), "R": routing_steps("R"), "F1": f_steps("F1"),
         "F2": routing_steps("F2") + f_steps("F2")}


A_BANKS, F_BANKS = ["S0", "S1", "TP", "OV"], ["X0", "X1", "X2", "X3"]


def banks_of(s):
    stage, k = s[:2]
    if s in PROLOGUE:
        return [A_BANKS[PROLOGUE.index(s) % 4]]
    if stage == "A":
        if k == "s":
            return [A_BANKS[s[2] % 2]]
        if k == "o":
            return ["OV"] if s[2] % 4 == 3 else []
        return ["TP"] if k in ("t", "g", "pt", "pp") else []
    if stage == "B":
        if k == "bp":
            return [A_BANKS[s[2] % 2]]
        return {"tr": ["TP"], "lat": ["OV"], "bo": ["TP"], "br": ["OV"]}.get(k, [])
    if k == "sc":
        return [F_BANKS[s[2] % 2]]
    if k == "tp":
        return [F_BANKS[2 + s[2] % 2]]
    if k == "bc":
        return ["X0" if s[2] == "o" and s[3] % 2 else "X3"]
    return {"tr": ["X2"], "gl": ["X1"], "gt": ["X2"], "qkve": ["X0", "X1", "X2"], "vt": ["X3"],
            "av": ["X0"], "oe": ["X1"], "ot": ["X2"]}.get(k, [])


def bank_of(s):
    (one,) = banks_of(s)
    return one


USES = {g: {b: [s for s in STEPS[g] if b in banks_of(s)] for b in (A_BANKS if g in "AB" else F_BANKS)} for g in STEPS}


def lo_on_dve(phase, e):
    return phase == "o" and e % 2 == 1


def parts(s):
    stage, k = s[:2]
    if k == "ln":
        return [("dve", 1.3), ("pool", 1.3), ("dve", .8)]
    if k == "sq":
        return [("dve", .9), ("pool", 1.3)]
    if k == "tr":
        return [("pe", .43), ("act", .5)] + [("dve", .65)] * (stage == "A")
    if k in ("gt", "bo", "vt", "t", "pt"):
        return [("pe", .43), ("act", .5)]
    if k == "ot":
        return [("pe", .43), ("dve", .65)] + [("act", .1)] * (stage == "F2")
    if k == "r":
        return [("pe", .64), ("act", 1.2), ("dve", .7)]
    if k in ("qk", "v"):
        return [("pe", .64), ("act", .55)]
    if k == "g":
        return [("pe", .22), ("act", .5)]
    if k == "s":
        return [("pe", .85), ("dve", .95), ("act", .65)]
    if k == "o":
        return [("pe", .43)] + [("dve", .8)] * (s[2] % 4 == 3)
    if k == "pp":
        return [("pe", 1.9), ("dve", .25)]
    if k == "gl":
        return [("pe", .25), ("dve", .35)] + [("dve", 1.4)] * 4
    if k == "ge":
        return [("act", .2), ("dve", 1.1), ("dve", 1.0)]
    if k == "bc":
        return [("pe", .22), ("dve", .62), ("act", .54), ("dve", .62) if lo_on_dve(*s[2:]) else ("pool", 1.13)]
    if k == "mm":
        return [("pe", 1.92 if s[2] == "qkv" else .64)]
    if k == "qkve":
        return [("act", 1.5)]
    if k == "sc":
        return [("pe", .22 * (s[2] + 1)), ("dve", .3 + .13 * s[2]), ("act", .2 + .11 * s[2])]
    if k == "tp":
        return [("dve", .3 + .08 * s[2]), ("pe", .11 * (s[2] + 1)), ("act", .2 + .11 * s[2])]
    if k == "av":
        return [("pe", 2.1), ("act", .5)]
    if k == "oe":
        return [("act", .5)]
    if k == "lat":
        return [("pe", .85), ("act", .6)]
    if k == "bp":
        return [("pe", .7), ("dve", .5), ("pool", 2.2)]
    if k == "bq":
        return [("dve", 2.25), ("dve", 2.25), ("dve", .4), ("dve", .35), ("act", .35)]
    if k == "bv":
        return [("dve", .35), ("pool", 3.9), ("dve", 2.4), ("dve", .3)]
    assert k == "br"
    return [("pe", 1.3), ("dve", .65)]


def needs(s):
    stage, k = s[:2]
    n = []
    if k in ("qk", "v", "r", "gl"):
        n = [(stage, "tr")] + [(stage, "sq")] * (k == "gl") + ([(stage, k, s[2] - 2)] if k == "r" and s[2] > 1 else [])
    elif k == "g":
        half = s[2] * 4 + s[3]
        return [(("A", "r", s[3]), 0)] + [(("A", "g") + divmod(half - 1, 4), 4.5)] * (s[3] % 2 == 0 and half > 0)
    elif k == "s":
        t, p = divmod(s[2], HP)
        n = [(("A", "v", 3, 1), 0), (("A", "g", t, p // 4 * 2 + 1), 10)]
        n += [(("A", "t", s[2] - 2), 0)] * (s[2] >= 2)
        return n + ([(("A", "s", (t - 1) * HP + p // 4 * 4 + 3), 4.5)] if t else [])
    elif k == "t":
        n = [("A", "s", s[2])] + [("A", "o", s[2] - 2)] * (s[2] >= 2)
    elif k == "o":
        before = s[2] - 4
        n = [("A", "t", s[2])] + [("A", "pt", before // HP, before % HP // 4)] * (s[2] % 4 == 3 and before > 0)
    elif k == "pt":
        n = [("A", "o", s[2] * HP + 4 * s[3] + 3)]
    elif k == "pp":
        n = [("A", "pt", s[2], h) for h in (0, 1)]
    elif k == "mm":
        n = [(stage, "bc") + s[2:]]
    elif k == "bc":
        n = [(stage, "gt") if s[2] == "qkv" else (stage, "av")] if s != ("F1", "bc", "qkv", s[3]) else []
        if s[3] >= 4:
            n += [(stage, "bc", s[2], s[3] - 4), (stage, "mm", s[2], s[3] - 4)]
    elif k == "qkve":
        n = [(stage, "mm", "qkv", NE - 1)]
    elif k == "oe":
        n = [(stage, "mm", "o", NE - 1)]
    elif k == "sc":
        n = [(stage, "qkve")]
    elif k == "tp":
        n = [(stage, "sc", s[2])]
    elif k == "av":
        n = [(stage, "vt")] + [(stage, "tp", t) for t in range(NT)]
    elif k == "tr":
        n = [(stage, "ln")]
    elif k == "bp":
        n = [(stage, "lat")]
    elif k == "bq":
        n = [(stage, "bp", s[2])]
    elif k == "bv":
        n = [(stage, "bq", s[2])]
    elif s == ("F2", "ln"):
        n = [("F1", "ot"), ("B", "br")]
    elif k != "ln":
        n = [STEPS[stage][STEPS[stage].index(s) - 1]]
    return [(x, 0) for x in n]


def frees(s):
    return 1 if s[1] in ("s", "bc", "sc", "gl", "bp") else len(parts(s)) - 1


def takes(s):
    if s[1] == "mm" and s[3] == 0:
        return ["X0", "X1", "X2"] if s[2] == "qkv" else ["X1"]
    if s[1] == "o" and s[2] % 4 == 0:
        return ["OV"]
    return [] if s[1] in ("o", "qkve", "oe") else banks_of(s)


def lane(s, n):
    stage, k = s[:2]
    engine = parts(s)[n][0]
    if engine == "pe":
        return engine, stage in "AB", k if k in ("s", "o", "bc", "mm") else ""
    if engine == "dve" and stage not in "AB":
        return engine, stage in "AB", "lo" if k == "bc" and n == 3 else ""
    return engine, stage in "AB", "" if engine == "pool" and k != "bv" else k


def in_order(stages):
    streams = [[s for g in gs if g in stages for s in STEPS[g]] for gs in (("B", "A"), ("F1", "F2", "R"))]
    before, last_of, last_use = {}, {}, {}
    for stream in streams:
        for s in stream:
            for n in range(len(parts(s))):
                b = [((s, n - 1), .15)] if n else [((x, len(parts(x)) - 1), .15 + d) for x, d in needs(s) if x[0] in stages]
                if parts(s)[n][0] == "pe":
                    b += [(last_use[x], .15) for x in takes(s) if x in last_use]
                if lane(s, n) in last_of:
                    b.append((last_of[lane(s, n)], 0))
                last_of[lane(s, n)] = (s, n)
                before[s, n] = b
            for x in banks_of(s):
                last_use[x] = (s, frees(s))
    after = {p: [] for p in before}
    for p, b in before.items():
        for q, d in b:
            after[q].append((p, d))
    way, waiting = {}, {p: len(b) for p, b in before.items()}

    def length(p):
        if p not in way:
            way[p] = parts(p[0])[p[1]][1] + max([d + length(q) for q, d in after[p]] + [0.0])
        return way[p]

    for p in reversed(list(before)):
        length(p)
    ends, free, out = {}, dict.fromkeys(("pe", "dve", "act", "pool"), 0.0), {e: [] for e in ("pe", "dve", "act", "pool")}
    ready = {p: 0.0 for p, b in before.items() if not b}
    while ready:
        p = min(ready, key=lambda p: (max(ready[p], free[parts(p[0])[p[1]][0]]), -way[p]))
        engine, d = parts(p[0])[p[1]]
        ends[p] = free[engine] = max(ready.pop(p), free[engine]) + d
        s, n = p
        out[engine].append((s, sum(e == engine for e, _ in parts(s)[:n])))
        for q, _ in after[p]:
            waiting[q] -= 1
            if not waiting[q]:
                ready[q] = max(ends[b] + d for b, d in before[q])
    assert len(ends) == len(before)
    return out


LAG = {"A": 0, "R": 1, "F1": 2, "B": 3, "F2": 3}
STAGE_BEFORE = {"A": [("B", -3)], "B": [("A", 2)], "F1": [("R", 0), ("F2", -2)], "F2": [("F1", 1)], "R": [("F2", -2)]}


class Signal:

    AHEAD = 3

    def __init__(self, ctx, nc, name, keys, unit=1):
        self.sem = ctx.enter_context(nc.semaphore(name))
        self.turn = {k: n for n, k in enumerate(keys)}
        self.per, self.unit = len(keys), unit
        assert len(self.turn) == self.per

    def start(self):
        return self.AHEAD * self.per * self.unit

    def at(self, b, key=None):
        n = self.turn[key] + 1 if key is not None else self.per
        return (b + self.AHEAD) * (self.per * self.unit) + n * self.unit

    def before(self, b, key):
        return (b + self.AHEAD) * (self.per * self.unit) + self.turn[key] * self.unit


def stack_kernel(nc, x, a_wq, a_bq, a_wk, a_wv, a_wproj, a_bproj, a_wr, a_br, a_bfun, b_wq, b_bq, b_wdown, b_bdown,
                 b_wup, b_bup, b_wout, b_bout, f_sim, f_gates, f_q, f_k, f_v, f_o, rope, part_rows, out):
    f32, bf16, f16 = mybir.dt.float32, mybir.dt.bfloat16, mybir.dt.float16
    ALU, ACT, AX = mybir.AluOpType, mybir.ActivationFunctionType, mybir.AxisListType
    ctx = ExitStack()
    with ctx:
        def sb(name, shape, dt=f32):
            return ctx.enter_context(nc.sbuf_tensor(name, shape, dt))

        wqkv = sb("wqkv", [P, 3, 2, H * DQ], f16)
        wproj = sb("wproj", [P, HP, C])
        wr = sb("wr", [P, 2, 4, P], f16)
        bq = sb("bq", [P, HP])
        br = sb("br", [P, 4])
        bfun = sb("bfun", [P, 4, WIN], f16)
        neg_parts = sb("neg_parts", [P, 2])
        rows = sb("rows", [1, 2, C])
        ones = sb("ones", [P, P])
        ident = sb("ident", [P, P])
        wf = sb("wf", [P, 4, 2, NE, P], f16)
        sim = sb("sim", [P, NE])
        simn = sb("simn", [P, NE])
        sig = sb("sig", [P, NE])
        rank = sb("rank", [P, NE])
        select = sb("select", [P, NE, P], bf16)
        fmask = sb("fmask", [P, 3 * P + P])
        wqb = sb("wqb", [P, C])
        wdown = sb("wdown", [P, LAT])
        bdown = sb("bdown", [LAT, 1])
        wup = sb("wup", [LAT, 2 * C])
        biasb = sb("biasb", [P, 3 * C])
        wout = sb("wout", [P, C])
        ropet = sb("ropet", [P, NT, 2, DB])
        mhalf = sb("mhalf", [P, NE])
        res_a = sb("res_a", [P, NT, C])
        res_r = sb("res_r", [P, NT, C])
        res_x = sb("res_x", [P, NT, C])
        res_y = sb("res_y", [P, NT, C])
        ln_a = sb("ln_a", [P, 10 * NT])
        a_xn = sb("a_xn", [P, NT, C])
        a_xT = sb("a_xT", [P, 2, TOK], f16)
        QT = sb("QT", [P, HP, TOK])
        KT = sb("KT", [P, HP, TOK])
        V = sb("V", [P, NT, H * DQ])
        RT = sb("RT", [P, 4, TOK], f16)
        G = sb("G", [P, HP, WIN])
        E = sb("E", [P, 2, HP, 2 * P])
        L = sb("L", [P, 2, 2, 2 * P])
        mx = sb("mx", [P, 2, 2])
        nmx = sb("nmx", [P, 2, 2])
        sums = sb("sums", [P, 2, H])
        rsums = sb("rsums", [P, 2, HP])
        PT = sb("PT", [P, 2, 4, P])
        AO = sb("AO", [P, TOK])
        AT = sb("AT", [P, HP, P])
        ln_f = sb("ln_f", [P, 10 * NT])
        f_xn = sb("f_xn", [P, NT, C])
        f_xT = sb("f_xT", [P, TOK])
        ss = sb("ss", [P, 3, NT])
        lg = sb("lg", [P, NT, NE])
        gt = sb("gt", [P, 12, NT, NE])
        g1 = sb("g1", [P, 10, NT])
        gb = sb("gb", [P, 2, NT, NE], bf16)
        rwsp = sb("rwsp", [P, NT, P])
        rwT = sb("rwT", [P, TOK], bf16)
        xs = sb("xs", [P, 4, TOK])
        qkvT = sb("qkvT", [P, 3, TOK])
        vr = sb("vr", [P, NT, P])
        fm = sb("fm", [P, 4, NT])
        FPT = sb("FPT", [P, NT, TOK])
        aoT = sb("aoT", [P, TOK])
        oT = sb("oT", [P, TOK])
        yout = sb("yout", [P, NT, C])

        def flat(t):
            return t[:, :, :].rearrange("p a n -> p (a n)")

        xparts = flat(FPT).bitcast(f16).rearrange("p (s k n) -> p s k n", s=4, k=2)
        FP = xs[:, 2:4]
        f_sq = xs[:, 0].rearrange("p (t c) -> p t c", t=NT)
        in_v, in_k, in_q = flat(V), flat(KT), flat(QT)
        W = in_v[:, 0:2048]
        qkvb = in_v[:, 2048:2048 + NT * 3 * C].rearrange("p (t n) -> p t n", t=NT)
        latT = V[0:LAT, NT - 1, H * DQ - TOK:]
        W2 = in_q[:, 2048:4096]
        rp = in_k[:, 0:512].rearrange("p (b n) -> p b n", b=2)
        att = in_k[:, 512:1536].rearrange("p (a n) -> p a n", a=NT)
        pb = in_k[:, 1536:2560].rearrange("p (a n) -> p a n", a=NT)
        ato = in_k[:, 2560:3072].rearrange("p (t c) -> p t c", t=NT)
        b_xT = in_k[:, 3072:3584]
        b_oT = in_k[:, 3584:4096]
        b_xn = in_q[:, 0:512].rearrange("p (t c) -> p t c", t=NT)
        ln_b = in_q[:, 512:512 + 10 * NT]
        bm = in_q[:, 600:600 + 3 * NT * HB].rearrange("p (a k h) -> p a k h", a=NT, k=3)
        qkr = in_q[:, 1024:2048].rearrange("p (a n) -> p a n", a=NT)
        stage_f = [in_q[:, 0:2048], in_q[:, 2048:4096], in_k[:, 0:2048], in_k[:, 2048:4096]]
        stage_qkv = [in_v[:, j * 1024:(j + 1) * 1024] for j in range(3)]
        stage_wr = flat(G)[:, 0:512]
        stage_bfun = flat(G)[:, 512:1024]

        names = A_BANKS + F_BANKS
        bank = {n: ctx.enter_context(nc.psum_tensor(f"bank_{n}", [P, TOK], f32)) for n in names}
        scratch = nc.dram_tensor("bias_scratch", (2 * NT, P, HP, 2 * P), f32, kind="Internal")
        row = HP * 2 * P

        def signal(name, keys, unit=1):
            return Signal(ctx, nc, name, keys, unit)

        full = {g: {n: signal(f"full_{g}_{n}", [s for s in u if s[1] != "o"]) for n, u in USES[g].items() if u}
                for g in USES}
        free = {g: {n: signal(f"free_{g}_{n}", u) for n, u in USES[g].items() if u} for g in USES}
        loaded = ctx.enter_context(nc.semaphore("loaded"))
        made = ctx.enter_context(nc.semaphore("made"))
        filled = ctx.enter_context(nc.semaphore("filled"))
        set_up = ctx.enter_context(nc.semaphore("set_up"))
        setup_mm = ctx.enter_context(nc.semaphore("setup_mm"))
        setup_act = ctx.enter_context(nc.semaphore("setup_act"))
        passed = ctx.enter_context(nc.semaphore("passed"))
        halves = [(t, g) for t in range(NT) for g in range(2)]
        x_in = signal("x_in", ["x"], 16)
        a_hi = signal("a_hi", ["x"])
        r_act = signal("r_act", [(g, k) for g in range(4) for k in (0, 1)])
        bias_out = signal("bias_out", halves, 16)
        bias_in = signal("bias_in", halves, 16)
        maxed = signal("maxed", list(range(U)))
        probs = signal("probs", list(range(U)))
        attended = signal("attended", list(range(U)))
        handed_r = signal("handed_r", ["x"])
        handed_x = signal("handed_x", ["x"])
        handed_y = signal("handed_y", ["x"])
        stats_of = ["A", "B", "R", "F2"]
        stats = {g: signal(f"stats_{g}", ["x"]) for g in stats_of}
        spread = {g: signal(f"spread_{g}", ["x"]) for g in stats_of}
        normed = {g: signal(f"normed_{g}", ["x"]) for g in stats_of}
        F, ROUTERS = ["F1", "F2"], ["R", "F2"]
        squared = {f: signal(f"squared_{f}", ["x"]) for f in ROUTERS}
        scaled = {f: signal(f"scaled_{f}", ["x"]) for f in ROUTERS}
        gated = {f: signal(f"gated_{f}", ["x"]) for f in ROUTERS}
        gate_exp = {f: signal(f"gate_exp_{f}", ["x"]) for f in ROUTERS}
        routed = {f: signal(f"routed_{f}", ["x"]) for f in ROUTERS}
        each = [(ph, e) for ph in ("qkv", "o") for e in range(NE)]
        x_hi = {f: signal(f"x_hi_{f}", each) for f in F}
        lo_pool = {f: signal(f"lo_pool_{f}", [k for k in each if not lo_on_dve(*k)]) for f in F}
        lo_dve = {f: signal(f"lo_dve_{f}", [k for k in each if lo_on_dve(*k)]) for f in F}
        tiles = list(range(NT))
        f_maxed = {f: signal(f"f_maxed_{f}", tiles) for f in F}
        f_probs = {f: signal(f"f_probs_{f}", tiles) for f in F}
        f_inv = {f: signal(f"f_inv_{f}", tiles) for f in F}
        f_norm = {f: signal(f"f_norm_{f}", tiles) for f in F}
        roped = signal("roped", tiles)
        b_shift = signal("b_shift", tiles)
        b_exp = signal("b_exp", tiles)
        b_sum = signal("b_sum", tiles)
        b_weighed = signal("b_weighed", tiles)
        b_att = signal("b_att", tiles)
        y_out = signal("y_out", ["y"], 16)
        dve_chain = {"A": signal("dve_A", list(range(1 + 2 * NT))), "B": signal("dve_B", list(range(1 + 4 * NT)))}
        dve_chain |= {f: signal(f"dve_{f}", list(range(1 + 27))) for f in ROUTERS}
        pool_chain = {"A": signal("pool_A", list(range(1))), "B": signal("pool_B", list(range(1 + 3 * NT)))}
        pool_chain |= {f: signal(f"pool_{f}", list(range(2))) for f in ROUTERS}

        def lo_of(f, phase, e):
            return (lo_dve if lo_on_dve(phase, e) else lo_pool)[f]

        def wait_apart(eng, sem, value):
            eng.wait_ge(sem, value)
            eng.sem_inc(passed, 1)

        class Chain:

            def __init__(self, eng, sig, b, apart=False):
                self.eng, self.sig, self.b, self.apart, self.n = eng, sig, b, apart, 0

            def __call__(self, ins):
                self.n += 1
                ins.then_inc(self.sig.sem, 1)
                self.eng.wait_ge(self.sig.sem, (self.b + Signal.AHEAD) * self.sig.per + self.n)
                if self.apart:
                    self.eng.sem_inc(passed, 1)

        def chains(eng, sigs, batch, apart=False):
            return {g: Chain(eng, sigs[g], batch[g], apart) for g in sigs if batch[g] is not None}

        def batches(eng, body):
            def of(i):
                return {g: i - lag if 0 <= i - lag < NBATCH else None for g, lag in LAG.items()}

            full_from = max(LAG.values())
            for i in range(full_from):
                body(of(i))
            with eng.Fori(full_from, NBATCH) as i:
                body({g: i - lag if lag else i for g, lag in LAG.items()})
            for i in range(NBATCH, NBATCH + full_from):
                body(of(i))

        def work(engine, batch):
            return [(s, batch[s[0]], n) for s, n in in_order([g for g in STEPS if batch[g] is not None])[engine]]

        def starts(eng, mine):
            for s in mine:
                eng.sem_inc(s.sem, s.start())

        up = b_wup.rearrange("l (h s d) -> l s h d", s=2, d=DB)
        bup = b_bup.rearrange("(a h s d) -> a s h d", a=1, s=2, d=DB)
        brv = a_br.rearrange("(g q n) -> q n g", g=4, n=NB)
        loads = list(zip(stage_qkv, (a_wq, a_wk, a_wv)))
        loads += [(bq[:, :], a_bq.rearrange("(j p) -> p j", p=P)), (neg_parts[:, :], part_rows),
                  (sim[:, :], f_sim), (sig[:, :], f_gates.rearrange("(a c) -> a c", a=1).to_broadcast([P, NE]))]
        loads += [(stage_f[j].rearrange("p (e h) -> p e h", e=NE), w.rearrange("e c h -> c e h"))
                  for j, w in enumerate((f_q, f_k, f_v, f_o))]
        loads += [(wproj[:, :, :], a_wproj.rearrange("(j p) c -> p j c", p=P)),
                  (rows[:, 0, :], a_bproj.rearrange("(a c) -> a c", a=1)),
                  (rows[:, 1, :], b_bout.rearrange("(a c) -> a c", a=1)),
                  (wqb[:, :], b_wq), (wdown[:, :], b_wdown), (bdown[:, :], b_bdown.rearrange("(p a) -> p a", a=1)),
                  (biasb[:, 0:C], b_bq.rearrange("(a c) -> a c", a=1).to_broadcast([P, C])),
                  (wout[:, :], b_wout), (ropet[:, :, :, :], rope)]
        for j in range(2):
            loads += [(wup[:, j * C:(j + 1) * C].rearrange("l (h d) -> l h d", d=DB), up[:, j]),
                      (biasb[:, (j + 1) * C:(j + 2) * C].rearrange("p (h d) -> p h d", d=DB),
                       bup[:, j].to_broadcast([P, HB, DB]))]
        LOADED = 16 * (len(loads) + 3 + 4 * 3 * 2)
        CLEARED, MADE = 4, 9 + NE + 5
        SPLITS = 3 + 4 + 2
        SET_UP = 5 + SPLITS

        xv = x.rearrange("b (t p) c -> b p t c", p=P)
        outv = out.rearrange("b (t p) c -> b p t c", p=P)

        block = ctx.enter_context(nc.Block())

        @block.sync
        def _(sp):
            starts(sp, [x_in, bias_out, bias_in])
            for dst, src in loads:
                sp.dma_start(dst, src, allow_slow_non_contiguous=True).then_inc(loaded, 16)
            wait_apart(sp, made, CLEARED)
            wr_heads = stage_wr.rearrange("c (h r) -> c h r", r=32)
            for k in range(3):
                sp.dma_start(wr_heads[:, :, k * NB:(k + 1) * NB],
                             a_wr.rearrange("c (h n) -> c h n", n=NB)).then_inc(loaded, 16)
                for q in range(4):
                    at = slice(32 * q + k * NB, 32 * q + (k + 1) * NB)
                    sp.dma_start(stage_bfun[at, q * WIN:(q + 1) * WIN], a_bfun).then_inc(loaded, 16)
                    sp.dma_start(br[at, :], brv[q], allow_slow_non_contiguous=True).then_inc(loaded, 16)
            for n in range(2 * NT):
                sp.dma_start(scratch.ap()[n].rearrange("p h k -> p (h k)"),
                             E[:, 0].rearrange("p h k -> p (h k)")).then_inc(filled, 16)
            wait_apart(sp, filled, 16 * 2 * NT)
            wait_apart(sp, set_up, SET_UP)

            def body(batch):
                a = batch["A"]
                if a is None:
                    return
                wait_apart(sp, handed_r.sem, handed_r.before(a, "x"))
                sp.dma_start(res_a[:, :, :], xv[a]).then_inc(x_in.sem, 16)
                for n, (t, g) in enumerate(halves):
                    made_by = ("A", "g", t, 2 * g + 1)
                    sig = free["A"][bank_of(made_by)]
                    wait_apart(sp, sig.sem, sig.at(a, made_by))
                    skew = bass.AP(tensor=scratch, offset=n * P * row + 1, ap=[[row + 1, P], [2 * P, HP], [1, WIN]])
                    sp.dma_start(skew, G[:, :, :]).then_inc(bias_out.sem, 16)
                    wait_apart(sp, bias_out.sem, bias_out.at(a, (t, g)))
                    last = ("A", "s", (t - 1) % NT * HP + 4 * g + 3)
                    sig = free["A"]["S1"]
                    wait_apart(sp, sig.sem, sig.at(a if t else a - 1, last))
                    sp.dma_start(E[:, g], scratch.ap()[n]).then_inc(bias_in.sem, 16)

            batches(sp, body)

        @block.gpsimd
        def _(pool):
            v = nc.gpsimd
            starts(pool, list(spread.values()) + list(pool_chain.values()) + list(scaled.values())
                   + list(lo_pool.values()) + [roped, b_weighed])
            v.memset(E[:, 0].rearrange("p h k -> p (h k)"), NEG).then_inc(made, 1)
            v.memset(stage_wr, 0.0).then_inc(made, 1)
            v.memset(stage_bfun, 0.0).then_inc(made, 1)
            v.memset(br[:, :], 0.0).then_inc(made, 1)
            v.memset(ident[:, :], 0.0).then_inc(made, 1)
            v.memset(select[:, :, :], 0.0).then_inc(made, 1)
            v.memset(fmask[:, :], 0.0).then_inc(made, 1)
            v.memset(ones[:, :], 1.0).then_inc(made, 1)
            v.memset(mhalf[:, :], -0.5).then_inc(made, 1)
            for e in range(NE):
                v.memset(rank[:, e:e + 1], float(NE - e)).then_inc(made, 1)
            n = 9 + NE
            wait_apart(pool, made, n)
            v.affine_select(out=ident[:, :], in_=ident[:, :], compare_op=ALU.not_equal, fill=1.0, base=0,
                            pattern=[[-1, P]], channel_multiplier=1).then_inc(made, 1)
            v.affine_select(out=fmask[:, 3 * P:], in_=fmask[:, 3 * P:], compare_op=ALU.is_ge, fill=FMASK, base=0,
                            pattern=[[-1, P]], channel_multiplier=1).then_inc(made, 1)
            for s in range(3):
                v.affine_select(out=select[:, :, :], in_=select[:, :, :], compare_op=ALU.not_equal, fill=SPLIT,
                                base=-NE * s, pattern=[[-1, NE], [0, P]], channel_multiplier=1).then_inc(made, 1)
                wait_apart(pool, made, n + 3 + s)
            assert n + 5 == MADE
            v.memset(rwsp[:, :, :], 0.0).then_inc(made, 1)
            wait_apart(pool, made, MADE + 1)
            wait_apart(pool, loaded, LOADED)
            wait_apart(pool, set_up, SET_UP - 1)
            v.tensor_tensor(out=lg[:, 1, :], in0=lg[:, 0, :], in1=mhalf[:, :], op=ALU.pow).then_inc(made, 1)
            wait_apart(pool, set_up, SET_UP)

            def deviation(g, b, then, ln):
                mv = ln[:, 6 * NT:8 * NT].rearrange("p (t k) -> p t k", k=2)
                rs = ln[:, 8 * NT:10 * NT].rearrange("p (k t) -> p k t", k=2)
                wait_apart(pool, stats[g].sem, stats[g].at(b, "x"))
                then(v.tensor_scalar(rs[:, 0], mv[:, :, 1], LN_EPS, None, ALU.add))
                v.tensor_tensor(out=rs[:, 1], in0=rs[:, 0], in1=mhalf[:, 0:NT], op=ALU.pow).then_inc(spread[g].sem, 1)

            def rotate(b, then, s):
                t = s[2]
                src = qkvb[:, t, 0:2 * C].rearrange("p (h s d) -> p h s d", s=2, d=DB // 2)
                both = qkvb[:, t, 0:2 * C].rearrange("p (h d) -> p h d", d=DB)
                cos = ropet[:, t, 0, :].unsqueeze(1).to_broadcast([P, 2 * HB, DB])
                r = rp
                swapped = r[:, 1].rearrange("p (h s d) -> p h s d", s=2, d=DB // 2)
                sig = free["B"][bank_of(s)]
                wait_apart(pool, sig.sem, sig.at(b, s))
                wait_apart(pool, roped.sem, roped.before(b, t))
                then(v.tensor_tensor(out=r[:, 0].rearrange("p (h d) -> p h d", d=DB), in0=both, in1=cos, op=ALU.mult))
                for h in range(2):
                    sin = ropet[:, t, 1, h * 4:h * 4 + 4].unsqueeze(1).to_broadcast([P, 2 * HB, DB // 2])
                    then(v.tensor_tensor(out=swapped[:, :, h], in0=src[:, :, 1 - h], in1=sin, op=ALU.mult))
                v.tensor_tensor(out=qkr[:, t], in0=r[:, 0], in1=r[:, 1], op=ALU.add).then_inc(roped.sem, 1)

            def body(batch):
                then = chains(pool, pool_chain, batch, apart=True)
                for s, b, _ in work("pool", batch):
                    g, k = s[:2]
                    if k == "ln":
                        deviation(g, b, then[g], {"A": ln_a[:, :], "B": ln_b}.get(g, ln_f[:, :]))
                    elif k == "sq":
                        wait_apart(pool, squared[g].sem, squared[g].at(b, "x"))
                        then[g](v.tensor_scalar(ss[:, 1], ss[:, 0], 1e-12, None, ALU.add))
                        v.tensor_tensor(out=ss[:, 2], in0=ss[:, 1], in1=mhalf[:, 0:NT],
                                        op=ALU.pow).then_inc(scaled[g].sem, 1)
                    elif k == "bc":
                        phase, e = s[2:]
                        wait_apart(pool, x_hi[g].sem, x_hi[g].at(b, (phase, e)))
                        v.tensor_tensor(out=xparts[:, e % 4, 1], in0=xs[:, e % 4], in1=xparts[:, e % 4, 0],
                                        op=ALU.subtract).then_inc(lo_pool[g].sem, 1)
                    elif k == "bp":
                        rotate(b, then[g], s)
                    elif k == "bv":
                        t = s[2]
                        full_shape = [P, HB, DB, HB]
                        wait_apart(pool, b_exp.sem, b_exp.at(b, t))
                        wait_apart(pool, b_att.sem, b_att.before(b, t))
                        v.tensor_tensor(out=W2.rearrange("p (h d g) -> p h d g", d=DB, g=HB),
                                        in0=pb[:, t].rearrange("p (h g) -> p h g", g=HB).unsqueeze(2).to_broadcast(full_shape),
                                        in1=qkvb[:, t, 2 * C:].rearrange("p (g d) -> p d g", d=DB).unsqueeze(1
                                            ).to_broadcast(full_shape), op=ALU.mult).then_inc(b_weighed.sem, 1)
                for g, c in then.items():
                    assert c.n == c.sig.per, (g, c.n)

            batches(pool, body)

        @block.scalar
        def _(act):
            v = nc.scalar
            starts(act, [s for g in full for n, s in free[g].items() if n in ("S0", "S1", "TP", "X2")]
                   + [probs, a_hi, r_act, b_exp, y_out] + list(gate_exp.values()) + list(f_probs.values())
                   + list(x_hi.values()))

            def copy(dst, src, scale=1.0):
                return v.activation(dst, src, ACT.Copy, scale=scale)

            act.wait_ge(loaded, LOADED)
            for j in range(3):
                copy(wqkv[:, j, 0], stage_qkv[j], SPLIT).then_inc(setup_act, 1)
            copy(wr[:, 0].rearrange("p g r -> p (g r)"), stage_wr, SPLIT).then_inc(setup_act, 1)
            copy(PT[:, 0, 0:2, :].rearrange("p a t -> p (a t)").bitcast(f16), stage_bfun, SPLIT).then_inc(setup_act, 1)
            for j in range(4):
                copy(wf[:, j, 0].rearrange("p e h -> p (e h)"), stage_f[j], SPLIT).then_inc(setup_act, 1)
            v.activation(sig[:, :], sig[:, :], ACT.Exp, scale=-1.0).then_inc(setup_act, 1)
            copy(bq[:, :], bq[:, :], DQ ** -0.5).then_inc(setup_act, 1)
            copy(br[:, :], br[:, :], SPLIT).then_inc(setup_act, 1)
            act.wait_ge(setup_act, SPLITS + 3)
            act.wait_ge(set_up, SET_UP)

            def body(batch):
                for s, b, _ in work("act", batch):
                    g, k = s[:2]

                    def filled_bank(n):
                        act.wait_ge(full[g][n].sem, full[g][n].at(b, s))
                        return bank[n]

                    if k == "tr" and g == "A":
                        copy(a_xT[:, 0], filled_bank(bank_of(s))[:, :], SPLIT).then_inc(a_hi.sem, 1)
                    elif k == "r":
                        r = s[2]
                        if r >= 2:
                            act.wait_ge(free[g][bank_of(("A", "r", r - 2))].sem,
                                        free[g][bank_of(("A", "r", r - 2))].at(b, ("A", "r", r - 2)))
                        v.activation(L[:, r % 2].rearrange("p h n -> p (h n)"), filled_bank(bank_of(s))[:, :],
                                     ACT.Identity, bias=br[:, r:r + 1], scale=1.0 / SPLIT).then_inc(r_act.sem, 1)
                        act.wait_ge(r_act.sem, r_act.at(b, (r, 0)))
                        copy(PT[:, r % 2, 0:2, :].rearrange("p a t -> p (a t)").bitcast(f16),
                             L[:, r % 2].rearrange("p h n -> p (h n)")).then_inc(r_act.sem, 1)
                    elif g == "A" and k in ("g", "qk", "v", "t", "pt"):
                        if k == "g" and s[3] % 2 == 0:
                            act.wait_ge(bias_out.sem, bias_out.before(b, (s[2], s[3] // 2)))
                        n = bank_of(s)
                        src = filled_bank(n)
                        if k == "g":
                            i = copy(G[:, 4 * (s[3] % 2):4 * (s[3] % 2) + 4, :],
                                     src[:, :].rearrange("p (h d) -> p h d", h=4), UNSPLIT)
                        elif k == "qk" and s[2] < HP:
                            i = v.activation(QT[:, s[2], :], src[:, :], ACT.Identity, bias=bq[:, s[2]:s[2] + 1],
                                             scale=UNSPLIT * DQ ** -0.5)
                        elif k == "qk":
                            i = copy(KT[:, s[2] - HP, :], src[:, :], UNSPLIT)
                        elif k == "v":
                            i = copy(V[:, s[2], s[3] * TOK:(s[3] + 1) * TOK], src[:, :], UNSPLIT)
                        elif k == "t":
                            m = 4 if s[2] >= HP else 2
                            i = copy(PT[:, s[2] % 2, 0:m, :], src[:, 0:m * P].rearrange("p (k t) -> p k t", t=P))
                        else:
                            i = copy(AT[:, 4 * s[3]:4 * s[3] + 4, :], src[:, :].rearrange("p (k t) -> p k t", t=P))
                        i.then_inc(free[g][n].sem, 1)
                    elif k == "s":
                        u = s[2]
                        t = u // HP
                        lo = 0 if t else P
                        act.wait_ge(maxed.sem, maxed.at(b, u))
                        for h, head in enumerate(heads(u)):
                            i = v.activation(L[:, u % 2, h, lo:], L[:, u % 2, h, lo:], ACT.Exp,
                                             bias=nmx[:, u % 2, h:h + 1], accum_out=sums[:, t % 2, head:head + 1])
                        i.then_inc(probs.sem, 1)
                    elif k in ("tr", "gt", "vt", "av", "oe", "bo"):
                        n = bank_of(s)
                        src = filled_bank(n)[:, :]
                        dst = {"tr": b_xT if g == "B" else f_xT[:, :], "gt": rwT[:, :],
                               "vt": vr[:, :, :].rearrange("p t h -> p (t h)"), "av": aoT[:, :], "oe": oT[:, :],
                               "bo": b_oT}[k]
                        copy(dst, src, UNSPLIT if k == "oe" else 1.0).then_inc(free[g][n].sem, 1)
                    elif k == "ge":
                        act.wait_ge(gated[g].sem, gated[g].at(b, "x"))
                        v.activation(gt[:, 11], gt[:, 10], ACT.Exp).then_inc(gate_exp[g].sem, 1)
                    elif k == "bc":
                        phase, e = s[2:]
                        made_xs = free[g][bank_of(s)]
                        act.wait_ge(made_xs.sem, made_xs.at(b, s))
                        copy(xparts[:, e % 4, 0], xs[:, e % 4]).then_inc(x_hi[g].sem, 1)
                    elif k == "qkve":
                        for j in range(3):
                            copy(qkvT[:, j, :], filled_bank(f"X{j}")[:, :], UNSPLIT).then_inc(free[g][f"X{j}"].sem, 1)
                    elif k == "sc":
                        t = s[2]
                        n = (t + 1) * P
                        act.wait_ge(f_maxed[g].sem, f_maxed[g].at(b, t))
                        v.activation(FP[:, t % 2, 0:n], FP[:, t % 2, 0:n], ACT.Exp, bias=fm[:, 1, t:t + 1],
                                     scale=P ** -0.5, accum_out=fm[:, 2, t:t + 1]).then_inc(f_probs[g].sem, 1)
                    elif k == "tp":
                        t = s[2]
                        n = bank_of(s)
                        copy(FPT[:, 0:t + 1, t * P:(t + 1) * P],
                             filled_bank(n)[:, 0:(t + 1) * P].rearrange("p (k t) -> p k t", t=P)
                             ).then_inc(free[g][n].sem, 1)
                    elif k == "ot" and g == "F2":
                        act.wait_ge(free[g]["X2"].sem, free[g]["X2"].at(b, s))
                        act.dma_start(outv[b], yout[:, :, :]).then_inc(y_out.sem, 16)
                    elif k == "lat":
                        v.activation(latT, filled_bank("OV")[0:LAT, :], ACT.Identity,
                                     bias=bdown[:, :]).then_inc(free[g]["OV"].sem, 1)
                    elif k == "bq":
                        t = s[2]
                        act.wait_ge(b_shift.sem, b_shift.at(b, t))
                        v.activation(pb[:, t], att[:, t], ACT.Exp, scale=DB ** -0.5).then_inc(b_exp.sem, 1)

            batches(act, body)
            act.wait_ge(y_out.sem, y_out.at(NBATCH - 1))

        @block.vector
        def _(dve):
            v = nc.vector
            starts(dve, [s for g in full for n, s in free[g].items() if n in ("OV", "X0", "X1", "X3")]
                   + [maxed, handed_r, handed_x, handed_y, b_shift, b_sum, b_att] + list(stats.values()) + list(normed.values()) + list(squared.values())
                   + list(gated.values()) + list(routed.values()) + list(lo_dve.values()) + list(f_maxed.values())
                   + list(f_inv.values()) + list(f_norm.values()) + list(dve_chain.values()))
            n = 0

            def then(ins):
                nonlocal n
                n += 1
                ins.then_inc(set_up, 1)
                dve.wait_ge(set_up, n)

            def split(dst, src, hi):
                return v.scalar_tensor_tensor(dst, src, SPLIT, hi, ALU.mult, ALU.subtract)

            dve.wait_ge(made, MADE)
            dve.wait_ge(loaded, LOADED)
            for j in range(3):
                dve.wait_ge(setup_act, j + 1)
                then(split(wqkv[:, j, 1], stage_qkv[j], wqkv[:, j, 0]))
            dve.wait_ge(setup_act, 4)
            then(split(wr[:, 1].rearrange("p g r -> p (g r)"), stage_wr, wr[:, 0].rearrange("p g r -> p (g r)")))
            dve.wait_ge(setup_act, 5)
            then(v.tensor_scalar(stage_bfun, stage_bfun, SPLIT, None, ALU.mult))
            then(v.scalar_tensor_tensor(bfun[:, :, :].rearrange("p q d -> p (q d)"),
                                        PT[:, 0, 0:2, :].rearrange("p a t -> p (a t)").bitcast(f16),
                                        neg_parts[:, 1:2], stage_bfun, ALU.mult, ALU.add))
            for j in range(4):
                dve.wait_ge(setup_act, 6 + j)
                w = wf[:, j].rearrange("p k e h -> p k (e h)")
                then(split(w[:, 1], stage_f[j], w[:, 0]))
            dve.wait_ge(setup_act, SPLITS + 3)
            v.tensor_scalar(sig[:, :], sig[:, :], 1.0, None, ALU.add).then_inc(setup_act, 1)
            dve.wait_ge(setup_act, SPLITS + 4)
            then(v.reciprocal(sig[:, :], sig[:, :]))
            then(v.tensor_tensor(out=simn[:, :], in0=sim[:, :], in1=sim[:, :], op=ALU.mult))
            dve.wait_ge(setup_mm, 1)
            then(v.tensor_scalar(lg[:, 0, :], bank["X3"][:, 0:NE], 1e-12, None, ALU.add))
            dve.wait_ge(made, MADE + 2)
            then(v.tensor_tensor(out=simn[:, :], in0=sim[:, :], in1=lg[:, 1, :], op=ALU.mult))
            assert n == SET_UP, n

            def statistics(g, b, then, src, ln):
                st = ln[:, 0:6 * NT].rearrange("p (t k) -> p t k", k=6)
                mv = ln[:, 6 * NT:8 * NT].rearrange("p (t k) -> p t k", k=2)
                for t in range(NT):
                    i = v.bn_stats(out=st[:, t], in_=src[:, t])
                then(i)
                dve.sem_inc(passed, 1)
                for t in range(NT):
                    i = v.bn_aggr(out=mv[:, t], in_=st[:, t])
                i.then_inc(stats[g].sem, 1)

            A = lambda n: gt[:, n]
            S = lambda n: g1[:, n]
            wide = lambda a: a.unsqueeze(2).to_broadcast([P, NT, NE])
            all_t = lambda a: a.unsqueeze(1).to_broadcast([P, NT, NE])
            tt = lambda o, a, c, op: v.tensor_tensor(out=o, in0=a, in1=c, op=op)
            red = lambda o, a, op: v.tensor_reduce(out=o, in_=a, axis=AX.X, op=op)

            def normalize(g, b, src, ln, xn):
                mv = ln[:, 6 * NT:8 * NT].rearrange("p (t k) -> p t k", k=2)
                dve.wait_ge(spread[g].sem, spread[g].at(b, "x"))
                for t in range(NT):
                    i = v.tensor_scalar(xn[:, t], src[:, t], mv[:, t, 0:1], ln[:, 9 * NT + t:9 * NT + t + 1],
                                        ALU.subtract, ALU.mult)
                i.then_inc(normed[g].sem, 1)

            def gate(f, then, quarter):
                if quarter == 0:
                    then(tt(A(0), lg[:, :, :], all_t(sig[:, :]), ALU.subtract))
                    then(v.tensor_scalar(A(1), A(0), 0.0, None, ALU.max))
                    then(v.tensor_scalar(A(2), A(0), 0.0, None, ALU.is_gt))
                    then(red(S(0), A(0), ALU.max))
                    then(tt(A(3), A(0), wide(S(0)), ALU.is_equal))
                    then(tt(A(4), A(3), all_t(rank[:, :]), ALU.mult))
                if quarter == 1:
                    then(red(S(1), A(4), ALU.max))
                    then(tt(A(5), A(4), wide(S(1)), ALU.is_equal))
                    then(v.scalar_tensor_tensor(A(7), A(5), -BIG, A(0), ALU.mult, ALU.add))
                    then(red(S(2), A(7), ALU.max))
                    then(tt(A(3), A(7), wide(S(2)), ALU.is_equal))
                if quarter == 2:
                    then(tt(A(4), A(3), all_t(rank[:, :]), ALU.mult))
                    then(red(S(3), A(4), ALU.max))
                    then(tt(A(6), A(4), wide(S(3)), ALU.is_equal))
                    then(tt(A(7), A(5), A(6), ALU.add))
                    then(red(S(4), A(2), ALU.max))
                if quarter == 3:
                    then(v.tensor_scalar(S(5), S(4), -1.0, 1.0, ALU.mult, ALU.add))
                    then(tt(A(8), A(7), wide(S(5)), ALU.mult))
                    then(tt(A(9), A(8), A(2), ALU.add))
                    then(red(S(6), A(1), ALU.max))
                    tt(A(10), A(1), wide(S(6)), ALU.subtract).then_inc(gated[f].sem, 1)

            def weigh(f, b, then, half):
                if half == 1:
                    then(tt(A(5), A(4), gb[:, 0], ALU.subtract))
                    then(v.tensor_copy(gb[:, 1], A(5)))
                    v.tensor_copy(rwsp[:, :, 0:NE], gb[:, 0])
                    v.tensor_copy(rwsp[:, :, NE:2 * NE], gb[:, 1])
                    tt(rwsp[:, :, 2 * NE:3 * NE], A(5), gb[:, 1], ALU.subtract).then_inc(routed[f].sem, 1)
                    return
                dve.wait_ge(gate_exp[f].sem, gate_exp[f].at(b, "x"))
                then(tt(A(3), A(11), A(9), ALU.mult))
                then(red(S(7), A(3), ALU.add))
                then(v.reciprocal(S(8), S(7)))
                then(tt(A(4), A(3), wide(S(8)), ALU.mult))
                then(v.tensor_copy(gb[:, 0], A(4)))

            def body(batch):
                chain = chains(dve, dve_chain, batch)
                for s, b, part in work("dve", batch):
                    g, k = s[:2]
                    then = chain.get(g)

                    def filled_bank(n):
                        dve.wait_ge(full[g][n].sem, full[g][n].at(b, s))
                        return bank[n]

                    def wait_step(stage, batch_no, step):
                        n = bank_of(step)
                        dve.wait_ge(free[stage][n].sem, free[stage][n].at(batch_no, step))

                    if k == "ln":
                        src, ln, xn, came = {"A": (res_a, ln_a[:, :], a_xn, x_in), "B": (res_y, ln_b, b_xn, handed_y),
                                             "R": (res_r, ln_f[:, :], f_xn, handed_r),
                                             "F2": (res_y, ln_f[:, :], f_xn, handed_y)}[g]
                        if part == 1:
                            normalize(g, b, src, ln, xn)
                        else:
                            dve.wait_ge(came.sem, came.at(b, "x"))
                            if g == "F2":
                                wait_step("B", b, ("B", "br"))
                            statistics(g, b, then, src, ln)
                    elif k == "tr" and g == "A":
                        n = bank_of(s)
                        dve.wait_ge(a_hi.sem, a_hi.at(b, "x"))
                        split(a_xT[:, 1], bank[n][:, :], a_xT[:, 0]).then_inc(free[g][n].sem, 1)
                    elif k == "r":
                        r = s[2]
                        dve.wait_ge(r_act.sem, r_act.at(b, (r, 1)))
                        v.scalar_tensor_tensor(RT[:, r], PT[:, r % 2, 0:2, :].rearrange("p a t -> p (a t)").bitcast(f16),
                                               neg_parts[:, 0:1], L[:, r % 2].rearrange("p h n -> p (h n)"),
                                               ALU.mult, ALU.add).then_inc(free[g][bank_of(s)].sem, 1)
                    elif k == "s":
                        u = s[2]
                        t, p = divmod(u, HP)
                        lo = 0 if t else P
                        n = bank_of(s)
                        dve.wait_ge(bias_in.sem, bias_in.at(b, (t, p // 4)))
                        wait_apart(dve, full[g][n].sem, full[g][n].at(b, s))
                        for h, head in enumerate(heads(u)):
                            i = v.tensor_tensor_reduce(
                                out=L[:, u % 2, h, lo:], in0=bank[n][:, h * 2 * P + lo:(h + 1) * 2 * P],
                                in1=E[:, p // 4, head % 8, lo:], scale=1.0, scalar=-3.0e38, op0=ALU.add, op1=ALU.max,
                                accum_out=mx[:, u % 2, h:h + 1])
                        i.then_inc(free[g][n].sem, 1)
                        wait_step(g, b, s)
                        v.tensor_scalar(nmx[:, u % 2], mx[:, u % 2], -1.0, None, ALU.mult).then_inc(maxed.sem, 1)
                    elif k == "o" and s[2] % 4 == 3:
                        u = s[2]
                        t, q = u // HP, u % HP // 4
                        dve.wait_ge(attended.sem, attended.at(b, u))
                        then(v.reciprocal(rsums[:, q], sums[:, t % 2, 8 * q:8 * q + 8]))
                        v.tensor_tensor(
                            out=AO[:, :].rearrange("p (h d) -> p h d", d=DQ),
                            in0=bank["OV"][:, :].rearrange("p (h d) -> p h d", d=DQ),
                            in1=rsums[:, q].unsqueeze(2).to_broadcast([P, 8, DQ]),
                            op=ALU.mult).then_inc(free[g]["OV"].sem, 1)
                    elif k == "pp":
                        v.tensor_tensor(out=res_a[:, s[2]], in0=filled_bank("TP")[:, 0:C], in1=res_a[:, s[2]],
                                        op=ALU.add).then_inc(free[g]["TP"].sem, 1)
                    elif k == "sq":
                        dve.wait_ge(normed[g].sem, normed[g].at(b, "x"))
                        for t in range(NT):
                            i = v.tensor_tensor_reduce(out=f_sq[:, t], in0=f_xn[:, t], in1=f_xn[:, t], scale=1.0,
                                                       scalar=0.0, op0=ALU.mult, op1=ALU.add,
                                                       accum_out=ss[:, 0, t:t + 1])
                        i.then_inc(squared[g].sem, 1)
                    elif k == "gl" and part:
                        gate(g, then, part - 1)
                    elif k == "gl":
                        dve.wait_ge(scaled[g].sem, scaled[g].at(b, "x"))
                        v.tensor_tensor(out=lg[:, :, :],
                                        in0=filled_bank("X1")[:, 0:NT * NE].rearrange("p (t e) -> p t e", e=NE),
                                        in1=ss[:, 2].unsqueeze(2).to_broadcast([P, NT, NE]),
                                        op=ALU.mult).then_inc(free[g]["X1"].sem, 1)
                        wait_step(g, b, s)
                    elif k == "ge":
                        weigh(g, b, then, part)
                    elif k == "bc" and part == 0:
                        phase, e = s[2:]
                        if phase == "o" and e == 0:
                            wait_step(g, b, (g, "av"))
                        if e >= 4:
                            low = lo_of(g, phase, e - 4)
                            dve.wait_ge(low.sem, low.at(b, (phase, e - 4)))
                        v.tensor_tensor(out=xs[:, e % 4], in0=filled_bank(bank_of(s))[:, :],
                                        in1=(f_xT if phase == "qkv" else aoT)[:, :],
                                        op=ALU.mult).then_inc(free[g][bank_of(s)].sem, 1)
                    elif k == "bc":
                        phase, e = s[2:]
                        dve.wait_ge(x_hi[g].sem, x_hi[g].at(b, (phase, e)))
                        v.tensor_tensor(out=xparts[:, e % 4, 1], in0=xs[:, e % 4], in1=xparts[:, e % 4, 0],
                                        op=ALU.subtract).then_inc(lo_dve[g].sem, 1)
                    elif k == "sc":
                        t = s[2]
                        n = (t + 1) * P
                        bk = bank_of(s)
                        wait_apart(dve, full[g][bk].sem, full[g][bk].at(b, s))
                        v.tensor_tensor_reduce(out=FP[:, t % 2, 0:n], in0=bank[bk][:, 0:n],
                                               in1=fmask[:, 4 * P - n:4 * P], scale=1.0, scalar=-3.0e38, op0=ALU.add,
                                               op1=ALU.max, accum_out=fm[:, 0, t:t + 1]).then_inc(free[g][bk].sem, 1)
                        wait_step(g, b, s)
                        v.tensor_scalar(fm[:, 1, t:t + 1], fm[:, 0, t:t + 1], -(P ** -0.5), None,
                                        ALU.mult).then_inc(f_maxed[g].sem, 1)
                    elif k == "tp":
                        t = s[2]
                        n = (t + 1) * P
                        dve.wait_ge(f_probs[g].sem, f_probs[g].at(b, t))
                        v.reciprocal(fm[:, 3, t:t + 1], fm[:, 2, t:t + 1]).then_inc(f_inv[g].sem, 1)
                        dve.wait_ge(f_inv[g].sem, f_inv[g].at(b, t))
                        v.tensor_scalar(FP[:, t % 2, 0:n], FP[:, t % 2, 0:n], fm[:, 3, t:t + 1], None,
                                        ALU.mult).then_inc(f_norm[g].sem, 1)
                    elif k in ("ot", "br"):
                        n = bank_of(s)
                        old, new = {"F1": (res_x, res_x), "B": (res_y, res_y), "F2": (res_y, yout)}[g]
                        if g == "F2":
                            dve.wait_ge(y_out.sem, y_out.before(b, "y"))
                        v.tensor_tensor(out=new[:, :, :], in0=filled_bank(n)[:, :].rearrange("p (t c) -> p t c", c=C),
                                        in1=old[:, :, :], op=ALU.add).then_inc(free[g][n].sem, 1)
                    elif k == "bp":
                        n = bank_of(s)
                        v.tensor_tensor(out=qkvb[:, s[2]], in0=filled_bank(n)[:, 0:3 * C], in1=biasb[:, :],
                                        op=ALU.add).then_inc(free[g][n].sem, 1)
                    elif k == "bq":
                        t = s[2]
                        q = qkr[:, t, 0:C].rearrange("p (h d) -> p h d", d=DB)
                        kk = qkr[:, t, C:].rearrange("p (h d) -> p h d", d=DB)
                        full_shape = [P, HB, HB, DB]
                        by_head = att[:, t].rearrange("p (h g) -> p h g", g=HB)
                        if part == 0:
                            dve.wait_ge(roped.sem, roped.at(b, t))
                            then(v.tensor_tensor(out=W.rearrange("p (h g d) -> p h g d", g=HB, d=DB),
                                                 in0=q.unsqueeze(2).to_broadcast(full_shape),
                                                 in1=kk.unsqueeze(1).to_broadcast(full_shape), op=ALU.mult))
                        elif part == 1:
                            then(red(att[:, t], W.rearrange("p (n d) -> p n d", d=DB), ALU.add))
                        elif part == 2:
                            then(red(bm[:, t, 0], by_head, ALU.max))
                        else:
                            tt(by_head, by_head, bm[:, t, 0].unsqueeze(2).to_broadcast([P, HB, HB]),
                               ALU.subtract).then_inc(b_shift.sem, 1)
                    elif k == "bv":
                        t = s[2]
                        o = ato[:, t].rearrange("p (h d) -> p h d", d=DB)
                        if part == 0:
                            dve.wait_ge(b_exp.sem, b_exp.at(b, t))
                            red(bm[:, t, 1], pb[:, t].rearrange("p (h g) -> p h g", g=HB), ALU.add).then_inc(b_sum.sem, 1)
                            dve.wait_ge(b_sum.sem, b_sum.at(b, t))
                            v.reciprocal(bm[:, t, 2], bm[:, t, 1])
                        elif part == 1:
                            dve.wait_ge(b_weighed.sem, b_weighed.at(b, t))
                            then(red(ato[:, t], W2.rearrange("p (n g) -> p n g", g=HB), ALU.add))
                        else:
                            tt(o, o, bm[:, t, 2].unsqueeze(2).to_broadcast([P, HB, DB]), ALU.mult).then_inc(b_att.sem, 1)
                a, r, f, y = batch["A"], batch["R"], batch["F1"], batch["F2"]
                if f is not None:
                    if y is not None:
                        dve.wait_ge(free["F2"]["X2"].sem, free["F2"]["X2"].at(y, ("F2", "ot")))
                    dve.wait_ge(free["F1"]["X2"].sem, free["F1"]["X2"].at(f, ("F1", "ot")))
                    v.tensor_copy(res_y[:, :, :], res_x[:, :, :]).then_inc(handed_y.sem, 1)
                if r is not None:
                    if f is not None:
                        dve.wait_ge(handed_y.sem, handed_y.at(f, "x"))
                    v.tensor_copy(res_x[:, :, :], res_r[:, :, :]).then_inc(handed_x.sem, 1)
                if a is not None:
                    if r is not None:
                        dve.wait_ge(normed["R"].sem, normed["R"].at(r, "x"))
                        dve.wait_ge(handed_x.sem, handed_x.at(r, "x"))
                    dve.wait_ge(free["A"]["TP"].sem, free["A"]["TP"].at(a, ("A", "pp", NT - 1)))
                    v.tensor_copy(res_r[:, :, :], res_a[:, :, :]).then_inc(handed_r.sem, 1)
                for g, c in chain.items():
                    assert c.n == c.sig.per, (g, c.n)

            batches(dve, body)

        @block.tensor
        def _(pe):
            mm, trp = nc.tensor.matmul, nc.tensor.transpose
            starts(pe, [s for g in full for s in full[g].values()] + [attended])
            pe.wait_ge(loaded, LOADED)
            pe.wait_ge(made, MADE)
            pe.wait_ge(set_up, SET_UP - 2)
            mm(bank["X3"][:, 0:NE], ones[:, :], simn[:, :], start=True, stop=True).then_inc(setup_mm, 1)
            pe.wait_ge(set_up, SET_UP)

            def cols(t):
                return slice(t * P, (t + 1) * P)

            def three(to, w, xv, start=True, stop=True):
                for n, (i, j) in enumerate(((0, 0), (0, 1), (1, 0))):
                    last = mm(to, w(i), xv(j), start=start and n == 0, stop=stop and n == 2)
                return last

            def body(batch):
                for s, b, _ in work("pe", batch):
                    g, k = s[:2]

                    def ready(*step, n=None):
                        n = n or bank_of(step)
                        pe.wait_ge(free[g][n].sem, free[g][n].at(b, step))

                    def clear(n, step=None):
                        step = step or s
                        before, ahead = [x for x in STAGE_BEFORE[g] if n in free[x[0]]][0]
                        if free[g][n].turn[step] == 0:
                            if not isinstance(b, int) or b + ahead < NBATCH:
                                pe.wait_ge(free[before][n].sem, free[before][n].at(b + ahead))
                        else:
                            pe.wait_ge(free[g][n].sem, free[g][n].before(b, step))
                        return bank[n]

                    if k == "tr":
                        pe.wait_ge(normed[g].sem, normed[g].at(b, "x"))
                        to = clear(bank_of(s))
                        xn = {"A": a_xn, "B": b_xn}.get(g, f_xn)
                        for t in range(NT):
                            i = trp(to[:, cols(t)], xn[:, t], ident[:, :])
                        i.then_inc(full[g][bank_of(s)].sem, 1)
                    elif k == "r":
                        if s[2] == 0:
                            ready("A", "tr")
                        three(clear(bank_of(s))[:, :], lambda i: wr[:, i, s[2], :],
                              lambda i: a_xT[:, i]).then_inc(full[g][bank_of(s)].sem, 1)
                    elif k == "g":
                        t, q = s[2:]
                        if t == 0:
                            ready("A", "r", q)
                        mm(clear(bank_of(s))[:, :], RT[:, q, cols(t)], bfun[:, :, :].rearrange("p q d -> p (q d)"),
                           start=True, stop=True).then_inc(full[g][bank_of(s)].sem, 1)
                    elif k == "qk":
                        j = s[2]
                        three(clear(bank_of(s))[:, :], lambda i: wqkv[:, j // HP, i, cols(j % HP)],
                              lambda i: a_xT[:, i]).then_inc(full[g][bank_of(s)].sem, 1)
                    elif k == "v":
                        t, h = s[2:]
                        three(clear(bank_of(s))[:, :], lambda i: a_xT[:, i, cols(t)],
                              lambda i: wqkv[:, 2, i, h * TOK:(h + 1) * TOK]).then_inc(full[g][bank_of(s)].sem, 1)
                    elif k == "s":
                        u = s[2]
                        t = u // HP
                        if u == 0:
                            ready("A", "v", NT - 1, 1)
                        n = bank_of(s)
                        to = clear(n)
                        lo = 0 if t else P
                        for h, head in enumerate(heads(u)):
                            part = slice(head % 2 * DQ, head % 2 * DQ + DQ)
                            i = mm(to[:, h * 2 * P + lo:(h + 1) * 2 * P], QT[part, head // 2, cols(t)],
                                   KT[part, head // 2, max(t - 1, 0) * P:(t + 1) * P], start=True, stop=True)
                        i.then_inc(full[g][n].sem, 1)
                    elif k == "t":
                        u = s[2]
                        pe.wait_ge(probs.sem, probs.at(b, u))
                        to = clear("TP")
                        for n, (h, c) in enumerate([(h, c) for h in range(2) for c in ((0, 1) if u >= HP else (1,))]):
                            i = trp(to[:, cols(n)], L[:, u % 2, h, cols(c)], ident[:, :])
                        i.then_inc(full[g]["TP"].sem, 1)
                    elif k == "o":
                        u = s[2]
                        t = u // HP
                        ready("A", "t", u)
                        if u % 4 == 0:
                            clear("OV", ("A", "o", u + 3))
                        keys = [t - 1, t] if t else [0]
                        for h, head in enumerate(heads(u)):
                            for n, kt in enumerate(keys):
                                i = mm(bank["OV"][:, head % 8 * DQ:(head % 8 + 1) * DQ],
                                       PT[:, u % 2, h * len(keys) + n, :], V[:, kt, head * DQ:(head + 1) * DQ],
                                       start=(n == 0), stop=(n == len(keys) - 1))
                        i.then_inc(attended.sem, 1)
                    elif k == "pt":
                        t, q = s[2:]
                        ready("A", "o", t * HP + 4 * q + 3)
                        to = clear("TP")
                        for j in range(4):
                            i = trp(to[:, cols(j)], AO[:, cols(j)], ident[:, :])
                        i.then_inc(full[g]["TP"].sem, 1)
                    elif k == "pp":
                        ready("A", "pt", s[2], 1)
                        to = clear("TP")[:, 0:C]
                        mm(to, ones[0:1, :], rows[0:1, 0, :], start=True, stop=False)
                        for j in range(HP):
                            i = mm(to, AT[:, j, :], wproj[:, j, :], start=False, stop=(j == HP - 1))
                        i.then_inc(full[g]["TP"].sem, 1)
                    elif k == "gl":
                        ready(g, "tr")
                        to = clear("X1")
                        for t in range(NT):
                            i = mm(to[:, t * NE:(t + 1) * NE], f_xT[:, cols(t)], simn[:, :], start=True, stop=True)
                        i.then_inc(full[g]["X1"].sem, 1)
                    elif k == "gt":
                        pe.wait_ge(routed[g].sem, routed[g].at(b, "x"))
                        to = clear("X2")
                        for t in range(NT):
                            i = trp(to[:, cols(t)], rwsp[:, t], ident[:, :])
                        i.then_inc(full[g]["X2"].sem, 1)
                    elif k == "bc":
                        if s[2:] == ("qkv", 0):
                            at = free["R" if g == "F1" else g]["X2"]
                            pe.wait_ge(at.sem, at.at(b, ("R" if g == "F1" else g, "gt")))
                        mm(clear(bank_of(s))[:, :], select[:, s[3], :], rwT[:, :],
                           start=True, stop=True).then_inc(full[g][bank_of(s)].sem, 1)
                    elif k == "mm":
                        phase, e = s[2:]
                        pe.wait_ge(lo_of(g, phase, e).sem, lo_of(g, phase, e).at(b, (phase, e)))
                        for n, j in ((("X0", 0), ("X1", 1), ("X2", 2)) if phase == "qkv" else (("X1", 3),)):
                            if e == 0:
                                clear(n, (g, "qkve" if phase == "qkv" else "oe"))
                            i = three(bank[n][:, :], lambda h: wf[:, j, h, e, :], lambda h: xparts[:, e % 4, h],
                                      start=(e == 0), stop=(e == NE - 1))
                            if e == NE - 1:
                                i.then_inc(full[g][n].sem, 1)
                    elif k == "vt":
                        ready(g, "qkve", n="X2")
                        to = clear("X3")
                        for t in range(NT):
                            i = trp(to[:, cols(t)], qkvT[:, 2, cols(t)], ident[:, :])
                        i.then_inc(full[g]["X3"].sem, 1)
                    elif k == "sc":
                        t = s[2]
                        if t == 0:
                            ready(g, "qkve", n="X0")
                            ready(g, "qkve", n="X1")
                        n = bank_of(s)
                        mm(clear(n)[:, 0:(t + 1) * P], qkvT[:, 0, cols(t)], qkvT[:, 1, 0:(t + 1) * P],
                           start=True, stop=True).then_inc(full[g][n].sem, 1)
                    elif k == "tp":
                        t = s[2]
                        n = bank_of(s)
                        pe.wait_ge(f_norm[g].sem, f_norm[g].at(b, t))
                        to = clear(n)
                        for j in range(t + 1):
                            i = trp(to[:, cols(j)], FP[:, t % 2, cols(j)], ident[:, :])
                        i.then_inc(full[g][n].sem, 1)
                    elif k == "av":
                        ready(g, "tp", NT - 1)
                        to = clear("X0")
                        for j in range(NT):
                            i = mm(to[:, j * P:], vr[:, j, :], FPT[:, j, j * P:], start=(j == 0), stop=(j == NT - 1))
                        i.then_inc(full[g]["X0"].sem, 1)
                    elif k == "ot":
                        ready(g, "oe")
                        to = clear("X2")
                        for t in range(NT):
                            i = trp(to[:, cols(t)], oT[:, cols(t)], ident[:, :])
                        i.then_inc(full[g]["X2"].sem, 1)
                    elif k == "lat":
                        ready("B", "tr")
                        mm(clear("OV")[0:LAT, :], wdown[:, :], b_xT, start=True, stop=True).then_inc(full[g]["OV"].sem, 1)
                    elif k == "bp":
                        n = bank_of(s)
                        if s[2] == 0:
                            ready("B", "lat")
                        to = clear(n)
                        mm(to[:, 0:C], b_xT[:, cols(s[2])], wqb[:, :], start=True, stop=True)
                        mm(to[:, C:3 * C], latT[:, cols(s[2])], wup[:, :], start=True, stop=True
                           ).then_inc(full[g][n].sem, 1)
                    elif k == "bo":
                        pe.wait_ge(b_att.sem, b_att.at(b, NT - 1))
                        to = clear("TP")
                        for t in range(NT):
                            i = trp(to[:, cols(t)], ato[:, t], ident[:, :])
                        i.then_inc(full[g]["TP"].sem, 1)
                    elif k == "br":
                        ready("B", "bo")
                        to = clear("OV")
                        for t in range(NT):
                            mm(to[:, cols(t)], ones[0:1, :], rows[0:1, 1, :], start=True, stop=False)
                            i = mm(to[:, cols(t)], b_oT[:, cols(t)], wout[:, :], start=False, stop=True)
                        i.then_inc(full[g]["OV"].sem, 1)

            batches(pe, body)


_ARGS = ["L0_attn_a_X", "L0_attn_a_Wq", "L0_attn_a_bq", "L0_attn_a_Wk", "L0_attn_a_Wv", "L0_attn_a_Wproj",
         "L0_attn_a_bproj", "L0_attn_a_Wr", "L0_attn_a_br", "L0_attn_a_b_nd", "L0_attn_b_Wq", "L0_attn_b_bq",
         "L0_attn_b_Wdown", "L0_attn_b_bdown", "L0_attn_b_Wup", "L0_attn_b_bup", "L0_attn_b_Wout", "L0_attn_b_bout",
         "L0_ffn_sim_matrix", "L0_ffn_gates", "L0_ffn_q_proj", "L0_ffn_k_proj", "L0_ffn_v_proj", "L0_ffn_o_proj"]


def rope_table():
    inv = 1.0 / 10000.0 ** (np.arange(0, DB, 2, dtype=np.float32) / np.float32(DB))
    angle = np.arange(TOK, dtype=np.float32)[:, None] * inv[None, :].astype(np.float32)
    cos, sin = np.cos(angle).astype(np.float32), np.sin(angle).astype(np.float32)
    table = np.stack([np.concatenate([cos, cos], 1), np.concatenate([-sin, sin], 1)], 1)
    return np.ascontiguousarray(table.reshape(NT, P, 2, DB).transpose(1, 0, 2, 3))


def part_rows():
    k = np.arange(P) % 32 // NB
    return np.ascontiguousarray(-np.stack([k == 1, k == 2], 1).astype(np.float32))


def kernel(**inputs):
    import concourse.bacc as _bacc
    from concourse import mybir as _mybir
    from concourse.bass_utils import run_bass_kernel_spmd as _run

    nc = _bacc.Bacc("TRN2", target_bir_lowering=False, num_devices=1)
    arrays, args = {}, []
    constants = {"rope": rope_table(), "part_rows": part_rows()}
    for name in _ARGS + list(constants):
        a = constants[name] if name in constants else np.asarray(inputs[name])
        if name == "L0_attn_a_b_nd":
            a = a[:, ::-1]
        a = np.ascontiguousarray(a)
        arrays[f"in_{name}"] = a
        args.append(nc.dram_tensor(f"in_{name}", a.shape, _mybir.dt.from_np(a.dtype), kind="ExternalInput").ap())
    args.append(nc.dram_tensor("out_0", (NBATCH, TOK, C), _mybir.dt.float32, kind="ExternalOutput").ap())
    stack_kernel(nc, *args)
    r = _run(nc, [arrays], core_ids=[0])
    return r.results[0]["out_0"]
```

```python
from contextlib import ExitStack

import numpy as np
import concourse.bass as bass
from concourse import mybir

NBATCH, TOK, C = 16, 512, 128
P = 128
NT = TOK // P
H, DQ, NB, WIN = 16, 64, 10, 128
HP = H // 2
NE = 16
HB, DB, LAT = 16, 8, 32
NEG = -1.0e9
FMASK = -1.0e30
BIG = 1.0e30
LN_EPS = 1e-5
U = NT * HP
SPLIT = 16.0
UNSPLIT = 1.0 / SPLIT ** 2


def heads(u):
    p = u % HP
    return [p // 2 * 4 + p % 2 + 2 * h for h in range(2)]


LOGITS = 3


Q_STEPS = [("Q", "ln"), ("Q", "tr")] + [("Q", "r", g) for g in range(4)] + [("Q", "g", 0, q) for q in range(4)]
PROLOGUE = [("A", "qk", j) for j in range(2 * HP)] + [("A", "v", t, h) for t in range(NT) for h in range(2)]


def a_steps():
    s = list(PROLOGUE)
    for u in range(U + 2):
        t, p = divmod(u, HP)
        if u < U:
            s.append(("A", "s", u))
        if 1 <= u <= U:
            s.append(("A", "t", u - 1))
        if u >= 2:
            s.append(("A", "o", u - 2))
        if p == 6:
            s.append(("A", "pt", t, 0))
        if t and p == 2:
            s.append(("A", "pt", t - 1, 1))
        if t and p == 3 and u < U:
            s.append(("A", "pp", t - 1))
        if t + 1 < NT and p % 2 == 1:
            s.append(("A", "g", t + 1, p // 2))
    return s + [("A", "pt", NT - 1, 1), ("A", "pp", NT - 1)]


def maker(f, phase, e):
    return "R" if f == "F1" and phase == "qkv" and e < AHEAD else f


def experts(f, phase):
    s = [(f, "bc", phase, e) for e in range(AHEAD) if maker(f, phase, e) == f]
    for e in range(NE):
        s.append((f, "mm", phase, e))
        if e + AHEAD < NE:
            s.append((f, "bc", phase, e + AHEAD))
    return s


AHEAD = 4


def routing_steps(f):
    return [(f, "ln"), (f, "sq"), (f, "tr"), (f, "gl"), (f, "ge"), (f, "gt")]


def f_steps(f):
    s = experts(f, "qkv") + [(f, "qkve"), (f, "vt")]
    for t in range(NT):
        s.append((f, "sc", t))
        if t:
            s.append((f, "tp", t - 1))
    return s + [(f, "tp", NT - 1), (f, "av")] + experts(f, "o") + [(f, "oe"), (f, "ot")]


def b_steps():
    s = [("B", "ln"), ("B", "tr"), ("B", "lat"), ("B", "bp", 0)]
    for t in range(NT):
        if t + 1 < NT:
            s.append(("B", "bp", t + 1))
        s += [("B", "bq", t, 0), ("B", "bq", t, 1), ("B", "bx", t), ("B", "bv", t, 0), ("B", "bv", t, 1)]
    return s + [("B", "bo"), ("B", "br")]


STEPS = {"Q": Q_STEPS, "A": a_steps(), "B": b_steps(),
         "R": routing_steps("R") + [("R", "bc", "qkv", e) for e in range(AHEAD)],
         "F1": f_steps("F1"), "F2": routing_steps("F2") + f_steps("F2")}


A_BANKS, F_BANKS = ["S0", "S1", "TP", "OV"], ["X0", "X1", "X2", "X3"]


def banks_of(s):
    stage, k = s[:2]
    if s in PROLOGUE:
        return [A_BANKS[PROLOGUE.index(s) % 4]]
    if stage == "Q":
        return [A_BANKS[Q_STEPS.index(s) % 2]] if k != "ln" else []
    if stage == "A":
        if k == "s":
            return [A_BANKS[s[2] % 2]]
        if k == "o":
            return ["OV"] if s[2] % 4 == 3 else []
        return ["TP"] if k in ("t", "pp") else [A_BANKS[1 - s[3] % 2]] if k in ("g", "pt") else []
    if stage == "B":
        if k == "bp":
            return [A_BANKS[s[2] % 2]]
        return {"tr": ["TP"], "lat": ["OV"], "bo": ["TP"], "br": ["OV"]}.get(k, [])
    if k == "sc":
        return [F_BANKS[s[2] % 2]]
    if k == "tp":
        return [F_BANKS[2 + s[2] % 2]]
    if k == "bc":
        return ["X0" if s[2] == "o" and s[3] % 2 else "X3"]
    return {"tr": ["X2"], "gl": ["X1"], "gt": ["X2"], "qkve": ["X0", "X1", "X2"], "vt": ["X3"],
            "av": ["X0"], "oe": ["X1"], "ot": ["X2"]}.get(k, [])


def bank_of(s):
    (one,) = banks_of(s)
    return one


USES = {g: {b: [s for s in STEPS[g] if b in banks_of(s)] for b in (A_BANKS if g in "QAB" else F_BANKS)} for g in STEPS}


def lo_on_dve(phase, e):
    return phase == "o" and e % 2 == 1


def parts(s):
    stage, k = s[:2]
    if k == "ln":
        return [("dve", 1.3), ("pool", 1.3), ("dve", .8)]
    if k == "sq":
        return [("dve", .9), ("pool", 1.3)]
    if k == "tr":
        return [("pe", .43), ("act", .5)] + [("dve", .65)] * (stage == "Q")
    if k in ("gt", "bo", "vt", "t", "pt"):
        return [("pe", .43), ("act", .5)]
    if k == "ot":
        return [("pe", .43), ("dve", .65)] + [("act", .1)] * (stage == "F2")
    if k == "r":
        return [("pe", .64), ("act", 1.2), ("dve", .7)]
    if k in ("qk", "v"):
        return [("pe", .64), ("act", .55)]
    if k == "g":
        return [("pe", .22), ("act", .5)]
    if k == "s":
        return [("pe", .85), ("dve", .95), ("act", .65)]
    if k == "o":
        return [("pe", .43)] + [("dve", .8)] * (s[2] % 4 == 3)
    if k == "pp":
        return [("pe", 1.9), ("dve", .25)]
    if k == "gl":
        return [("pe", .25), ("dve", .35)] + [("dve", 1.4)] * 4
    if k == "ge":
        return [("act", .2), ("dve", 1.1), ("dve", 1.0)]
    if k == "bc":
        return [("pe", .22), ("dve", .62), ("act", .54), ("dve", .62) if lo_on_dve(*s[2:]) else ("pool", 1.13)]
    if k == "mm":
        return [("pe", .64)] * (3 if s[2] == "qkv" else 1)
    if k == "qkve":
        return [("act", 1.5)]
    if k == "sc":
        return [("pe", .22 * (s[2] + 1)), ("dve", .3 + .13 * s[2]), ("act", .2 + .11 * s[2])]
    if k == "tp":
        return [("dve", .1), ("act", .3 + .11 * s[2]), ("pe", .11 * (s[2] + 1)), ("act", .2 + .11 * s[2])]
    if k == "av":
        return [("pe", 2.1), ("act", .5)]
    if k == "oe":
        return [("act", .5)]
    if k == "lat":
        return [("pe", .85), ("act", .6)]
    if k == "bp":
        return [("pe", 1.3), ("act", .4), ("pool", 2.2)]
    if k == "bq":
        return [("pool", 2.0) if s[3] else ("dve", 1.2), ("dve", 1.2)]
    if k == "bx":
        return [("dve", .4), ("dve", .35), ("act", .35), ("dve", .6)]
    if k == "bv":
        return [("pool", 2.0), ("dve", 1.2)] + [("dve", .25)] * s[3]
    assert k == "br"
    return [("pe", 1.3), ("dve", .65)]


def g_step(t, q):
    return "A" if t else "Q", "g", t, q


def needs(s):
    stage, k = s[:2]
    n = []
    if k in ("qk", "v"):
        n = [("Q", "tr"), ("B", "br")]
    elif k in ("r", "gl"):
        n = [(stage, "tr")] + ([(stage, "sq")] if k == "gl" else [(stage, "r", s[2] - 2)] if s[2] > 1 else [])
    elif k == "g":
        half = s[2] * 4 + s[3]
        return [(("Q", "r", s[3]), 0)] + [(g_step(*divmod(half - 1, 4)), 4.5)] * (s[3] % 2 == 0 and half > 0)
    elif k == "s":
        t, p = divmod(s[2], HP)
        n = [(("A", "v", 3, 1), 0), (g_step(t, p // 4 * 2 + 1), 10)]
        n += [(("A", "t", s[2] - LOGITS), 0)] * (s[2] >= LOGITS)
        return n + ([(("A", "s", (t - 1) * HP + p // 4 * 4 + 3), 4.5)] if t else [])
    elif k == "t":
        n = [("A", "s", s[2])] + [("A", "o", s[2] - 2)] * (s[2] >= 2)
    elif k == "o":
        before = s[2] - 4
        n = [("A", "t", s[2])] + [("A", "pt", before // HP, before % HP // 4)] * (s[2] % 4 == 3 and before > 0)
    elif k == "pt":
        n = [("A", "o", s[2] * HP + 4 * s[3] + 3)]
    elif k == "pp":
        n = [("A", "pt", s[2], h) for h in (0, 1)]
    elif k == "mm":
        n = [(maker(stage, *s[2:]), "bc") + s[2:]]
    elif k == "bc":
        n = [(stage, "gt") if s[2] == "qkv" else (stage, "av")] if maker(stage, s[2], 0) == stage or s[2] == "o" else []
        if s[3] >= 4:
            n += [(maker(stage, s[2], s[3] - 4), "bc", s[2], s[3] - 4), (stage, "mm", s[2], s[3] - 4)]
    elif k == "qkve":
        n = [(stage, "mm", "qkv", NE - 1)]
    elif k == "oe":
        n = [(stage, "mm", "o", NE - 1)]
    elif k == "sc":
        n = [(stage, "qkve")]
    elif k == "tp":
        n = [(stage, "sc", s[2])]
    elif k == "av":
        n = [(stage, "vt")] + [(stage, "tp", t) for t in range(NT)]
    elif k == "tr":
        n = [(stage, "ln")]
    elif k == "bp":
        n = [(stage, "lat")]
    elif k == "bq":
        n = [(stage, "bp", s[2])] + [(stage, "bq", s[2] - 1, s[3])] * (s[2] > 0)
    elif k == "bx":
        n = [(stage, "bq", s[2], h) for h in (0, 1)]
    elif k == "bv":
        n = [(stage, "bx", s[2])] + [(stage, "bv", s[2] - 1, s[3])] * (s[2] > 0)
    elif s == ("F2", "ln"):
        n = [("F1", "ot"), ("B", "br")]
    elif k != "ln":
        n = [STEPS[stage][STEPS[stage].index(s) - 1]]
    return [(x, 0) for x in n]


def frees(s):
    return 1 if s[1] in ("s", "bc", "sc", "gl", "bp") else len(parts(s)) - 1


def takes(s):
    if s[1] == "mm" and s[3] == 0:
        return ["X0", "X1", "X2"] if s[2] == "qkv" else ["X1"]
    if s[1] == "o" and s[2] % 4 == 0:
        return ["OV"]
    return [] if s[1] in ("o", "qkve", "oe") else banks_of(s)


def lane(s, n):
    stage, k = s[:2]
    engine = parts(s)[n][0]
    if engine == "pe":
        apart = ("s", "o", "t", "pp", "pt", "bc", "mm", "sc", "tp")
        return engine, stage in "QAB", "b" if k in ("bo", "br") else k if k in apart else ""
    if engine == "dve" and stage not in "AB":
        return engine, stage in "QAB", "lo" if k == "bc" and n == 3 else ""
    return engine, stage in "QAB", "" if engine == "pool" and k not in ("bv", "bq") else k


PREFER = {("pe", "g"): 15, ("act", "F2"): 10, ("pe", "B"): 30, ("dve", "tp"): 10, ("act", "Q"): 33, ("pe",
          "bc"): 40, ("pe", "Q"): 54, ("pe", "pt"): 50, ("act", "tp"): 50, ("dve", "F1"): 63, ("act", "B"): -66,
          ("act", "r"): -40, ("dve", "sc"): -30, ("act", "g"): 50, ("pe", "tp"): 60, ("pool", "ln"): -20,
          ("dve", "R"): 40, ("pe", "sc"): 90, ("dve", "Q"): -30, "F1": 9, "A": 9, "bv": -12, "F2": 15, "sc":
          -24, "g": 30, "bc": 30, "Q": 33, "v": -30, "t": 39, "tr": -42, "B": 48, "gl": -30, "ge": -30, "ln":
          57, "pp": 10, "tp": -60}
PREFER_LATER = {"bc": 40, "ln": 70, "B": 40, "F2": 70}
PATIENCE = {"pe": 0, "dve": 0, "act": 0, "pool": 1}


def in_order(stages):
    prefer = PREFER if "A" in stages else PREFER_LATER
    streams = [[s for g in gs if g in stages for s in STEPS[g]] for gs in (("B", "Q", "A"), ("F1", "F2", "R"))]
    before, last_of, last_use = {}, {}, {}

    def later(p, q):
        engines = {parts(s)[n][0] for s, n in (p, q)}
        return 0 if engines == {"pe"} else .07 if len(engines) == 1 else .14 if engines == {"dve", "act"} else .2

    for stream in streams:
        for s in stream:
            for n in range(len(parts(s))):
                b = [((s, n - 1), 0)] if n else [
                      ((x, len(parts(x)) - 1), d) for x, d in needs(s)
                      if x[0] in stages and (s[0] == "R" or x[0] != "R")
                      and (x[0] != "B" or "F1" in stages or s[0] != "F2")]
                if parts(s)[n][0] == "pe":
                    b += [(last_use[x], 0) for x in takes(s) if x in last_use]
                b = [(p, d + later(p, (s, n))) for p, d in b]
                if lane(s, n) in last_of:
                    b.append((last_of[lane(s, n)], 0))
                last_of[lane(s, n)] = (s, n)
                before[s, n] = b
            for x in banks_of(s):
                last_use[x] = (s, frees(s))
    after = {p: [] for p in before}
    for p, b in before.items():
        for q, d in b:
            after[q].append((p, d))
    way, waiting = {}, {p: len(b) for p, b in before.items()}

    def length(p):
        if p not in way:
            way[p] = parts(p[0])[p[1]][1] + max([d + length(q) for q, d in after[p]] + [0.0])
        return way[p]

    for p in reversed(list(before)):
        length(p)
    ends, free, out = {}, dict(pe=0.0, dve=1.0, act=0.0, pool=0.0), {e: [] for e in ("pe", "dve", "act", "pool")}
    ready = {p: 0.0 for p, b in before.items() if not b}
    while ready:
        start = {p: max(ready[p], free[parts(p[0])[p[1]][0]]) for p in ready}
        first = min(start, key=start.get)
        engine = parts(first[0])[first[1]][0]
        p = max([p for p in ready if parts(p[0])[p[1]][0] == engine and start[p] <= start[first] + PATIENCE[engine]],
                key=lambda p: (way[p] + sum(prefer.get(x, 0) + prefer.get((engine, x), 0) for x in p[0][:2]),
                               -start[p]))
        d = parts(p[0])[p[1]][1] + (.04 if engine != "pe" else .06 if p[0][1] != "mm" or p[1] == 0 else 0)
        ends[p] = free[engine] = max(ready.pop(p), free[engine]) + d
        s, n = p
        out[engine].append((s, sum(e == engine for e, _ in parts(s)[:n])))
        for q, _ in after[p]:
            waiting[q] -= 1
            if not waiting[q]:
                ready[q] = max(ends[b] + d for b, d in before[q])
    assert len(ends) == len(before)
    return out


LAG = {"Q": 0, "A": 0, "R": 1, "F1": 2, "B": 3, "F2": 3}
STAGE_BEFORE = {"Q": [("B", -3)], "A": [("Q", 0), ("B", -3)], "B": [("A", 2)], "F1": [("R", 0), ("F2", -2)], "F2": [("F1", 1)], "R": [("F2", -2)]}


class Signal:

    AHEAD = 3

    def __init__(self, ctx, nc, name, keys, unit=1):
        self.sem = ctx.enter_context(nc.semaphore(name))
        self.turn = {k: n for n, k in enumerate(keys)}
        self.per, self.unit = len(keys), unit
        assert len(self.turn) == self.per

    def start(self):
        return self.AHEAD * self.per * self.unit

    def at(self, b, key=None):
        n = self.turn[key] + 1 if key is not None else self.per
        return (b + self.AHEAD) * (self.per * self.unit) + n * self.unit

    def before(self, b, key):
        return (b + self.AHEAD) * (self.per * self.unit) + self.turn[key] * self.unit


def stack_kernel(nc, x, a_wq, a_bq, a_wk, a_wv, a_wproj, a_bproj, a_wr, a_br, a_bfun, b_wq, b_bq, b_wdown, b_bdown,
                 b_wup, b_bup, b_wout, b_bout, f_sim, f_gates, f_q, f_k, f_v, f_o, rope, part_rows, out):
    f32, bf16, f16 = mybir.dt.float32, mybir.dt.bfloat16, mybir.dt.float16
    ALU, ACT, AX = mybir.AluOpType, mybir.ActivationFunctionType, mybir.AxisListType
    ctx = ExitStack()
    with ctx:
        def sb(name, shape, dt=f32):
            return ctx.enter_context(nc.sbuf_tensor(name, shape, dt))

        wqkv = sb("wqkv", [P, 3, 2, H * DQ], f16)
        wproj = sb("wproj", [P, HP, C])
        wr = sb("wr", [P, 2, 4, P], f16)
        bq = sb("bq", [P, HP])
        br = sb("br", [P, 4])
        bfun = sb("bfun", [P, 4, WIN], f16)
        neg_parts = sb("neg_parts", [P, 2])
        rows = sb("rows", [1, 2, C])
        ones = sb("ones", [P, P])
        ident = sb("ident", [P, P])
        wf = sb("wf", [P, 4, 2, NE, P], f16)
        sim = sb("sim", [P, NE])
        simn = sb("simn", [P, NE])
        sig = sb("sig", [P, NE])
        rank = sb("rank", [P, NE])
        select = sb("select", [P, NE, P], bf16)
        fmask = sb("fmask", [P, 3 * P + P])
        wqb = sb("wqb", [P, C])
        wdown = sb("wdown", [P, LAT])
        bdown = sb("bdown", [LAT, 1])
        wup = sb("wup", [LAT, 2 * C])
        biasb = sb("biasb", [1, 3 * C])
        wout = sb("wout", [P, C])
        ropet = sb("ropet", [P, NT, 2, DB])
        mhalf = sb("mhalf", [P, NE])
        res_a = sb("res_a", [P, NT, C])
        res_r = sb("res_r", [P, NT, C])
        res_x = sb("res_x", [P, NT, C])
        res_y = sb("res_y", [P, NT, C])
        ln_a = sb("ln_a", [P, 10 * NT])
        a_xn = sb("a_xn", [P, NT, C])
        a_xT = sb("a_xT", [P, 2, TOK], f16)
        QT = sb("QT", [P, HP, TOK])
        KT = sb("KT", [P, HP, TOK])
        V = sb("V", [P, NT, H * DQ])
        RT = sb("RT", [P, 4, TOK], f16)
        G = sb("G", [P, HP, WIN])
        E = sb("E", [P, 2, HP, 2 * P])
        L = sb("L", [P, LOGITS, 2, 2 * P])
        mx = sb("mx", [P, LOGITS, 2])
        nmx = sb("nmx", [P, LOGITS, 2])
        sums = sb("sums", [P, 2, H])
        rsums = sb("rsums", [P, 2, HP])
        PT = sb("PT", [P, 2, 4, P])
        AO = sb("AO", [P, TOK])
        AT = sb("AT", [P, HP, P])
        ln_f = sb("ln_f", [P, 10 * NT])
        f_xn = sb("f_xn", [P, NT, C])
        f_xT = sb("f_xT", [P, TOK])
        ss = sb("ss", [P, 3, NT])
        lg = sb("lg", [P, NT, NE])
        gt = sb("gt", [P, 12, NT, NE])
        g1 = sb("g1", [P, 10, NT])
        gb = sb("gb", [P, 2, NT, NE], bf16)
        rwsp = sb("rwsp", [P, NT, P])
        rwT = sb("rwT", [P, TOK], bf16)
        xs = sb("xs", [P, 4, TOK])
        qkvT = sb("qkvT", [P, 3, TOK])
        vr = sb("vr", [P, NT, P])
        fm = sb("fm", [P, 4, NT])
        FPT = sb("FPT", [P, NT, TOK])
        aoT = sb("aoT", [P, TOK])
        oT = sb("oT", [P, TOK])

        def flat(t):
            return t[:, :, :].rearrange("p a n -> p (a n)")

        xparts = flat(FPT).bitcast(f16).rearrange("p (s k n) -> p s k n", s=4, k=2)
        f_sq = xs[:, 0].rearrange("p (t c) -> p t c", t=NT)
        in_v, in_k, in_q = flat(V), flat(KT), flat(QT)
        W = in_v[:, 0:2048]
        qkvb = in_v[:, 2048:2048 + NT * 3 * C].rearrange("p (t n) -> p t n", t=NT)
        latT = V[0:LAT, NT - 1, H * DQ - TOK:]
        W2 = in_q[:, 2048:4096]
        rp = in_k[:, 0:512].rearrange("p (b n) -> p b n", b=2)
        att = in_k[:, 512:1536].rearrange("p (a n) -> p a n", a=NT)
        pb = in_k[:, 1536:2560].rearrange("p (a n) -> p a n", a=NT)
        ato = in_k[:, 2560:3072].rearrange("p (t c) -> p t c", t=NT)
        b_xT = in_k[:, 3072:3584]
        b_oT = in_k[:, 3584:4096]
        b_xn = in_q[:, 0:512].rearrange("p (t c) -> p t c", t=NT)
        ln_b = in_q[:, 512:512 + 10 * NT]
        bm = in_q[:, 600:600 + 3 * NT * HB].rearrange("p (a k h) -> p a k h", a=NT, k=3)
        qkr = in_q[:, 1024:2048].rearrange("p (a n) -> p a n", a=NT)
        stage_f = [in_q[:, 0:2048], in_q[:, 2048:4096], in_k[:, 0:2048], in_k[:, 2048:4096]]
        stage_qkv = [in_v[:, j * 1024:(j + 1) * 1024] for j in range(3)]
        stage_wr = flat(G)[:, 0:512]
        stage_bfun = flat(G)[:, 512:1024]

        names = A_BANKS + F_BANKS
        bank = {n: ctx.enter_context(nc.psum_tensor(f"bank_{n}", [P, TOK], f32)) for n in names}
        scratch = nc.dram_tensor("bias_scratch", (2 * NT, P, HP, 2 * P), f32, kind="Internal")
        row = HP * 2 * P

        def signal(name, keys, unit=1):
            return Signal(ctx, nc, name, keys, unit)

        full = {g: {n: signal(f"full_{g}_{n}", [s for s in u if s[1] != "o"]) for n, u in USES[g].items() if u}
                for g in USES}
        free = {g: {n: signal(f"free_{g}_{n}", u) for n, u in USES[g].items() if u} for g in USES}
        loaded = ctx.enter_context(nc.semaphore("loaded"))
        made = ctx.enter_context(nc.semaphore("made"))
        filled = ctx.enter_context(nc.semaphore("filled"))
        set_up = ctx.enter_context(nc.semaphore("set_up"))
        setup_mm = ctx.enter_context(nc.semaphore("setup_mm"))
        setup_act = ctx.enter_context(nc.semaphore("setup_act"))
        passed = ctx.enter_context(nc.semaphore("passed"))
        halves = [(t, g) for t in range(NT) for g in range(2)]
        x_in = signal("x_in", ["x"], 16)
        a_hi = signal("a_hi", ["x"])
        r_act = signal("r_act", [(g, k) for g in range(4) for k in (0, 1)])
        bias_out = signal("bias_out", halves, 16)
        bias_in = signal("bias_in", halves, 16)
        maxed = signal("maxed", list(range(U)))
        probs = signal("probs", list(range(U)))
        attended = signal("attended", list(range(U)))
        handed_r = signal("handed_r", ["x"])
        handed_x = signal("handed_x", ["x"])
        handed_y = signal("handed_y", ["x"])
        stats_of = ["Q", "B", "R", "F2"]
        stats = {g: signal(f"stats_{g}", ["x"]) for g in stats_of}
        spread = {g: signal(f"spread_{g}", ["x"]) for g in stats_of}
        normed = {g: signal(f"normed_{g}", ["x"]) for g in stats_of}
        F, ROUTERS = ["F1", "F2"], ["R", "F2"]
        squared = {f: signal(f"squared_{f}", ["x"]) for f in ROUTERS}
        scaled = {f: signal(f"scaled_{f}", ["x"]) for f in ROUTERS}
        gated = {f: signal(f"gated_{f}", ["x"]) for f in ROUTERS}
        gate_exp = {f: signal(f"gate_exp_{f}", ["x"]) for f in ROUTERS}
        routed = {f: signal(f"routed_{f}", ["x"]) for f in ROUTERS}
        each = [(ph, e) for ph in ("qkv", "o") for e in range(NE)]
        made_in = {g: [k for k in each if maker(f, *k) == g] for g, f in (("R", "F1"), ("F1", "F1"), ("F2", "F2"))}
        x_hi = {g: signal(f"x_hi_{g}", keys) for g, keys in made_in.items()}
        lo_pool = {g: signal(f"lo_pool_{g}", [k for k in keys if not lo_on_dve(*k)]) for g, keys in made_in.items()}
        lo_dve = {g: signal(f"lo_dve_{g}", [k for k in keys if lo_on_dve(*k)]) for g, keys in made_in.items() if g != "R"}
        tiles = list(range(NT))
        f_maxed = {f: signal(f"f_maxed_{f}", tiles) for f in F}
        f_probs = {f: signal(f"f_probs_{f}", tiles) for f in F}
        f_inv = {f: signal(f"f_inv_{f}", tiles) for f in F}
        f_norm = {f: signal(f"f_norm_{f}", tiles) for f in F}
        roped = signal("roped", tiles)
        b_shift = signal("b_shift", tiles)
        b_exp = signal("b_exp", tiles)
        b_sum = signal("b_sum", tiles)
        tile_halves = [(t, h) for t in range(NT) for h in range(2)]
        b_weighed = signal("b_weighed", tile_halves)
        b_summed = signal("b_summed", tile_halves)
        b_multiplied = signal("b_multiplied", tiles)
        b_scored = signal("b_scored", tiles)
        b_att = signal("b_att", tiles)
        y_out = signal("y_out", ["y"], 16)
        dve_chain = {"Q": signal("dve_Q", list(range(1))), "A": signal("dve_A", list(range(2 * NT))),
                     "B": signal("dve_B", list(range(1 + 3 * NT)))}
        dve_chain |= {f: signal(f"dve_{f}", list(range(1 + 27))) for f in ROUTERS}
        pool_chain = {"Q": signal("pool_Q", list(range(1))), "B": signal("pool_B", list(range(1 + 3 * NT)))}
        pool_chain |= {f: signal(f"pool_{f}", list(range(2))) for f in ROUTERS}

        def lo_of(f, phase, e):
            return (lo_dve if lo_on_dve(phase, e) else lo_pool)[maker(f, phase, e)]

        def wait_apart(eng, sem, value):
            eng.wait_ge(sem, value)
            eng.sem_inc(passed, 1)

        class Chain:

            def __init__(self, eng, sig, b, apart=False):
                self.eng, self.sig, self.b, self.apart, self.n = eng, sig, b, apart, 0

            def __call__(self, ins):
                self.n += 1
                ins.then_inc(self.sig.sem, 1)
                self.eng.wait_ge(self.sig.sem, (self.b + Signal.AHEAD) * self.sig.per + self.n)
                if self.apart:
                    self.eng.sem_inc(passed, 1)

        def chains(eng, sigs, batch, apart=False):
            return {g: Chain(eng, sigs[g], batch[g], apart) for g in sigs if batch[g] is not None}

        def batches(eng, body):
            def of(i):
                return {g: i - lag if 0 <= i - lag < NBATCH else None for g, lag in LAG.items()}

            full_from = max(LAG.values())
            for i in range(full_from):
                body(of(i))
            with eng.Fori(full_from, NBATCH) as i:
                body({g: i - lag if lag else i for g, lag in LAG.items()})
            end = NBATCH - 1
            body(of(NBATCH))
            for some in ({"F1": end, "B": end - 1}, {"B": end, "F2": end - 1}, {"F2": end}):
                body({g: some.get(g) for g in LAG})

        def work(engine, batch):
            return [(s, batch[s[0]], n) for s, n in in_order([g for g in STEPS if batch[g] is not None])[engine]]

        def starts(eng, mine):
            for s in mine:
                eng.sem_inc(s.sem, s.start())

        up = b_wup.rearrange("l (h s d) -> l s h d", s=2, d=DB)
        bup = b_bup.rearrange("(a h s d) -> a s h d", a=1, s=2, d=DB)
        brv = a_br.rearrange("(g q n) -> q n g", g=4, n=NB)
        loads = list(zip(stage_qkv, (a_wq, a_wk, a_wv)))
        loads += [(bq[:, :], a_bq.rearrange("(j p) -> p j", p=P)), (neg_parts[:, :], part_rows),
                  (sim[:, :], f_sim), (sig[:, :], f_gates.rearrange("(a c) -> a c", a=1).to_broadcast([P, NE]))]
        loads += [(stage_f[j].rearrange("p (e h) -> p e h", e=NE), w.rearrange("e c h -> c e h"))
                  for j, w in enumerate((f_q, f_k, f_v, f_o))]
        loads += [(wproj[:, :, :], a_wproj.rearrange("(j p) c -> p j c", p=P)),
                  (rows[:, 0, :], a_bproj.rearrange("(a c) -> a c", a=1)),
                  (rows[:, 1, :], b_bout.rearrange("(a c) -> a c", a=1)),
                  (wqb[:, :], b_wq), (wdown[:, :], b_wdown), (bdown[:, :], b_bdown.rearrange("(p a) -> p a", a=1)),
                  (biasb[:, 0:C], b_bq.rearrange("(a c) -> a c", a=1)),
                  (wout[:, :], b_wout), (ropet[:, :, :, :], rope)]
        for j in range(2):
            loads += [(wup[:, j * C:(j + 1) * C].rearrange("l (h d) -> l h d", d=DB), up[:, j]),
                      (biasb[:, (j + 1) * C:(j + 2) * C].rearrange("p (h d) -> p h d", d=DB),
                       bup[:, j])]
        LOADED = 16 * (len(loads) + 3 + 4 * 3 * 2)
        CLEARED, MADE = 4, 9 + NE + 5
        SPLITS = 3 + 4 + 2
        SET_UP = 5 + SPLITS

        xv = x.rearrange("b (t p) c -> b p t c", p=P)
        outv = out.rearrange("b (t p) c -> b p t c", p=P)

        def multiply_qk(engine, t, half):
            shape = [P, HB // 2, HB, DB]
            q = qkr[:, t, half * 64:half * 64 + 64].rearrange("p (h d) -> p h d", d=DB)
            return engine.tensor_tensor(
                out=W[:, half * 1024:half * 1024 + 1024].rearrange("p (h g d) -> p h g d", g=HB, d=DB),
                in0=q.unsqueeze(2).to_broadcast(shape),
                in1=qkr[:, t, C:].rearrange("p (h d) -> p h d", d=DB).unsqueeze(1).to_broadcast(shape), op=ALU.mult)

        block = ctx.enter_context(nc.Block())

        @block.sync
        def _(sp):
            starts(sp, [x_in, bias_out, bias_in])
            for dst, src in loads:
                sp.dma_start(dst, src, allow_slow_non_contiguous=True).then_inc(loaded, 16)
            wait_apart(sp, made, CLEARED)
            wr_heads = stage_wr.rearrange("c (h r) -> c h r", r=32)
            for k in range(3):
                sp.dma_start(wr_heads[:, :, k * NB:(k + 1) * NB],
                             a_wr.rearrange("c (h n) -> c h n", n=NB)).then_inc(loaded, 16)
                for q in range(4):
                    at = slice(32 * q + k * NB, 32 * q + (k + 1) * NB)
                    sp.dma_start(stage_bfun[at, q * WIN:(q + 1) * WIN], a_bfun).then_inc(loaded, 16)
                    sp.dma_start(br[at, :], brv[q], allow_slow_non_contiguous=True).then_inc(loaded, 16)
            for n in range(2 * NT):
                sp.dma_start(scratch.ap()[n].rearrange("p h k -> p (h k)"),
                             E[:, 0].rearrange("p h k -> p (h k)")).then_inc(filled, 16)
            wait_apart(sp, filled, 16 * 2 * NT)
            wait_apart(sp, set_up, SET_UP)

            def body(batch):
                a = batch["A"]
                if a is None:
                    return
                wait_apart(sp, handed_r.sem, handed_r.before(a, "x"))
                sp.dma_start(res_a[:, :, :], xv[a]).then_inc(x_in.sem, 16)
                for n, (t, g) in enumerate(halves):
                    made_by = g_step(t, 2 * g + 1)
                    sig = free[made_by[0]][bank_of(made_by)]
                    wait_apart(sp, sig.sem, sig.at(a, made_by))
                    skew = bass.AP(tensor=scratch, offset=n * P * row + 1, ap=[[row + 1, P], [2 * P, HP], [1, WIN]])
                    sp.dma_start(skew, G[:, :, :]).then_inc(bias_out.sem, 16)
                    wait_apart(sp, bias_out.sem, bias_out.at(a, (t, g)))
                    last = ("A", "s", (t - 1) % NT * HP + 4 * g + 3)
                    sig = free["A"]["S1"]
                    wait_apart(sp, sig.sem, sig.at(a if t else a - 1, last))
                    sp.dma_start(E[:, g], scratch.ap()[n]).then_inc(bias_in.sem, 16)

            batches(sp, body)

        @block.gpsimd
        def _(pool):
            v = nc.gpsimd
            starts(pool, list(spread.values()) + list(pool_chain.values()) + list(scaled.values())
                   + list(lo_pool.values()) + [roped, b_weighed, b_multiplied])
            v.memset(E[:, 0].rearrange("p h k -> p (h k)"), NEG).then_inc(made, 1)
            v.memset(stage_wr, 0.0).then_inc(made, 1)
            v.memset(stage_bfun, 0.0).then_inc(made, 1)
            v.memset(br[:, :], 0.0).then_inc(made, 1)
            v.memset(ident[:, :], 0.0).then_inc(made, 1)
            v.memset(select[:, :, :], 0.0).then_inc(made, 1)
            v.memset(fmask[:, :], 0.0).then_inc(made, 1)
            v.memset(ones[:, :], 1.0).then_inc(made, 1)
            v.memset(mhalf[:, :], -0.5).then_inc(made, 1)
            for e in range(NE):
                v.memset(rank[:, e:e + 1], float(NE - e)).then_inc(made, 1)
            n = 9 + NE
            wait_apart(pool, made, n)
            v.affine_select(out=ident[:, :], in_=ident[:, :], compare_op=ALU.not_equal, fill=1.0, base=0,
                            pattern=[[-1, P]], channel_multiplier=1).then_inc(made, 1)
            v.affine_select(out=fmask[:, 3 * P:], in_=fmask[:, 3 * P:], compare_op=ALU.is_ge, fill=FMASK, base=0,
                            pattern=[[-1, P]], channel_multiplier=1).then_inc(made, 1)
            for s in range(3):
                v.affine_select(out=select[:, :, :], in_=select[:, :, :], compare_op=ALU.not_equal, fill=SPLIT,
                                base=-NE * s, pattern=[[-1, NE], [0, P]], channel_multiplier=1).then_inc(made, 1)
                wait_apart(pool, made, n + 3 + s)
            assert n + 5 == MADE
            v.memset(rwsp[:, :, :], 0.0).then_inc(made, 1)
            wait_apart(pool, made, MADE + 1)
            wait_apart(pool, loaded, LOADED)
            wait_apart(pool, set_up, SET_UP - 1)
            v.tensor_tensor(out=lg[:, 1, :], in0=lg[:, 0, :], in1=mhalf[:, :], op=ALU.pow).then_inc(made, 1)
            wait_apart(pool, set_up, SET_UP)

            def deviation(g, b, then, ln):
                mv = ln[:, 6 * NT:8 * NT].rearrange("p (t k) -> p t k", k=2)
                rs = ln[:, 8 * NT:10 * NT].rearrange("p (k t) -> p k t", k=2)
                wait_apart(pool, stats[g].sem, stats[g].at(b, "x"))
                then(v.tensor_scalar(rs[:, 0], mv[:, :, 1], LN_EPS, None, ALU.add))
                v.tensor_tensor(out=rs[:, 1], in0=rs[:, 0], in1=mhalf[:, 0:NT], op=ALU.pow).then_inc(spread[g].sem, 1)

            def rotate(b, then, s):
                t = s[2]
                src = qkvb[:, t, 0:2 * C].rearrange("p (h s d) -> p h s d", s=2, d=DB // 2)
                both = qkvb[:, t, 0:2 * C].rearrange("p (h d) -> p h d", d=DB)
                cos = ropet[:, t, 0, :].unsqueeze(1).to_broadcast([P, 2 * HB, DB])
                r = rp
                swapped = r[:, 1].rearrange("p (h s d) -> p h s d", s=2, d=DB // 2)
                sig = free["B"][bank_of(s)]
                wait_apart(pool, sig.sem, sig.at(b, s))
                wait_apart(pool, roped.sem, roped.before(b, t))
                then(v.tensor_tensor(out=r[:, 0].rearrange("p (h d) -> p h d", d=DB), in0=both, in1=cos, op=ALU.mult))
                for h in range(2):
                    sin = ropet[:, t, 1, h * 4:h * 4 + 4].unsqueeze(1).to_broadcast([P, 2 * HB, DB // 2])
                    then(v.tensor_tensor(out=swapped[:, :, h], in0=src[:, :, 1 - h], in1=sin, op=ALU.mult))
                v.tensor_tensor(out=qkr[:, t], in0=r[:, 0], in1=r[:, 1], op=ALU.add).then_inc(roped.sem, 1)

            def body(batch):
                then = chains(pool, pool_chain, batch, apart=True)
                for s, b, _ in work("pool", batch):
                    g, k = s[:2]
                    if k == "ln":
                        deviation(g, b, then[g], {"Q": ln_a[:, :], "B": ln_b}.get(g, ln_f[:, :]))
                    elif k == "sq":
                        wait_apart(pool, squared[g].sem, squared[g].at(b, "x"))
                        then[g](v.tensor_scalar(ss[:, 1], ss[:, 0], 1e-12, None, ALU.add))
                        v.tensor_tensor(out=ss[:, 2], in0=ss[:, 1], in1=mhalf[:, 0:NT],
                                        op=ALU.pow).then_inc(scaled[g].sem, 1)
                    elif k == "bc":
                        phase, e = s[2:]
                        wait_apart(pool, x_hi[g].sem, x_hi[g].at(b, (phase, e)))
                        v.tensor_tensor(out=xparts[:, e % 4, 1], in0=xs[:, e % 4], in1=xparts[:, e % 4, 0],
                                        op=ALU.subtract).then_inc(lo_pool[g].sem, 1)
                    elif k == "bp":
                        rotate(b, then[g], s)
                    elif k == "bq":
                        t = s[2]
                        wait_apart(pool, roped.sem, roped.at(b, t))
                        wait_apart(pool, b_scored.sem, b_scored.before(b, t))
                        multiply_qk(v, t, 1).then_inc(b_multiplied.sem, 1)
                    elif k == "bv":
                        t, half = s[2:]
                        shape = [P, HB // 2, DB, HB]
                        wait_apart(pool, b_exp.sem, b_exp.at(b, t))
                        wait_apart(pool, b_summed.sem, b_summed.at(b if t else b - 1, ((t - 1) % NT, half)))
                        v.tensor_tensor(
                            out=W2[:, half * 1024:half * 1024 + 1024].rearrange("p (h d g) -> p h d g", d=DB, g=HB),
                            in0=pb[:, t, half * 128:half * 128 + 128].rearrange("p (h g) -> p h g", g=HB
                                ).unsqueeze(2).to_broadcast(shape),
                            in1=qkvb[:, t, 2 * C:].rearrange("p (g d) -> p d g", d=DB).unsqueeze(1).to_broadcast(shape),
                            op=ALU.mult).then_inc(b_weighed.sem, 1)
                for g, c in then.items():
                    assert c.n == c.sig.per, (g, c.n)

            batches(pool, body)

        @block.scalar
        def _(act):
            v = nc.scalar
            starts(act, [s for g in full for n, s in free[g].items() if n in ("S0", "S1", "TP", "X2")]
                   + [probs, a_hi, r_act, b_exp, y_out] + list(gate_exp.values()) + list(f_probs.values())
                   + list(x_hi.values()) + list(f_norm.values()))

            def copy(dst, src, scale=1.0):
                return v.activation(dst, src, ACT.Copy, scale=scale)

            act.wait_ge(loaded, LOADED)
            for j in range(3):
                copy(wqkv[:, j, 0], stage_qkv[j], SPLIT).then_inc(setup_act, 1)
            copy(wr[:, 0].rearrange("p g r -> p (g r)"), stage_wr, SPLIT).then_inc(setup_act, 1)
            copy(PT[:, 0, 0:2, :].rearrange("p a t -> p (a t)").bitcast(f16), stage_bfun, SPLIT).then_inc(setup_act, 1)
            for j in range(4):
                copy(wf[:, j, 0].rearrange("p e h -> p (e h)"), stage_f[j], SPLIT).then_inc(setup_act, 1)
            v.activation(sig[:, :], sig[:, :], ACT.Exp, scale=-1.0).then_inc(setup_act, 1)
            copy(bq[:, :], bq[:, :], DQ ** -0.5).then_inc(setup_act, 1)
            copy(br[:, :], br[:, :], SPLIT).then_inc(setup_act, 1)
            act.wait_ge(setup_act, SPLITS + 3)
            act.wait_ge(set_up, SET_UP)

            def body(batch):
                for s, b, part in work("act", batch):
                    g, k = s[:2]

                    def filled_bank(n):
                        act.wait_ge(full[g][n].sem, full[g][n].at(b, s))
                        return bank[n]

                    if k == "tr" and g == "Q":
                        copy(a_xT[:, 0], filled_bank(bank_of(s))[:, :], SPLIT).then_inc(a_hi.sem, 1)
                    elif k == "r":
                        r = s[2]
                        if r >= 2:
                            two_before = free[g][bank_of(("Q", "r", r - 2))]
                            act.wait_ge(two_before.sem, two_before.at(b, ("Q", "r", r - 2)))
                        v.activation(L[:, r % 2].rearrange("p h n -> p (h n)"), filled_bank(bank_of(s))[:, :],
                                     ACT.Identity, bias=br[:, r:r + 1], scale=1.0 / SPLIT).then_inc(r_act.sem, 1)
                        act.wait_ge(r_act.sem, r_act.at(b, (r, 0)))
                        copy(PT[:, r % 2, 0:2, :].rearrange("p a t -> p (a t)").bitcast(f16),
                             L[:, r % 2].rearrange("p h n -> p (h n)")).then_inc(r_act.sem, 1)
                    elif g in "QA" and k in ("g", "qk", "v", "t", "pt"):
                        if k == "g" and s[3] % 2 == 0:
                            act.wait_ge(bias_out.sem, bias_out.before(b, (s[2], s[3] // 2)))
                        n = bank_of(s)
                        src = filled_bank(n)
                        if k == "g":
                            i = copy(G[:, 4 * (s[3] % 2):4 * (s[3] % 2) + 4, :],
                                     src[:, :].rearrange("p (h d) -> p h d", h=4), UNSPLIT)
                        elif k == "qk" and s[2] < HP:
                            i = v.activation(QT[:, s[2], :], src[:, :], ACT.Identity, bias=bq[:, s[2]:s[2] + 1],
                                             scale=UNSPLIT * DQ ** -0.5)
                        elif k == "qk":
                            i = copy(KT[:, s[2] - HP, :], src[:, :], UNSPLIT)
                        elif k == "v":
                            i = copy(V[:, s[2], s[3] * TOK:(s[3] + 1) * TOK], src[:, :], UNSPLIT)
                        elif k == "t":
                            m = 4 if s[2] >= HP else 2
                            i = copy(PT[:, s[2] % 2, 0:m, :], src[:, 0:m * P].rearrange("p (k t) -> p k t", t=P))
                        else:
                            i = copy(AT[:, 4 * s[3]:4 * s[3] + 4, :], src[:, :].rearrange("p (k t) -> p k t", t=P))
                        i.then_inc(free[g][n].sem, 1)
                    elif k == "s":
                        u = s[2]
                        t = u // HP
                        lo = 0 if t else P
                        act.wait_ge(maxed.sem, maxed.at(b, u))
                        for h, head in enumerate(heads(u)):
                            i = v.activation(L[:, u % LOGITS, h, lo:], L[:, u % LOGITS, h, lo:], ACT.Exp,
                                             bias=nmx[:, u % LOGITS, h:h + 1], accum_out=sums[:, t % 2, head:head + 1])
                        i.then_inc(probs.sem, 1)
                    elif k in ("tr", "gt", "vt", "av", "oe", "bo"):
                        n = bank_of(s)
                        src = filled_bank(n)[:, :]
                        dst = {"tr": b_xT if g == "B" else f_xT[:, :], "gt": rwT[:, :],
                               "vt": vr[:, :, :].rearrange("p t h -> p (t h)"), "av": aoT[:, :], "oe": oT[:, :],
                               "bo": b_oT}[k]
                        copy(dst, src, UNSPLIT if k == "oe" else 1.0).then_inc(free[g][n].sem, 1)
                    elif k == "ge":
                        act.wait_ge(gated[g].sem, gated[g].at(b, "x"))
                        v.activation(gt[:, 11], gt[:, 10], ACT.Exp).then_inc(gate_exp[g].sem, 1)
                    elif k == "bc":
                        phase, e = s[2:]
                        made_xs = free[g][bank_of(s)]
                        act.wait_ge(made_xs.sem, made_xs.at(b, s))
                        copy(xparts[:, e % 4, 0], xs[:, e % 4]).then_inc(x_hi[g].sem, 1)
                    elif k == "qkve":
                        for j in range(3):
                            copy(qkvT[:, j, :], filled_bank(f"X{j}")[:, :], UNSPLIT).then_inc(free[g][f"X{j}"].sem, 1)
                    elif k == "sc":
                        t = s[2]
                        n = (t + 1) * P
                        act.wait_ge(f_maxed[g].sem, f_maxed[g].at(b, t))
                        v.activation(xs[:, t, 0:n], xs[:, t, 0:n], ACT.Exp, bias=fm[:, 1, t:t + 1],
                                     scale=P ** -0.5, accum_out=fm[:, 2, t:t + 1]).then_inc(f_probs[g].sem, 1)
                    elif k == "tp" and part == 0:
                        t = s[2]
                        act.wait_ge(f_inv[g].sem, f_inv[g].at(b, t))
                        copy(xs[:, t, 0:(t + 1) * P], xs[:, t, 0:(t + 1) * P], fm[:, 3, t:t + 1]).then_inc(f_norm[g].sem, 1)
                    elif k == "tp":
                        t = s[2]
                        n = bank_of(s)
                        copy(FPT[:, 0:t + 1, t * P:(t + 1) * P],
                             filled_bank(n)[:, 0:(t + 1) * P].rearrange("p (k t) -> p k t", t=P)
                             ).then_inc(free[g][n].sem, 1)
                    elif k == "ot" and g == "F2":
                        act.wait_ge(free[g]["X2"].sem, free[g]["X2"].at(b, s))
                        act.dma_start(outv[b], res_y[:, :, :]).then_inc(y_out.sem, 16)
                    elif k == "bp":
                        n = bank_of(s)
                        copy(qkvb[:, s[2]], filled_bank(n)[:, 0:3 * C]).then_inc(free[g][n].sem, 1)
                    elif k == "lat":
                        v.activation(latT, filled_bank("OV")[0:LAT, :], ACT.Identity,
                                     bias=bdown[:, :]).then_inc(free[g]["OV"].sem, 1)
                    elif k == "bx":
                        t = s[2]
                        act.wait_ge(b_shift.sem, b_shift.at(b, t))
                        v.activation(pb[:, t], att[:, t], ACT.Exp, scale=DB ** -0.5).then_inc(b_exp.sem, 1)

            batches(act, body)
            act.wait_ge(y_out.sem, y_out.at(NBATCH - 1))

        @block.vector
        def _(dve):
            v = nc.vector
            starts(dve, [s for g in full for n, s in free[g].items() if n in ("OV", "X0", "X1", "X3")]
                   + [maxed, handed_r, handed_x, handed_y, b_shift, b_sum, b_summed, b_scored, b_att] + list(stats.values()) + list(normed.values()) + list(squared.values())
                   + list(gated.values()) + list(routed.values()) + list(lo_dve.values()) + list(f_maxed.values())
                   + list(f_inv.values()) + list(dve_chain.values()))
            n = 0

            def then(ins):
                nonlocal n
                n += 1
                ins.then_inc(set_up, 1)
                dve.wait_ge(set_up, n)

            def split(dst, src, hi):
                return v.scalar_tensor_tensor(dst, src, SPLIT, hi, ALU.mult, ALU.subtract)

            dve.wait_ge(made, MADE)
            dve.wait_ge(loaded, LOADED)
            for j in range(3):
                dve.wait_ge(setup_act, j + 1)
                then(split(wqkv[:, j, 1], stage_qkv[j], wqkv[:, j, 0]))
            dve.wait_ge(setup_act, 4)
            then(split(wr[:, 1].rearrange("p g r -> p (g r)"), stage_wr, wr[:, 0].rearrange("p g r -> p (g r)")))
            dve.wait_ge(setup_act, 5)
            then(v.tensor_scalar(stage_bfun, stage_bfun, SPLIT, None, ALU.mult))
            then(v.scalar_tensor_tensor(bfun[:, :, :].rearrange("p q d -> p (q d)"),
                                        PT[:, 0, 0:2, :].rearrange("p a t -> p (a t)").bitcast(f16),
                                        neg_parts[:, 1:2], stage_bfun, ALU.mult, ALU.add))
            for j in range(4):
                dve.wait_ge(setup_act, 6 + j)
                w = wf[:, j].rearrange("p k e h -> p k (e h)")
                then(split(w[:, 1], stage_f[j], w[:, 0]))
            dve.wait_ge(setup_act, SPLITS + 3)
            v.tensor_scalar(sig[:, :], sig[:, :], 1.0, None, ALU.add).then_inc(setup_act, 1)
            dve.wait_ge(setup_act, SPLITS + 4)
            then(v.reciprocal(sig[:, :], sig[:, :]))
            then(v.tensor_tensor(out=simn[:, :], in0=sim[:, :], in1=sim[:, :], op=ALU.mult))
            dve.wait_ge(setup_mm, 1)
            then(v.tensor_scalar(lg[:, 0, :], bank["X3"][:, 0:NE], 1e-12, None, ALU.add))
            dve.wait_ge(made, MADE + 2)
            then(v.tensor_tensor(out=simn[:, :], in0=sim[:, :], in1=lg[:, 1, :], op=ALU.mult))
            assert n == SET_UP, n

            def statistics(g, b, then, src, ln):
                st = ln[:, 0:6 * NT].rearrange("p (t k) -> p t k", k=6)
                mv = ln[:, 6 * NT:8 * NT].rearrange("p (t k) -> p t k", k=2)
                for t in range(NT):
                    i = v.bn_stats(out=st[:, t], in_=src[:, t])
                then(i)
                dve.sem_inc(passed, 1)
                for t in range(NT):
                    i = v.bn_aggr(out=mv[:, t], in_=st[:, t])
                i.then_inc(stats[g].sem, 1)

            A = lambda n: gt[:, n]
            S = lambda n: g1[:, n]
            wide = lambda a: a.unsqueeze(2).to_broadcast([P, NT, NE])
            all_t = lambda a: a.unsqueeze(1).to_broadcast([P, NT, NE])
            tt = lambda o, a, c, op: v.tensor_tensor(out=o, in0=a, in1=c, op=op)
            red = lambda o, a, op: v.tensor_reduce(out=o, in_=a, axis=AX.X, op=op)

            def normalize(g, b, src, ln, xn):
                mv = ln[:, 6 * NT:8 * NT].rearrange("p (t k) -> p t k", k=2)
                dve.wait_ge(spread[g].sem, spread[g].at(b, "x"))
                for t in range(NT):
                    i = v.tensor_scalar(xn[:, t], src[:, t], mv[:, t, 0:1], ln[:, 9 * NT + t:9 * NT + t + 1],
                                        ALU.subtract, ALU.mult)
                i.then_inc(normed[g].sem, 1)

            def gate(f, then, quarter):
                if quarter == 0:
                    then(tt(A(0), lg[:, :, :], all_t(sig[:, :]), ALU.subtract))
                    then(v.tensor_scalar(A(1), A(0), 0.0, None, ALU.max))
                    then(v.tensor_scalar(A(2), A(0), 0.0, None, ALU.is_gt))
                    then(red(S(0), A(0), ALU.max))
                    then(tt(A(3), A(0), wide(S(0)), ALU.is_equal))
                    then(tt(A(4), A(3), all_t(rank[:, :]), ALU.mult))
                if quarter == 1:
                    then(red(S(1), A(4), ALU.max))
                    then(tt(A(5), A(4), wide(S(1)), ALU.is_equal))
                    then(v.scalar_tensor_tensor(A(7), A(5), -BIG, A(0), ALU.mult, ALU.add))
                    then(red(S(2), A(7), ALU.max))
                    then(tt(A(3), A(7), wide(S(2)), ALU.is_equal))
                if quarter == 2:
                    then(tt(A(4), A(3), all_t(rank[:, :]), ALU.mult))
                    then(red(S(3), A(4), ALU.max))
                    then(tt(A(6), A(4), wide(S(3)), ALU.is_equal))
                    then(tt(A(7), A(5), A(6), ALU.add))
                    then(red(S(4), A(2), ALU.max))
                if quarter == 3:
                    then(v.tensor_scalar(S(5), S(4), -1.0, 1.0, ALU.mult, ALU.add))
                    then(tt(A(8), A(7), wide(S(5)), ALU.mult))
                    then(tt(A(9), A(8), A(2), ALU.add))
                    then(red(S(6), A(1), ALU.max))
                    tt(A(10), A(1), wide(S(6)), ALU.subtract).then_inc(gated[f].sem, 1)

            def weigh(f, b, then, half):
                if half == 1:
                    then(tt(A(5), A(4), gb[:, 0], ALU.subtract))
                    then(v.tensor_copy(gb[:, 1], A(5)))
                    v.tensor_copy(rwsp[:, :, 0:NE], gb[:, 0])
                    v.tensor_copy(rwsp[:, :, NE:2 * NE], gb[:, 1])
                    tt(rwsp[:, :, 2 * NE:3 * NE], A(5), gb[:, 1], ALU.subtract).then_inc(routed[f].sem, 1)
                    return
                dve.wait_ge(gate_exp[f].sem, gate_exp[f].at(b, "x"))
                then(tt(A(3), A(11), A(9), ALU.mult))
                then(red(S(7), A(3), ALU.add))
                then(v.reciprocal(S(8), S(7)))
                then(tt(A(4), A(3), wide(S(8)), ALU.mult))
                then(v.tensor_copy(gb[:, 0], A(4)))

            def is_last(b):
                return isinstance(b, int) and b == NBATCH - 1

            def hand_on(batch):
                r, f, y = batch["R"], batch["F1"], batch["F2"]
                if is_last(batch["B"]):
                    dve.wait_ge(y_out.sem, y_out.at(y, "y"))
                    dve.wait_ge(free["B"]["OV"].sem, free["B"]["OV"].at(batch["B"], ("B", "br")))
                    v.tensor_copy(res_y[:, :, :], res_x[:, :, :]).then_inc(handed_y.sem, 1)
                elif f is not None and not is_last(f):
                    if y is not None:
                        dve.wait_ge(y_out.sem, y_out.at(y, "y"))
                    dve.wait_ge(free["F1"]["X2"].sem, free["F1"]["X2"].at(f, ("F1", "ot")))
                    v.tensor_copy(res_y[:, :, :], res_x[:, :, :]).then_inc(handed_y.sem, 1)
                if r is not None:
                    if f is not None:
                        dve.wait_ge(handed_y.sem, handed_y.at(f, "x"))
                    v.tensor_copy(res_x[:, :, :], res_r[:, :, :]).then_inc(handed_x.sem, 1)

            def body(batch):
                chain = chains(dve, dve_chain, batch)
                done = set()
                for s, b, part in work("dve", batch):
                    g, k = s[:2]
                    done.add(s)
                    if s == ("A", "pp", NT - 1):
                        assert all(batch[f] is None or (f, "ot") in done for f in F)
                        hand_on(batch)
                    then = chain.get(g)

                    def filled_bank(n):
                        dve.wait_ge(full[g][n].sem, full[g][n].at(b, s))
                        return bank[n]

                    def wait_step(stage, batch_no, step):
                        n = bank_of(step)
                        dve.wait_ge(free[stage][n].sem, free[stage][n].at(batch_no, step))

                    if k == "ln":
                        src, ln, xn, came = {"Q": (res_a, ln_a[:, :], a_xn, x_in), "B": (res_y, ln_b, b_xn, handed_y),
                                             "R": (res_r, ln_f[:, :], f_xn, handed_r),
                                             "F2": (res_y, ln_f[:, :], f_xn, handed_y)}[g]
                        if g == "B" and is_last(b):
                            src = res_x
                        if part == 1:
                            normalize(g, b, src, ln, xn)
                        elif g == "B" and is_last(b):
                            wait_step("F1", b, ("F1", "ot"))
                            statistics(g, b, then, src, ln)
                        else:
                            dve.wait_ge(came.sem, came.at(b, "x"))
                            if g == "F2":
                                wait_step("B", b, ("B", "br"))
                            statistics(g, b, then, src, ln)
                    elif k == "tr":
                        n = bank_of(s)
                        dve.wait_ge(a_hi.sem, a_hi.at(b, "x"))
                        split(a_xT[:, 1], bank[n][:, :], a_xT[:, 0]).then_inc(free[g][n].sem, 1)
                    elif k == "r":
                        r = s[2]
                        dve.wait_ge(r_act.sem, r_act.at(b, (r, 1)))
                        v.scalar_tensor_tensor(RT[:, r], PT[:, r % 2, 0:2, :].rearrange("p a t -> p (a t)").bitcast(f16),
                                               neg_parts[:, 0:1], L[:, r % 2].rearrange("p h n -> p (h n)"),
                                               ALU.mult, ALU.add).then_inc(free[g][bank_of(s)].sem, 1)
                    elif k == "s":
                        u = s[2]
                        t, p = divmod(u, HP)
                        lo = 0 if t else P
                        n = bank_of(s)
                        dve.wait_ge(bias_in.sem, bias_in.at(b, (t, p // 4)))
                        wait_apart(dve, full[g][n].sem, full[g][n].at(b, s))
                        for h, head in enumerate(heads(u)):
                            i = v.tensor_tensor_reduce(
                                out=L[:, u % LOGITS, h, lo:], in0=bank[n][:, h * 2 * P + lo:(h + 1) * 2 * P],
                                in1=E[:, p // 4, head % 8, lo:], scale=1.0, scalar=-3.0e38, op0=ALU.add, op1=ALU.max,
                                accum_out=mx[:, u % LOGITS, h:h + 1])
                        i.then_inc(free[g][n].sem, 1)
                        wait_step(g, b, s)
                        v.tensor_scalar(nmx[:, u % LOGITS], mx[:, u % LOGITS], -1.0, None, ALU.mult).then_inc(maxed.sem, 1)
                    elif k == "o" and s[2] % 4 == 3:
                        u = s[2]
                        t, q = u // HP, u % HP // 4
                        dve.wait_ge(attended.sem, attended.at(b, u))
                        then(v.reciprocal(rsums[:, q], sums[:, t % 2, 8 * q:8 * q + 8]))
                        v.tensor_tensor(
                            out=AO[:, :].rearrange("p (h d) -> p h d", d=DQ),
                            in0=bank["OV"][:, :].rearrange("p (h d) -> p h d", d=DQ),
                            in1=rsums[:, q].unsqueeze(2).to_broadcast([P, 8, DQ]),
                            op=ALU.mult).then_inc(free[g]["OV"].sem, 1)
                    elif k == "pp":
                        v.tensor_tensor(out=res_a[:, s[2]], in0=filled_bank("TP")[:, 0:C], in1=res_a[:, s[2]],
                                        op=ALU.add).then_inc(free[g]["TP"].sem, 1)
                    elif k == "sq":
                        dve.wait_ge(normed[g].sem, normed[g].at(b, "x"))
                        for t in range(NT):
                            i = v.tensor_tensor_reduce(out=f_sq[:, t], in0=f_xn[:, t], in1=f_xn[:, t], scale=1.0,
                                                       scalar=0.0, op0=ALU.mult, op1=ALU.add,
                                                       accum_out=ss[:, 0, t:t + 1])
                        i.then_inc(squared[g].sem, 1)
                    elif k == "gl" and part:
                        gate(g, then, part - 1)
                    elif k == "gl":
                        dve.wait_ge(scaled[g].sem, scaled[g].at(b, "x"))
                        v.tensor_tensor(out=lg[:, :, :],
                                        in0=filled_bank("X1")[:, 0:NT * NE].rearrange("p (t e) -> p t e", e=NE),
                                        in1=ss[:, 2].unsqueeze(2).to_broadcast([P, NT, NE]),
                                        op=ALU.mult).then_inc(free[g]["X1"].sem, 1)
                        wait_step(g, b, s)
                    elif k == "ge":
                        weigh(g, b, then, part)
                    elif k == "bc" and part == 0:
                        phase, e = s[2:]
                        if phase == "o" and e == 0:
                            wait_step(g, b, (g, "av"))
                        if e >= 4:
                            low = lo_of(g, phase, e - 4)
                            dve.wait_ge(low.sem, low.at(b, (phase, e - 4)))
                        v.tensor_tensor(out=xs[:, e % 4], in0=filled_bank(bank_of(s))[:, :],
                                        in1=(f_xT if phase == "qkv" else aoT)[:, :],
                                        op=ALU.mult).then_inc(free[g][bank_of(s)].sem, 1)
                    elif k == "bc":
                        phase, e = s[2:]
                        dve.wait_ge(x_hi[g].sem, x_hi[g].at(b, (phase, e)))
                        v.tensor_tensor(out=xparts[:, e % 4, 1], in0=xs[:, e % 4], in1=xparts[:, e % 4, 0],
                                        op=ALU.subtract).then_inc(lo_dve[g].sem, 1)
                    elif k == "sc":
                        t = s[2]
                        n = (t + 1) * P
                        bk = bank_of(s)
                        wait_apart(dve, full[g][bk].sem, full[g][bk].at(b, s))
                        v.tensor_tensor_reduce(out=xs[:, t, 0:n], in0=bank[bk][:, 0:n],
                                               in1=fmask[:, 4 * P - n:4 * P], scale=1.0, scalar=-3.0e38, op0=ALU.add,
                                               op1=ALU.max, accum_out=fm[:, 0, t:t + 1]).then_inc(free[g][bk].sem, 1)
                        wait_step(g, b, s)
                        v.tensor_scalar(fm[:, 1, t:t + 1], fm[:, 0, t:t + 1], -(P ** -0.5), None,
                                        ALU.mult).then_inc(f_maxed[g].sem, 1)
                    elif k == "tp":
                        t = s[2]
                        dve.wait_ge(f_probs[g].sem, f_probs[g].at(b, t))
                        v.reciprocal(fm[:, 3, t:t + 1], fm[:, 2, t:t + 1]).then_inc(f_inv[g].sem, 1)
                    elif k in ("ot", "br"):
                        n = bank_of(s)
                        res = res_x if g == "F1" or (g == "B" and is_last(b)) else res_y
                        v.tensor_tensor(out=res[:, :, :], in0=filled_bank(n)[:, :].rearrange("p (t c) -> p t c", c=C),
                                        in1=res[:, :, :], op=ALU.add).then_inc(free[g][n].sem, 1)
                    elif k == "bq":
                        t, half = s[2:]
                        scored = lambda: red(att[:, t, half * 128:half * 128 + 128],
                                             W[:, half * 1024:half * 1024 + 1024].rearrange("p (n d) -> p n d", d=DB),
                                             ALU.add)
                        if half:
                            dve.wait_ge(b_multiplied.sem, b_multiplied.at(b, t))
                            scored().then_inc(b_scored.sem, 1)
                        elif part == 0:
                            dve.wait_ge(roped.sem, roped.at(b, t))
                            then(multiply_qk(v, t, 0))
                        else:
                            then(scored())
                    elif k == "bx":
                        t = s[2]
                        by_head = att[:, t].rearrange("p (h g) -> p h g", g=HB)
                        if part == 0:
                            dve.wait_ge(b_scored.sem, b_scored.at(b, t))
                            then(red(bm[:, t, 0], by_head, ALU.max))
                        elif part == 1:
                            tt(by_head, by_head, bm[:, t, 0].unsqueeze(2).to_broadcast([P, HB, HB]),
                               ALU.subtract).then_inc(b_shift.sem, 1)
                        else:
                            dve.wait_ge(b_exp.sem, b_exp.at(b, t))
                            red(bm[:, t, 1], pb[:, t].rearrange("p (h g) -> p h g", g=HB), ALU.add).then_inc(b_sum.sem, 1)
                            dve.wait_ge(b_sum.sem, b_sum.at(b, t))
                            v.reciprocal(bm[:, t, 2], bm[:, t, 1])
                    elif k == "bv":
                        t, half = s[2:]
                        o = ato[:, t].rearrange("p (h d) -> p h d", d=DB)
                        if part == 0:
                            dve.wait_ge(b_weighed.sem, b_weighed.at(b, (t, half)))
                            red(ato[:, t, half * 64:half * 64 + 64],
                                W2[:, half * 1024:half * 1024 + 1024].rearrange("p (n g) -> p n g", g=HB),
                                ALU.add).then_inc(b_summed.sem, 1)
                        else:
                            dve.wait_ge(b_summed.sem, b_summed.at(b, (t, 1)))
                            tt(o, o, bm[:, t, 2].unsqueeze(2).to_broadcast([P, HB, DB]), ALU.mult).then_inc(b_att.sem, 1)
                for g, c in chain.items():
                    assert c.n == c.sig.per, (g, c.n)
                if batch["A"] is None:
                    hand_on(batch)
                else:
                    dve.wait_ge(free["A"]["TP"].sem, free["A"]["TP"].at(batch["A"], ("A", "pp", NT - 1)))
                    if batch["R"] is not None:
                        dve.wait_ge(normed["R"].sem, normed["R"].at(batch["R"], "x"))
                        dve.wait_ge(handed_x.sem, handed_x.at(batch["R"], "x"))
                    v.tensor_copy(res_r[:, :, :], res_a[:, :, :]).then_inc(handed_r.sem, 1)

            batches(dve, body)

        @block.tensor
        def _(pe):
            mm, trp = nc.tensor.matmul, nc.tensor.transpose
            starts(pe, [s for g in full for s in full[g].values()] + [attended])
            pe.wait_ge(loaded, LOADED)
            pe.wait_ge(made, MADE)
            pe.wait_ge(set_up, SET_UP - 2)
            mm(bank["X3"][:, 0:NE], ones[:, :], simn[:, :], start=True, stop=True).then_inc(setup_mm, 1)
            pe.wait_ge(set_up, SET_UP)

            def cols(t):
                return slice(t * P, (t + 1) * P)

            def three(to, w, xv, start=True, stop=True):
                for n, (i, j) in enumerate(((0, 0), (0, 1), (1, 0))):
                    last = mm(to, w(i), xv(j), start=start and n == 0, stop=stop and n == 2)
                return last

            def body(batch):
                for s, b, part in work("pe", batch):
                    g, k = s[:2]

                    def ready(*step, n=None):
                        n = n or bank_of(step)
                        pe.wait_ge(free[g][n].sem, free[g][n].at(b, step))

                    def clear(n, step=None):
                        step = step or s
                        before, ahead = [x for x in STAGE_BEFORE[g] if n in free[x[0]]][0]
                        if free[g][n].turn[step] == 0:
                            if not isinstance(b, int) or b + ahead < NBATCH:
                                pe.wait_ge(free[before][n].sem, free[before][n].at(b + ahead))
                        else:
                            pe.wait_ge(free[g][n].sem, free[g][n].before(b, step))
                        return bank[n]

                    if k == "tr":
                        pe.wait_ge(normed[g].sem, normed[g].at(b, "x"))
                        to = clear(bank_of(s))
                        xn = {"Q": a_xn, "B": b_xn}.get(g, f_xn)
                        for t in range(NT):
                            i = trp(to[:, cols(t)], xn[:, t], ident[:, :])
                        i.then_inc(full[g][bank_of(s)].sem, 1)
                    elif k == "r":
                        if s[2] == 0:
                            ready("Q", "tr")
                        three(clear(bank_of(s))[:, :], lambda i: wr[:, i, s[2], :],
                              lambda i: a_xT[:, i]).then_inc(full[g][bank_of(s)].sem, 1)
                    elif k == "g":
                        t, q = s[2:]
                        if t == 0:
                            ready("Q", "r", q)
                        mm(clear(bank_of(s))[:, :], RT[:, q, cols(t)], bfun[:, :, :].rearrange("p q d -> p (q d)"),
                           start=True, stop=True).then_inc(full[g][bank_of(s)].sem, 1)
                    elif k == "qk":
                        j = s[2]
                        if j == 0:
                            pe.wait_ge(free["B"]["OV"].sem, free["B"]["OV"].at(b - LAG["B"], ("B", "br")))
                        three(clear(bank_of(s))[:, :], lambda i: wqkv[:, j // HP, i, cols(j % HP)],
                              lambda i: a_xT[:, i]).then_inc(full[g][bank_of(s)].sem, 1)
                    elif k == "v":
                        t, h = s[2:]
                        three(clear(bank_of(s))[:, :], lambda i: a_xT[:, i, cols(t)],
                              lambda i: wqkv[:, 2, i, h * TOK:(h + 1) * TOK]).then_inc(full[g][bank_of(s)].sem, 1)
                    elif k == "s":
                        u = s[2]
                        t = u // HP
                        if u == 0:
                            ready("A", "v", NT - 1, 1)
                        n = bank_of(s)
                        to = clear(n)
                        lo = 0 if t else P
                        for h, head in enumerate(heads(u)):
                            part = slice(head % 2 * DQ, head % 2 * DQ + DQ)
                            i = mm(to[:, h * 2 * P + lo:(h + 1) * 2 * P], QT[part, head // 2, cols(t)],
                                   KT[part, head // 2, max(t - 1, 0) * P:(t + 1) * P], start=True, stop=True)
                        i.then_inc(full[g][n].sem, 1)
                    elif k == "t":
                        u = s[2]
                        pe.wait_ge(probs.sem, probs.at(b, u))
                        to = clear("TP")
                        for n, (h, c) in enumerate([(h, c) for h in range(2) for c in ((0, 1) if u >= HP else (1,))]):
                            i = trp(to[:, cols(n)], L[:, u % LOGITS, h, cols(c)], ident[:, :])
                        i.then_inc(full[g]["TP"].sem, 1)
                    elif k == "o":
                        u = s[2]
                        t = u // HP
                        ready("A", "t", u)
                        if u % 4 == 0:
                            clear("OV", ("A", "o", u + 3))
                        keys = [t - 1, t] if t else [0]
                        for h, head in enumerate(heads(u)):
                            for n, kt in enumerate(keys):
                                i = mm(bank["OV"][:, head % 8 * DQ:(head % 8 + 1) * DQ],
                                       PT[:, u % 2, h * len(keys) + n, :], V[:, kt, head * DQ:(head + 1) * DQ],
                                       start=(n == 0), stop=(n == len(keys) - 1))
                        i.then_inc(attended.sem, 1)
                    elif k == "pt":
                        t, q = s[2:]
                        ready("A", "o", t * HP + 4 * q + 3)
                        n = bank_of(s)
                        to = clear(n)
                        for j in range(4):
                            i = trp(to[:, cols(j)], AO[:, cols(j)], ident[:, :])
                        i.then_inc(full[g][n].sem, 1)
                    elif k == "pp":
                        ready("A", "pt", s[2], 1)
                        to = clear("TP")[:, 0:C]
                        mm(to, ones[0:1, :], rows[0:1, 0, :], start=True, stop=False)
                        for j in range(HP):
                            i = mm(to, AT[:, j, :], wproj[:, j, :], start=False, stop=(j == HP - 1))
                        i.then_inc(full[g]["TP"].sem, 1)
                    elif k == "gl":
                        ready(g, "tr")
                        to = clear("X1")
                        for t in range(NT):
                            i = mm(to[:, t * NE:(t + 1) * NE], f_xT[:, cols(t)], simn[:, :], start=True, stop=True)
                        i.then_inc(full[g]["X1"].sem, 1)
                    elif k == "gt":
                        pe.wait_ge(routed[g].sem, routed[g].at(b, "x"))
                        to = clear("X2")
                        for t in range(NT):
                            i = trp(to[:, cols(t)], rwsp[:, t], ident[:, :])
                        i.then_inc(full[g]["X2"].sem, 1)
                    elif k == "bc":
                        if s[2:] == ("qkv", 0):
                            ready(g, "gt")
                        mm(clear(bank_of(s))[:, :], select[:, s[3], :], rwT[:, :],
                           start=True, stop=True).then_inc(full[g][bank_of(s)].sem, 1)
                    elif k == "mm":
                        phase, e = s[2:]
                        n, j = (f"X{part}", part) if phase == "qkv" else ("X1", 3)
                        if part == 0:
                            pe.wait_ge(lo_of(g, phase, e).sem, lo_of(g, phase, e).at(b, (phase, e)))
                        if e == 0:
                            clear(n, (g, "qkve" if phase == "qkv" else "oe"))
                        i = three(bank[n][:, :], lambda h: wf[:, j, h, e, :], lambda h: xparts[:, e % 4, h],
                                  start=(e == 0), stop=(e == NE - 1))
                        if e == NE - 1:
                            i.then_inc(full[g][n].sem, 1)
                    elif k == "vt":
                        ready(g, "qkve", n="X2")
                        to = clear("X3")
                        for t in range(NT):
                            i = trp(to[:, cols(t)], qkvT[:, 2, cols(t)], ident[:, :])
                        i.then_inc(full[g]["X3"].sem, 1)
                    elif k == "sc":
                        t = s[2]
                        if t == 0:
                            ready(g, "qkve", n="X0")
                            ready(g, "qkve", n="X1")
                        n = bank_of(s)
                        mm(clear(n)[:, 0:(t + 1) * P], qkvT[:, 0, cols(t)], qkvT[:, 1, 0:(t + 1) * P],
                           start=True, stop=True).then_inc(full[g][n].sem, 1)
                    elif k == "tp":
                        t = s[2]
                        n = bank_of(s)
                        pe.wait_ge(f_norm[g].sem, f_norm[g].at(b, t))
                        to = clear(n)
                        for j in range(t + 1):
                            i = trp(to[:, cols(j)], xs[:, t, cols(j)], ident[:, :])
                        i.then_inc(full[g][n].sem, 1)
                    elif k == "av":
                        ready(g, "tp", NT - 1)
                        to = clear("X0")
                        for j in range(NT):
                            i = mm(to[:, j * P:], vr[:, j, :], FPT[:, j, j * P:], start=(j == 0), stop=(j == NT - 1))
                        i.then_inc(full[g]["X0"].sem, 1)
                    elif k == "ot":
                        ready(g, "oe")
                        to = clear("X2")
                        for t in range(NT):
                            i = trp(to[:, cols(t)], oT[:, cols(t)], ident[:, :])
                        i.then_inc(full[g]["X2"].sem, 1)
                    elif k == "lat":
                        ready("B", "tr")
                        mm(clear("OV")[0:LAT, :], wdown[:, :], b_xT, start=True, stop=True).then_inc(full[g]["OV"].sem, 1)
                    elif k == "bp":
                        n = bank_of(s)
                        if s[2] == 0:
                            ready("B", "lat")
                        to = clear(n)
                        mm(to[:, 0:C], ones[0:1, :], biasb[0:1, 0:C], start=True, stop=False)
                        mm(to[:, 0:C], b_xT[:, cols(s[2])], wqb[:, :], start=False, stop=True)
                        mm(to[:, C:3 * C], ones[0:1, :], biasb[0:1, C:3 * C], start=True, stop=False)
                        mm(to[:, C:3 * C], latT[:, cols(s[2])], wup[:, :], start=False, stop=True
                           ).then_inc(full[g][n].sem, 1)
                    elif k == "bo":
                        pe.wait_ge(b_att.sem, b_att.at(b, NT - 1))
                        to = clear("TP")
                        for t in range(NT):
                            i = trp(to[:, cols(t)], ato[:, t], ident[:, :])
                        i.then_inc(full[g]["TP"].sem, 1)
                    elif k == "br":
                        ready("B", "bo")
                        to = clear("OV")
                        for t in range(NT):
                            mm(to[:, cols(t)], ones[0:1, :], rows[0:1, 1, :], start=True, stop=False)
                            i = mm(to[:, cols(t)], b_oT[:, cols(t)], wout[:, :], start=False, stop=True)
                        i.then_inc(full[g]["OV"].sem, 1)

            batches(pe, body)


_ARGS = ["L0_attn_a_X", "L0_attn_a_Wq", "L0_attn_a_bq", "L0_attn_a_Wk", "L0_attn_a_Wv", "L0_attn_a_Wproj",
         "L0_attn_a_bproj", "L0_attn_a_Wr", "L0_attn_a_br", "L0_attn_a_b_nd", "L0_attn_b_Wq", "L0_attn_b_bq",
         "L0_attn_b_Wdown", "L0_attn_b_bdown", "L0_attn_b_Wup", "L0_attn_b_bup", "L0_attn_b_Wout", "L0_attn_b_bout",
         "L0_ffn_sim_matrix", "L0_ffn_gates", "L0_ffn_q_proj", "L0_ffn_k_proj", "L0_ffn_v_proj", "L0_ffn_o_proj"]


def rope_table():
    inv = 1.0 / 10000.0 ** (np.arange(0, DB, 2, dtype=np.float32) / np.float32(DB))
    angle = np.arange(TOK, dtype=np.float32)[:, None] * inv[None, :].astype(np.float32)
    cos, sin = np.cos(angle).astype(np.float32), np.sin(angle).astype(np.float32)
    table = np.stack([np.concatenate([cos, cos], 1), np.concatenate([-sin, sin], 1)], 1)
    return np.ascontiguousarray(table.reshape(NT, P, 2, DB).transpose(1, 0, 2, 3))


def part_rows():
    k = np.arange(P) % 32 // NB
    return np.ascontiguousarray(-np.stack([k == 1, k == 2], 1).astype(np.float32))


def kernel(**inputs):
    import concourse.bacc as _bacc
    from concourse import mybir as _mybir
    from concourse.bass_utils import run_bass_kernel_spmd as _run

    nc = _bacc.Bacc("TRN2", target_bir_lowering=False, num_devices=1)
    arrays, args = {}, []
    constants = {"rope": rope_table(), "part_rows": part_rows()}
    for name in _ARGS + list(constants):
        a = constants[name] if name in constants else np.asarray(inputs[name])
        if name == "L0_attn_a_b_nd":
            a = a[:, ::-1]
        a = np.ascontiguousarray(a)
        arrays[f"in_{name}"] = a
        args.append(nc.dram_tensor(f"in_{name}", a.shape, _mybir.dt.from_np(a.dtype), kind="ExternalInput").ap())
    args.append(nc.dram_tensor("out_0", (NBATCH, TOK, C), _mybir.dt.float32, kind="ExternalOutput").ap())
    stack_kernel(nc, *args)
    r = _run(nc, [arrays], core_ids=[0])
    return r.results[0]["out_0"]
```
